# Optimizing a Trainium2 kernel written in Bass

```python
import numpy as np
import jax
import jax.numpy as jnp

def _softmax(x, axis=-1):
    return jax.nn.softmax(x, axis=axis)

def _gelu(x):
    return jax.nn.gelu(x, approximate=True)

def _silu(x):
    return jax.nn.silu(x)

def _sigmoid(x):
    return jax.nn.sigmoid(x)

def _layernorm(x, axis=-1, eps=1e-05):
    m = jnp.mean(x, axis=axis, keepdims=True)
    v = jnp.var(x, axis=axis, keepdims=True)
    return (x - m) / jnp.sqrt(v + eps)

def _scatter_add(tgt, idx, src, axis=0):
    return tgt.at[idx].add(src)

def _segment_sum(src, seg, n):
    return jax.ops.segment_sum(src, seg, n)
kernel_name = 'mk_flamingo_gated_d2_seqx_r8_7550d1'

def setup_inputs(seed: int=0):
    np.random.seed(seed)
    _w = jnp.asarray

    def _rec_inputs():
        import jax
        import jax.numpy as jnp
        _rk = jax.random.key(seed)
        x = 7.22e-05 + 1 * jax.random.normal(jax.random.fold_in(_rk, 1), (32, 100, 256), jnp.float32)
        _lenS = 100 - jax.random.randint(jax.random.fold_in(_rk, 7), (32,), 0, max(1, 100 // 4) + 1, jnp.int32)
        _lenS2 = 1444 - jax.random.randint(jax.random.fold_in(_rk, 8), (32,), 0, max(1, 1444 // 4) + 1, jnp.int32)
        _ctx_512P = jax.random.normal(jax.random.fold_in(_rk, 11), (32, 16, 64), jnp.float32)
        _ctx_512c = jax.random.dirichlet(jax.random.fold_in(_rk, 511), 0.3 * jnp.ones((16,), jnp.float32), (32, 1444))
        _ctx_512t = jnp.einsum('bsk,bkd->bsd', _ctx_512c, _ctx_512P)
        _ctx_512t = _ctx_512t * jax.lax.rsqrt(jnp.mean(jnp.square(_ctx_512t)) + 1e-12) * 0.953939
        ctx_512 = -0.000514642 + 1.00011 * (_ctx_512t + 0.3 * jax.random.normal(jax.random.fold_in(_rk, 611), (32, 1444, 64), jnp.float32))
        _g = jax.random.normal(jax.random.fold_in(_rk, 9001), (2, 2), jnp.float32)
        _g = jnp.sign(_g) * jnp.maximum(jnp.abs(_g), 1.0) + (_g == 0) * 1.0
        g_xattn = _g[0]
        g_ffn = _g[1]
        return (x, ctx_512, g_xattn, g_ffn)
    x, ctx_512, g_xattn, g_ffn = _rec_inputs()

    def _L0_xattn_setup():
        import jax, jax.numpy as jnp
        import numpy as np
        B, S, H, NH, L = (2, 256, 256, 16, 64)
        HD = H // NH
        key = jax.random.key(seed)
        k1, k2, k3, k4, k5 = jax.random.split(key, 5)
        scale = 0.02
        return {'q': jax.random.normal(k1, (B, S, H), dtype=jnp.float32), 'latent_kv': jax.random.normal(k2, (B, S, L), dtype=jnp.float32), 'Wq': jax.random.normal(k3, (H, H), dtype=jnp.float32) * scale, 'Wkv_expand': jax.random.normal(k4, (2 * H, L), dtype=jnp.float32) * scale, 'Wout': jax.random.normal(k5, (H, H), dtype=jnp.float32) * scale}
    _L0_xattn_all = _L0_xattn_setup()
    _L0_xattn_in = {k: v for k, v in _L0_xattn_all.items() if k in ('Wq', 'Wkv_expand', 'Wout')}
    del _L0_xattn_all

    def _L0_ffn_setup():
        import jax, jax.numpy as jnp
        import numpy as np
        HIDDEN = 256
        INTER = 176
        N_EXPERTS = 8
        TOP_K = 2
        BSZ, SEQ = (1, 256)
        key = jax.random.key(seed)
        k1, k2, k3, k4, k5 = jax.random.split(key, 5)
        scale_h = 1.0 / np.sqrt(HIDDEN)
        scale_i = 1.0 / np.sqrt(INTER)
        return {'hidden_states': jax.random.normal(k1, (BSZ, SEQ, HIDDEN), dtype=jnp.float32), 'router_w': jax.random.uniform(k2, (N_EXPERTS, HIDDEN), jnp.float32, -scale_h, scale_h), 'w_gate': jax.random.uniform(k3, (N_EXPERTS, INTER, HIDDEN), jnp.float32, -scale_h, scale_h), 'w_up': jax.random.uniform(k4, (N_EXPERTS, INTER, HIDDEN), jnp.float32, -scale_h, scale_h), 'w_down': jax.random.uniform(k5, (N_EXPERTS, HIDDEN, INTER), jnp.float32, -scale_i, scale_i)}
    _L0_ffn_all = _L0_ffn_setup()
    _L0_ffn_in = {k: v for k, v in _L0_ffn_all.items() if k in ('router_w', 'w_gate', 'w_up', 'w_down')}
    del _L0_ffn_all

    def _L1_xattn_setup():
        import jax, jax.numpy as jnp
        import numpy as np
        B, S, L = (2, 128, 128)
        DIM_Q, H, K, D_C, D_CQ, R = (256, 16, 128, 64, 192, 64)

        def _rope_tables(length, dim):
            inv = 1.0 / 10000.0 ** (jnp.arange(0, dim, 2, dtype=jnp.float32) / dim)
            f = jnp.arange(length, dtype=jnp.float32)[:, None] * inv[None, :]
            sin = jnp.repeat(jnp.sin(f), 2, axis=-1)
            cos = jnp.repeat(jnp.cos(f), 2, axis=-1)
            return (sin, cos)

        def _rotate_half(x):
            half = x.shape[-1] // 2
            return jnp.concatenate([-x[..., half:], x[..., :half]], axis=-1)

        def _apply_rope(x, sin, cos):
            return x * cos + _rotate_half(x) * sin
        key = jax.random.key(seed)
        ks = jax.random.split(key, 8)
        return {'hidden_q': jax.random.normal(ks[0], (B, S, DIM_Q), jnp.float32), 'kv_c': jax.random.normal(ks[1], (B, L, D_C), jnp.float32), 'Wq': jax.random.normal(ks[2], (H * K, DIM_Q), jnp.float32) / np.sqrt(DIM_Q).astype(np.float32), 'w_kc_q': jax.random.normal(ks[3], (H, K, D_CQ), jnp.float32) / np.sqrt(K).astype(np.float32), 'w_kc_kv': jax.random.normal(ks[4], (H, K, D_C), jnp.float32) / np.sqrt(K).astype(np.float32), 'W_qr': jax.random.normal(ks[5], (H, D_CQ, R), jnp.float32) / np.float32(np.sqrt(D_CQ) * np.sqrt(R)), 'W_kr': jax.random.normal(ks[6], (H, D_C, R), jnp.float32) / np.sqrt(D_C).astype(np.float32), 'Wo': jax.random.normal(ks[7], (DIM_Q, H * K), jnp.float32) / np.sqrt(H * K).astype(np.float32)}
    _L1_xattn_all = _L1_xattn_setup()
    _L1_xattn_in = {k: v for k, v in _L1_xattn_all.items() if k in ('Wq', 'w_kc_q', 'w_kc_kv', 'W_qr', 'W_kr', 'Wo')}
    del _L1_xattn_all

    def _L1_ffn_setup():
        import jax, jax.numpy as jnp
        import numpy as np
        B, S, D, F = (4, 256, 256, 1024)
        EPS = 1e-05

        def activation_quant(x):
            scale = 127.0 / jnp.clip(jnp.max(jnp.abs(x), axis=-1, keepdims=True), EPS, None)
            return jnp.clip(jnp.round(x * scale), -128.0, 127.0) / scale

        def weight_quant(w):
            scale = 1.0 / jnp.clip(jnp.mean(jnp.abs(w)), EPS, None)
            return jnp.clip(jnp.round(w * scale), -1.0, 1.0) / scale

        def bitlinear(x, w, b):
            xq = activation_quant(x)
            wq = weight_quant(w)
            return jnp.einsum('bsd,fd->bsf', xq, wq) + b

        def layernorm(x, gamma, beta):
            mu = jnp.mean(x, axis=-1, keepdims=True)
            var = jnp.var(x, axis=-1, keepdims=True)
            return (x - mu) * jax.lax.rsqrt(var + EPS) * gamma + beta
        key = jax.random.key(seed)
        ks = jax.random.split(key, 7)
        return {'x': jax.random.normal(ks[0], (B, S, D), dtype=jnp.float32), 'w1': jax.random.normal(ks[1], (F, D), dtype=jnp.float32) * D ** (-0.5), 'b1': jax.random.normal(ks[2], (F,), dtype=jnp.float32) * 0.01, 'gamma': jnp.ones((F,), dtype=jnp.float32), 'beta': jnp.zeros((F,), dtype=jnp.float32), 'w2': jax.random.normal(ks[3], (D, F), dtype=jnp.float32) * F ** (-0.5), 'b2': jax.random.normal(ks[4], (D,), dtype=jnp.float32) * 0.01}
    _L1_ffn_all = _L1_ffn_setup()
    _L1_ffn_in = {k: v for k, v in _L1_ffn_all.items() if k in ('w1', 'b1', 'gamma', 'beta', 'w2', 'b2')}
    del _L1_ffn_all
    return {'x': x, 'ctx_512': ctx_512, 'g_xattn': g_xattn, 'g_ffn': g_ffn, 'L0_xattn_Wq': _L0_xattn_in['Wq'], 'L0_xattn_Wkv_expand': _L0_xattn_in['Wkv_expand'], 'L0_xattn_Wout': _L0_xattn_in['Wout'], 'L0_ffn_router_w': _L0_ffn_in['router_w'], 'L0_ffn_w_gate': _L0_ffn_in['w_gate'], 'L0_ffn_w_up': _L0_ffn_in['w_up'], 'L0_ffn_w_down': _L0_ffn_in['w_down'], 'L1_xattn_Wq': _L1_xattn_in['Wq'], 'L1_xattn_w_kc_q': _L1_xattn_in['w_kc_q'], 'L1_xattn_w_kc_kv': _L1_xattn_in['w_kc_kv'], 'L1_xattn_W_qr': _L1_xattn_in['W_qr'], 'L1_xattn_W_kr': _L1_xattn_in['W_kr'], 'L1_xattn_Wo': _L1_xattn_in['Wo'], 'L1_ffn_w1': _L1_ffn_in['w1'], 'L1_ffn_b1': _L1_ffn_in['b1'], 'L1_ffn_gamma': _L1_ffn_in['gamma'], 'L1_ffn_beta': _L1_ffn_in['beta'], 'L1_ffn_w2': _L1_ffn_in['w2'], 'L1_ffn_b2': _L1_ffn_in['b2']}

def reference(x, ctx_512, g_xattn, g_ffn, L0_xattn_Wq, L0_xattn_Wkv_expand, L0_xattn_Wout, L0_ffn_router_w, L0_ffn_w_gate, L0_ffn_w_up, L0_ffn_w_down, L1_xattn_Wq, L1_xattn_w_kc_q, L1_xattn_w_kc_kv, L1_xattn_W_qr, L1_xattn_W_kr, L1_xattn_Wo, L1_ffn_w1, L1_ffn_b1, L1_ffn_gamma, L1_ffn_beta, L1_ffn_w2, L1_ffn_b2):
    import jax
    import jax.numpy as jnp

    def _L0_xattn_ref(q, latent_kv, Wq, Wkv_expand, Wout):
        import jax, jax.numpy as jnp
        import numpy as np
        B, S, H, NH, L = (2, 256, 256, 16, 64)
        HD = H // NH
        b, sq, _ = q.shape
        sk = latent_kv.shape[1]
        qp = q @ Wq.T
        kv = latent_kv @ Wkv_expand.T
        k, v = jnp.split(kv, 2, axis=-1)
        qh = qp.reshape(b, sq, NH, HD).transpose(0, 2, 1, 3)
        kh = k.reshape(b, sk, NH, HD).transpose(0, 2, 1, 3)
        vh = v.reshape(b, sk, NH, HD).transpose(0, 2, 1, 3)
        inv_sqrt_d = 1.0 / jnp.sqrt(jnp.float32(HD))
        scores = jnp.einsum('bhqd,bhkd->bhqk', qh, kh) * inv_sqrt_d
        causal = jnp.tril(jnp.ones((sq, sk), dtype=bool))
        scores = jnp.where(causal, scores, jnp.finfo(scores.dtype).min)
        attn = jax.nn.softmax(scores, axis=-1)
        out = jnp.einsum('bhqk,bhkd->bhqd', attn, vh)
        out = out.transpose(0, 2, 1, 3).reshape(b, sq, H)
        return out @ Wout.T

    def _L0_ffn_ref(hidden_states, router_w, w_gate, w_up, w_down):
        import jax, jax.numpy as jnp
        import numpy as np
        HIDDEN = 256
        INTER = 176
        N_EXPERTS = 8
        TOP_K = 2
        BSZ, SEQ = (1, 256)
        B, S, H = hidden_states.shape
        x = hidden_states.reshape(-1, H)
        T = x.shape[0]
        logits = jnp.einsum('th,eh->te', x.astype(jnp.float32), router_w.astype(jnp.float32))
        probs = jax.nn.softmax(logits, axis=-1)
        scores, topk_idx = jax.lax.top_k(probs, TOP_K)
        topk_w = scores / (jnp.sum(scores, axis=-1, keepdims=True) + 1e-20)
        g = jnp.einsum('th,eih->tei', x, w_gate)
        u = jnp.einsum('th,eih->tei', x, w_up)
        act = jax.nn.silu(g) * u
        y = jnp.einsum('tei,ehi->teh', act, w_down)
        comb = jnp.zeros((T, N_EXPERTS), x.dtype).at[jnp.arange(T)[:, None], topk_idx].set(topk_w.astype(x.dtype))
        out = jnp.einsum('te,teh->th', comb, y)
        return out.reshape(B, S, H)

    def _L1_xattn_ref(hidden_q, kv_c, Wq, w_kc_q, w_kc_kv, W_qr, W_kr, Wo):
        import jax, jax.numpy as jnp
        import numpy as np
        B, S, L = (2, 128, 128)
        DIM_Q, H, K, D_C, D_CQ, R = (256, 16, 128, 64, 192, 64)

        def _rope_tables(length, dim):
            inv = 1.0 / 10000.0 ** (jnp.arange(0, dim, 2, dtype=jnp.float32) / dim)
            f = jnp.arange(length, dtype=jnp.float32)[:, None] * inv[None, :]
            sin = jnp.repeat(jnp.sin(f), 2, axis=-1)
            cos = jnp.repeat(jnp.cos(f), 2, axis=-1)
            return (sin, cos)

        def _rotate_half(x):
            half = x.shape[-1] // 2
            return jnp.concatenate([-x[..., half:], x[..., :half]], axis=-1)

        def _apply_rope(x, sin, cos):
            return x * cos + _rotate_half(x) * sin
        Bv, Sv, _ = hidden_q.shape
        _, Lv, _ = kv_c.shape
        q_hk = (hidden_q @ Wq.T).reshape(Bv, Sv, H, K)
        q_big = jnp.einsum('bshk,hkq->bshq', q_hk, w_kc_q)
        sin_q, cos_q = _rope_tables(Sv, D_CQ)
        q_big = _apply_rope(q_big, sin_q[None, :, None, :], cos_q[None, :, None, :])
        sin_k, cos_k = _rope_tables(Lv, D_C)
        kv_r = _apply_rope(kv_c, sin_k[None], cos_k[None])
        q_r = jnp.einsum('bshq,hqr->bhsr', q_big, W_qr)
        k_r = jnp.einsum('bld,hdr->bhlr', kv_r, W_kr)
        scores = jnp.einsum('bhsr,bhlr->bhsl', q_r, k_r)
        attn = jax.nn.softmax(scores, axis=-1)
        ctx_c = jnp.einsum('bhsl,bld->bhsd', attn, kv_r)
        ctx_lat = jnp.einsum('bhsd,hkd->bhsk', ctx_c, w_kc_kv)
        ctx = ctx_lat.transpose(0, 2, 1, 3).reshape(Bv, Sv, H * K)
        return ctx @ Wo.T

    def _L1_ffn_ref(x, w1, b1, gamma, beta, w2, b2):
        import jax, jax.numpy as jnp
        import numpy as np
        B, S, D, F = (4, 256, 256, 1024)
        EPS = 1e-05

        def activation_quant(x):
            scale = 127.0 / jnp.clip(jnp.max(jnp.abs(x), axis=-1, keepdims=True), EPS, None)
            return jnp.clip(jnp.round(x * scale), -128.0, 127.0) / scale

        def weight_quant(w):
            scale = 1.0 / jnp.clip(jnp.mean(jnp.abs(w)), EPS, None)
            return jnp.clip(jnp.round(w * scale), -1.0, 1.0) / scale

        def bitlinear(x, w, b):
            xq = activation_quant(x)
            wq = weight_quant(w)
            return jnp.einsum('bsd,fd->bsf', xq, wq) + b

        def layernorm(x, gamma, beta):
            mu = jnp.mean(x, axis=-1, keepdims=True)
            var = jnp.var(x, axis=-1, keepdims=True)
            return (x - mu) * jax.lax.rsqrt(var + EPS) * gamma + beta
        h = bitlinear(x, w1, b1)
        h = jax.nn.gelu(h, approximate=False)
        h = layernorm(h, gamma, beta)
        return bitlinear(h, w2, b2)
    x = x + jnp.tanh(g_xattn[0]) * _L0_xattn_ref(_layernorm(x, axis=-1), ctx_512, L0_xattn_Wq, L0_xattn_Wkv_expand, L0_xattn_Wout)
    x = x + jnp.tanh(g_ffn[0]) * _L0_ffn_ref(_layernorm(x, axis=-1), L0_ffn_router_w, L0_ffn_w_gate, L0_ffn_w_up, L0_ffn_w_down)
    x = x + jnp.tanh(g_xattn[1]) * _L1_xattn_ref(_layernorm(x, axis=-1), ctx_512, L1_xattn_Wq, L1_xattn_w_kc_q, L1_xattn_w_kc_kv, L1_xattn_W_qr, L1_xattn_W_kr, L1_xattn_Wo)
    x = x + jnp.tanh(g_ffn[1]) * _L1_ffn_ref(_layernorm(x, axis=-1), L1_ffn_w1, L1_ffn_b1, L1_ffn_gamma, L1_ffn_beta, L1_ffn_w2, L1_ffn_b2)
    return x

_drawn_inputs = setup_inputs


def setup_inputs(seed=0):
    import zlib

    import numpy as np

    out = dict(_drawn_inputs(seed))
    spreads = {'g_ffn': (-1.0, 0.2), 'L1_ffn_gamma': (1.0, 0.2), 'L1_ffn_beta': (0.0, 0.1)}
    factors = {'L0_xattn_Wq': 50.435, 'L1_ffn_b1': 4.82, 'L1_ffn_b2': 8.0}
    for name, (base, spread) in spreads.items():
        noise = np.random.default_rng([zlib.crc32(name.encode()), seed]).standard_normal(out[name].shape)
        drawn = base * np.exp(spread * noise) if base else spread * noise
        out[name] = jnp.asarray(drawn.astype(out[name].dtype))
    for name, factor in factors.items():
        out[name] = (out[name] * factor).astype(out[name].dtype)
    return out
```

```python
from contextlib import ExitStack

import concourse.bass as bass
from concourse import mybir

F32 = mybir.dt.float32
F32R = mybir.dt.float32r
BF16 = mybir.dt.bfloat16
U32 = mybir.dt.uint32
ALU = mybir.AluOpType
ACT = mybir.ActivationFunctionType
AX = mybir.AxisListType

B, S, D = 32, 100, 256
LK, DL = 1444, 64
G = 4
NG = B // G
T = G * S
KT = D // 128
H = 16
HD = D // H
E, I = 8, 176
IT = E * I // 128
HK, CQ, R = 128, 192, 64
HALF = CQ // 2
NT = 12
KP = 121
CH = 2
CQS = H * S // CH
QT = [128] * 6 + [32]
F = 1024
EPS = 1e-5
PRIMED = 1
ROUND = 12582912.0


def keys_of(r):
    return KP if r < 4 else KP - 1


def layernorm_stats(v, x, stats, mv, ve, n, done, at, carrier):
    for j in range(n):
        v.bn_stats(stats[:, j, :], x(j)).then_inc(done, 1)
    v.wait_ge(done, PRIMED + at + n)
    v.sem_inc(carrier, 1)
    for j in range(n):
        v.bn_aggr(mv[:, j, :], stats[:, j, :]).then_inc(done, 1)
    v.wait_ge(done, PRIMED + at + 2 * n)
    v.tensor_scalar(ve[:, 0:n], mv[:, 0:n, 1], EPS, None, ALU.add).then_inc(done, 1)


def phase_load(nc, ctx, sem, io, m):
    loaded, gates = sem("inputs_loaded"), sem("gates_ready")
    with nc.Block() as block:
        @block.sync
        def _(sp):
            for c in range(4):
                sp.dma_start(m.x[:, c * 8 * D:(c + 1) * 8 * D].rearrange("s (b d) -> s b d", b=8),
                             io["x"][c * 8:(c + 1) * 8].rearrange("b s d -> s b d")).then_inc(loaded, 16)
            sp.dma_start(m.ident[:], io["ident"]).then_inc(loaded, 16)
            sp.dma_start(m.gates[:, 0:2], io["g_xattn"].partition_broadcast(128)).then_inc(loaded, 16)
            sp.dma_start(m.gates[:, 2:4], io["g_ffn"].partition_broadcast(128)).then_inc(loaded, 16)
            sp.wait_ge(loaded, 16 * 7)

        @block.scalar
        def _(a):
            a.wait_ge(loaded, 16 * 7)
            a.activation(m.tg[:], m.gates[:], ACT.Tanh).then_inc(gates, 1)

        @block.vector
        def _(v):
            v.memset(m.mhalf[:], -0.5).then_inc(gates, 1)
            v.wait_ge(loaded, 16 * 7)
            v.tensor_copy(m.identr[:], m.ident[:]).then_inc(gates, 1)
            v.tensor_copy(m.identb[:], m.ident[:]).then_inc(gates, 1)


def phase_l0_attention(nc, outer, sem, io, m):
    NQ = 4
    counters = []
    with ExitStack() as ctx:
        sb = lambda n, s, d=F32: ctx.enter_context(nc.sbuf_tensor(n, s, d))
        ps = lambda n, s, d=F32: ctx.enter_context(nc.psum_tensor(n, s, d))

        def count(name):
            counters.append(sem(name))
            return counters[-1]
        wq_raw, wk_raw, wv_raw = sb("a_wq_raw", [128, KT, D]), sb("a_wk_raw", [DL, D]), sb("a_wv_raw", [DL, D])
        wq = [sb(f"a_wq{i}", [128, KT, D], F32R) for i in range(2)]
        wk = [sb(f"a_wk{i}", [DL, D], F32R) for i in range(2)]
        wv = [sb(f"a_wv{i}", [DL, D], F32R) for i in range(2)]
        wo = sb("a_wo", [128, KT, D])
        lat = sb("a_lat", [S, B * DL])
        mask_raw = sb("a_mask_raw", [S, S])
        mask = sb("a_mask", [S, 4, S], BF16)
        headsel_raw, headsel = sb("a_headsel_raw", [128, 8]), sb("a_headsel", [128, 8, S])
        latg = sb("a_latg", [S, G + 1, DL])
        stats, mv, ve, rstd = sb("a_stats", [S, G, 6]), sb("a_mv", [S, G, 2]), sb("a_ve", [S, G]), sb("a_rstd", [S, G])
        xn = sb("a_xn", [S, G, D])
        xt = [sb(f"a_xt{i}", [128, KT, T], F32R) for i in range(2)]
        latt = [sb(f"a_latt{i}", [DL, T], F32R) for i in range(2)]
        qt = sb("a_qt", [128, KT, T])
        kt = sb("a_kt", [128, KT, T])
        kbd = [sb(f"a_kbd{i}", [128, KT, 8, S]) for i in range(2)]
        va = sb("a_va", [S, G, H, HD + 1])
        mx = sb("a_mx", [S, NQ, 4])
        diff = sb("a_diff", [S, NQ, 4, S])
        prob = sb("a_prob", [S, NQ, 4, S])
        pt = sb("a_pt", [S, 2, 4, S])
        rden = sb("a_rden", [S, H])
        cn = sb("a_cn", [S, D])
        ct = sb("a_ct", [128, KT, S])
        s_ps = ps("a_s_ps", [128, 4, 512])
        p_ps = ps("a_p_ps", [128, 2, 512])
        o_ps = ps("a_o_ps", [128, 512])
        f_ps = ps("a_f_ps", [128, 512])
        w_loaded, w_ready = sem("a_w_loaded"), count("a_w_ready")
        ln, rstd_ready, xn_ready = count("a_ln"), count("a_rstd_ready"), count("a_xn_ready")
        dense_mm, dense_out = count("a_dense_mm"), count("a_dense_out")
        kbd_ready, split_hi, latg_ready = count("a_kbd_ready"), count("a_split_hi"), count("a_latg_ready")
        s_ready, max_ready, diff_ready = count("a_s_ready"), count("a_max_ready"), count("a_diff_ready")
        prob_ready, pt_ready, pt_copied, pv_done = count("a_prob_ready"), count("a_pt_ready"), count("a_pt_copied"), count("a_pv_done")
        rden_ready, cn_ready, ct_ready, ct_copied = count("a_rden_ready"), count("a_cn_ready"), count("a_ct_ready"), count("a_ct_copied")
        f_ready, x_added = count("a_f_ready"), count("a_x_added")
        NLOAD = 7
        NW = 10
        ND = 9

        with nc.Block() as block:
            @block.sync
            def _(sp):
                for c in counters:
                    sp.sem_inc(c, PRIMED)
                sp.dma_start(wq_raw[:], io["L0_WqT"].rearrange("(k p) n -> p k n", p=128)).then_inc(w_loaded, 16)
                sp.dma_start(wk_raw[:], io["L0_WkvT"][:, 0:D]).then_inc(w_loaded, 16)
                sp.dma_start(wv_raw[:], io["L0_WkvT"][:, D:2 * D]).then_inc(w_loaded, 16)
                sp.dma_start(wo[:], io["L0_WoutT"].rearrange("(k p) n -> p k n", p=128)).then_inc(w_loaded, 16)
                sp.dma_start(lat[:].rearrange("s (b d) -> s b d", b=B),
                             io["ctx_512"][:, 0:S, :].rearrange("b s d -> s b d")).then_inc(w_loaded, 16)
                sp.dma_start(mask_raw[:], io["causal"]).then_inc(w_loaded, 16)
                sp.dma_start(headsel_raw[:], io["headsel"]).then_inc(w_loaded, 16)
                sp.wait_ge(w_loaded, 16 * NLOAD)

            @block.gpsimd
            def _(g):
                g.wait_ge(w_loaded, 16 * NLOAD)
                with g.Fori(0, NG) as it:
                    g.wait_ge(dense_mm, PRIMED + it * ND)
                    g.tensor_copy(latg[:, 0:G, :].rearrange("s j d -> s (j d)"), lat[:, bass.ds(it * G * DL, G * DL)]).then_inc(latg_ready, 1)
                    g.wait_ge(ln, PRIMED + (it + 1) * (2 * G + 1))
                    g.tensor_tensor(rstd[:], ve[:], m.mhalf[0:S, 0:G], ALU.pow).then_inc(rstd_ready, 1)

            @block.vector
            def _(v):
                v.wait_ge(w_loaded, 16 * NLOAD)
                for raw, w in ((wq_raw, wq), (wk_raw, wk), (wv_raw, wv)):
                    v.tensor_copy(w[0][:], raw[:]).then_inc(w_ready, 1)
                v.wait_ge(w_ready, PRIMED + 3)
                for raw, w in ((wq_raw, wq), (wk_raw, wk), (wv_raw, wv)):
                    v.tensor_tensor(w[1][:], raw[:], w[0][:].bitcast(F32), ALU.subtract).then_inc(w_ready, 1)
                v.tensor_copy(mask[:], mask_raw[:].unsqueeze(1).broadcast_to((S, 4, S))).then_inc(w_ready, 1)
                v.memset(va[:, :, :, HD], 1.0).then_inc(w_ready, 1)
                v.memset(latg[:, G, :], 0.0).then_inc(w_ready, 1)
                v.tensor_copy(headsel[:], headsel_raw[:].unsqueeze(2).broadcast_to((128, 8, S))).then_inc(w_ready, 1)
                v.wait_ge(w_ready, PRIMED + NW)
                with v.Fori(0, NG) as it:
                    xg = lambda j: m.x[:, bass.ds((it * G + j) * D, D)]
                    layernorm_stats(v, xg, stats, mv, ve, G, ln, it * (2 * G + 1), m.carrier)
                    v.wait_ge(rstd_ready, PRIMED + it + 1)
                    for j in range(G):
                        v.tensor_scalar(xn[:, j, :], xg(j), mv[:, j, 0:1], rstd[:, j:j + 1],
                                        ALU.subtract, ALU.mult).then_inc(xn_ready, 1)
                    for n in range(ND):
                        v.wait_ge(dense_mm, PRIMED + it * ND + n + 1)
                        src = p_ps[:, n % 2, 0:T]
                        if n < 3:
                            hi, lo = (xt[0][:, n, :], xt[1][:, n, :]) if n < 2 else (latt[0][:], latt[1][:])
                            src = src if n < 2 else p_ps[0:DL, 0, 0:T]
                            v.tensor_copy(hi, src).then_inc(split_hi, 1)
                            v.wait_ge(split_hi, PRIMED + it * 3 + n + 1)
                            v.tensor_tensor(lo, src, hi.bitcast(F32), ALU.subtract).then_inc(dense_out, 1)
                        elif n < 5:
                            v.tensor_copy(qt[:, n - 3, :], src).then_inc(dense_out, 1)
                        elif n < 7:
                            v.tensor_copy(kt[:, n - 5, :], src).then_inc(dense_out, 1)
                        else:
                            for j in range(2):
                                ins = v.tensor_copy(va[:, 2 * (n - 7) + j, :, 0:HD],
                                                    p_ps[0:S, n % 2, j * D:(j + 1) * D].rearrange("p (h d) -> p h d", h=H))
                            ins.then_inc(dense_out, 1)

                    def block_keys(b):
                        if b >= 2:
                            v.wait_ge(s_ready, PRIMED + (it * G + b - 1) * NQ)
                        for k in range(KT):
                            ins = v.tensor_tensor(kbd[b % 2][:, k], headsel[:],
                                                  kt[:, k, b * S:(b + 1) * S].unsqueeze(1).broadcast_to((128, 8, S)),
                                                  ALU.mult)
                        ins.then_inc(kbd_ready, 1)

                    v.wait_ge(dense_out, PRIMED + it * ND + 7)
                    block_keys(0)
                    block_keys(1)
                    for b in range(G):
                        for q in range(NQ):
                            n = it * G * NQ + b * NQ + q
                            v.wait_ge(s_ready, PRIMED + n + 1)
                            sc = s_ps[0:S, q, 0:4 * S].rearrange("p (h k) -> p h k", h=4)
                            v.tensor_reduce(mx[:, q, :], sc, AX.X, ALU.max).then_inc(max_ready, 1)
                            v.wait_ge(max_ready, PRIMED + n + 1)
                            if b > 0:
                                v.wait_ge(prob_ready, PRIMED + n - NQ + 1)
                            v.tensor_tensor(diff[:, q], sc, mx[:, q, :].unsqueeze(2).broadcast_to((S, 4, S)),
                                            ALU.subtract).then_inc(diff_ready, 1)
                        if b + 2 < G:
                            block_keys(b + 2)
                        nb = it * G + b
                        v.wait_ge(pv_done, PRIMED + (nb + 1) * NQ)
                        o = o_ps[0:S, 0:H * (HD + 1)].rearrange("p (h d) -> p h d", h=H)
                        v.reciprocal(rden[:], o[:, :, HD]).then_inc(rden_ready, 1)
                        v.wait_ge(rden_ready, PRIMED + nb + 1)
                        v.tensor_tensor(cn[:].rearrange("p (h d) -> p h d", h=H), o[:, :, 0:HD],
                                        rden[:].unsqueeze(2).broadcast_to((S, H, HD)), ALU.mult).then_inc(cn_ready, 1)
                        v.wait_ge(f_ready, PRIMED + nb + 1)
                        v.scalar_tensor_tensor(xg(b), f_ps[0:S, 0:D], m.tg[0:S, 0:1], xg(b), ALU.mult, ALU.add).then_inc(x_added, 1)
                    v.wait_ge(x_added, PRIMED + (it + 1) * G)

            @block.scalar
            def _(a):
                with a.Fori(0, NG) as it:
                    for b in range(G):
                        def copy_pt(q):
                            n = it * G * NQ + b * NQ + q
                            a.wait_ge(pt_ready, PRIMED + n + 1)
                            if b * NQ + q >= 2:
                                a.wait_ge(pv_done, PRIMED + n - 1)
                            a.activation(pt[:, q % 2], p_ps[0:S, q % 2, 0:4 * S].rearrange("p (h k) -> p h k", h=4),
                                         ACT.Copy).then_inc(pt_copied, 1)
                        for q in range(NQ):
                            n = it * G * NQ + b * NQ + q
                            a.wait_ge(diff_ready, PRIMED + n + 1)
                            if b > 0:
                                a.wait_ge(pt_ready, PRIMED + n - NQ + 1)
                            a.activation(prob[:, q], diff[:, q], ACT.Exp, scale=HD ** -0.5).then_inc(prob_ready, 1)
                            if q > 0:
                                copy_pt(q - 1)
                        copy_pt(NQ - 1)
                        nb = it * G + b
                        a.wait_ge(ct_ready, PRIMED + nb + 1)
                        a.activation(ct[:], f_ps[:, 256:256 + KT * S].rearrange("p (k s) -> p k s", k=KT), ACT.Copy).then_inc(ct_copied, 1)

            @block.tensor
            def _(pe):
                pe.wait_ge(w_ready, PRIMED + NW)
                with pe.Fori(0, NG) as it:
                    def out_of(n):
                        if n >= 2:
                            pe.wait_ge(dense_out, PRIMED + it * ND + n - 1)
                        else:
                            pe.wait_ge(pt_copied, PRIMED + it * G * NQ)
                        return p_ps[:, n % 2, 0:T]
                    pe.wait_ge(xn_ready, PRIMED + (it + 1) * G)
                    for k in range(KT):
                        o = out_of(k)
                        for j in range(G):
                            mm = pe.transpose(o[:, j * S:(j + 1) * S], xn[:, j, k * 128:(k + 1) * 128], m.ident[0:S, 0:S])
                        mm.then_inc(dense_mm, 1)
                    o = out_of(2)
                    pe.wait_ge(latg_ready, PRIMED + it + 1)
                    for j in range(G):
                        mm = pe.transpose(o[:, j * S:(j + 1) * S], latg[:, j:j + 2, :], m.ident[0:S, 0:S])
                    mm.then_inc(dense_mm, 1)
                    pe.wait_ge(dense_out, PRIMED + it * ND + 2)
                    for n in range(2):
                        o = out_of(3 + n)
                        for i, (w, x) in enumerate(((0, 0), (0, 1), (1, 0))):
                            for k in range(KT):
                                mm = pe.matmul(o, wq[w][:, k, n * 128:(n + 1) * 128], xt[x][:, k, :],
                                               start=(i == 0 and k == 0), stop=(i == 2 and k == KT - 1))
                        mm.then_inc(dense_mm, 1)
                    pe.wait_ge(dense_out, PRIMED + it * ND + 3)
                    for n in range(2):
                        o = out_of(5 + n)
                        for i, (w, x) in enumerate(((0, 0), (0, 1), (1, 0))):
                            mm = pe.matmul(o, wk[w][:, n * 128:(n + 1) * 128], latt[x][:], start=(i == 0), stop=(i == 2))
                        mm.then_inc(dense_mm, 1)
                    for n in range(2):
                        out_of(7 + n)
                        for j in range(2):
                            cols = slice((2 * n + j) * S, (2 * n + j + 1) * S)
                            for i, (w, x) in enumerate(((0, 0), (0, 1), (1, 0))):
                                mm = pe.matmul(p_ps[0:S, (7 + n) % 2, j * D:(j + 1) * D], latt[x][:, cols], wv[w][:],
                                               start=(i == 0), stop=(i == 2))
                        mm.then_inc(dense_mm, 1)

                    def scores(b, q):
                        n = it * G * NQ + b * NQ + q
                        pe.wait_ge(kbd_ready, PRIMED + it * G + b + 1)
                        pe.wait_ge(diff_ready, PRIMED + n - NQ + 1 if b > 0 else it * G * NQ)
                        o = s_ps[0:S, q, 0:4 * S]
                        pe.matmul(o, m.identb[0:S, 0:S], mask[:].rearrange("p h k -> p (h k)"), start=True, stop=False)
                        mm = pe.matmul(o, qt[:, q // 2, b * S:(b + 1) * S],
                                       kbd[b % 2][:, q // 2, 4 * (q % 2):4 * (q % 2) + 4, :].rearrange("p h k -> p (h k)"),
                                       start=False, stop=True)
                        mm.then_inc(s_ready, 1)

                    pe.wait_ge(dense_out, PRIMED + (it + 1) * ND)
                    for q in range(NQ):
                        scores(0, q)
                    for b in range(G):
                        nb = it * G + b

                        def probs_value(q):
                            n = nb * NQ + q
                            pe.wait_ge(pt_copied, PRIMED + n + 1)
                            if q == 0:
                                pe.wait_ge(cn_ready, PRIMED + nb)
                            for h in range(4):
                                mm = pe.matmul(o_ps[0:S, (4 * q + h) * (HD + 1):(4 * q + h + 1) * (HD + 1)],
                                               pt[:, q % 2, h, :], va[:, b, 4 * q + h, :], start=True, stop=True)
                            mm.then_inc(pv_done, 1)
                        for q in range(NQ):
                            n = nb * NQ + q
                            if b + 1 < G:
                                scores(b + 1, q)
                            pe.wait_ge(prob_ready, PRIMED + n + 1)
                            if b * NQ + q >= 2:
                                pe.wait_ge(pt_copied, PRIMED + n - 1)
                            for h in range(4):
                                mm = pe.transpose(p_ps[0:S, q % 2, h * S:(h + 1) * S], prob[:, q, h, :], m.ident[0:S, 0:S])
                            mm.then_inc(pt_ready, 1)
                            if q > 0:
                                probs_value(q - 1)
                        probs_value(NQ - 1)
                        pe.wait_ge(cn_ready, PRIMED + nb + 1)
                        pe.wait_ge(x_added, PRIMED + nb)
                        for k in range(KT):
                            mm = pe.transpose(f_ps[:, 256 + k * S:256 + (k + 1) * S], cn[:, k * 128:(k + 1) * 128], m.ident[0:S, 0:S])
                        mm.then_inc(ct_ready, 1)
                        pe.wait_ge(ct_copied, PRIMED + nb + 1)
                        for k in range(KT):
                            mm = pe.matmul(f_ps[0:S, 0:D], ct[:, k, :], wo[:, k, :], start=(k == 0), stop=(k == KT - 1))
                        mm.then_inc(f_ready, 1)


def phase_moe(nc, outer, sem, io, m):
    counters = []
    with ExitStack() as ctx:
        sb = lambda n, s, d=F32: ctx.enter_context(nc.sbuf_tensor(n, s, d))
        ps = lambda n, s, d=F32: ctx.enter_context(nc.psum_tensor(n, s, d))

        def count(name):
            counters.append(sem(name))
            return counters[-1]
        EI = E * I
        raw = [sb(f"b_raw{i}", [128, KT, EI]) for i in range(2)]
        wg = [sb(f"b_wg{i}", [128, KT, EI], F32R) for i in range(2)]
        wu = [sb(f"b_wu{i}", [128, KT, EI], F32R) for i in range(2)]
        wd = sb("b_wd", [128, IT, D])
        wr_raw = sb("b_wr_raw", [128, KT, E])
        wr = [sb(f"b_wr{i}", [128, KT, E], F32R) for i in range(2)]
        expert_raw = sb("b_expert_raw", [40, IT, 128])
        expert = sb("b_expert", [40, IT, 128], F32R)
        iota8 = sb("b_iota8", [S, E])
        stats, mv, ve, rstd = sb("b_stats", [S, G, 6]), sb("b_mv", [S, G, 2]), sb("b_ve", [S, G]), sb("b_rstd", [S, G])
        xn = sb("b_xn", [S, G, D])
        xt = [sb(f"b_xt{i}", [128, KT, T], F32R) for i in range(2)]
        rmax, rdiff, rexp, rsum, rinv = (sb("b_rmax", [S, G]), sb("b_rdiff", [S, G, E]), sb("b_rexp", [S, G, E]),
                                         sb("b_rsum", [S, G]), sb("b_rinv", [S, G]))
        rprob, top, topi, topf = sb("b_rprob", [S, G, E]), sb("b_top", [S, G, 8]), sb("b_topi", [S, G, 8], U32), sb("b_topf", [S, G, 2])
        wsum, winv, wtop = sb("b_wsum", [S, G]), sb("b_winv", [S, G]), sb("b_wtop", [S, G, 2])
        comb1, comb2, comb = sb("b_comb1", [S, G, E]), sb("b_comb2", [S, G, E]), sb("b_comb", [S, G, E])
        combt = sb("b_combt", [40, T], F32R)
        silu = sb("b_silu", [128, 2, T])
        gated = sb("b_gated", [128, 2, T])
        act = sb("b_act", [128, 2, T])
        gu_ps = ps("b_gu_ps", [128, 2, 3, 512])
        y_ps = ps("b_y_ps", [128, 2, 512])
        w_loaded, w_ready, raw_split = sem("b_w_loaded"), count("b_w_ready"), count("b_raw_split")
        ln, rstd_ready, xn_ready = count("b_ln"), count("b_rstd_ready"), count("b_xn_ready")
        xt_ps_ready, split_hi, xt_ready = count("b_xt_ps_ready"), count("b_split_hi"), count("b_xt_ready")
        logits_ready, router, rexp_ready = count("b_logits_ready"), count("b_router"), count("b_rexp_ready")
        combt_ps_ready, combt_hi, combt_ready = count("b_combt_ps_ready"), count("b_combt_hi"), count("b_combt_ready")
        gate_ready, up_ready, spread_ready = count("b_gate_ready"), count("b_up_ready"), count("b_spread_ready")
        silu_ready, gated_ready, act_ready, down_done = count("b_silu_ready"), count("b_gated_ready"), count("b_act_ready"), count("b_down_done")
        x_added = count("b_x_added")
        NW = 8
        NR = 11 + 4 * G

        with nc.Block() as block:
            @block.sync
            def _(sp):
                for c in counters:
                    sp.sem_inc(c, PRIMED)
                sp.dma_start(raw[0][:], io["L0_gateT"].rearrange("(k p) n -> p k n", p=128)).then_inc(w_loaded, 16)
                sp.dma_start(raw[1][:], io["L0_upT"].rearrange("(k p) n -> p k n", p=128)).then_inc(w_loaded, 16)
                sp.dma_start(wd[:], io["L0_downT"].rearrange("(t p) n -> p t n", p=128)).then_inc(w_loaded, 16)
                sp.dma_start(wr_raw[:], io["L0_routerT"].rearrange("(k p) n -> p k n", p=128)).then_inc(w_loaded, 16)
                sp.dma_start(expert_raw[:].rearrange("p t n -> p (t n)"), io["expert_rows"]).then_inc(w_loaded, 16)
                sp.dma_start(iota8[:], io["iota8"].partition_broadcast(S)).then_inc(w_loaded, 16)
                sp.wait_ge(w_loaded, 16 * 6)

            @block.gpsimd
            def _(g):
                with g.Fori(0, NG) as it:
                    g.wait_ge(ln, PRIMED + (it + 1) * (2 * G + 1))
                    g.tensor_tensor(rstd[:], ve[:], m.mhalf[0:S, 0:G], ALU.pow).then_inc(rstd_ready, 1)

            @block.vector
            def _(v):
                v.wait_ge(w_loaded, 16 * 6)
                for r_, w in ((raw[0], wg), (raw[1], wu), (wr_raw, wr)):
                    v.tensor_copy(w[0][:], r_[:]).then_inc(w_ready, 1)
                v.wait_ge(w_ready, PRIMED + 3)
                for r_, w in ((raw[0], wg), (raw[1], wu), (wr_raw, wr)):
                    v.tensor_tensor(w[1][:], r_[:], w[0][:].bitcast(F32), ALU.subtract).then_inc(w_ready, 1)
                v.tensor_copy(expert[:], expert_raw[:]).then_inc(w_ready, 1)
                v.memset(combt[:].bitcast(F32), 0.0).then_inc(w_ready, 1)
                v.wait_ge(w_ready, PRIMED + NW)
                with v.Fori(0, NG) as it:
                    xg = lambda j: m.x[:, bass.ds((it * G + j) * D, D)]
                    layernorm_stats(v, xg, stats, mv, ve, G, ln, it * (2 * G + 1), m.carrier)
                    v.wait_ge(rstd_ready, PRIMED + it + 1)
                    for j in range(G):
                        v.tensor_scalar(xn[:, j, :], xg(j), mv[:, j, 0:1], rstd[:, j:j + 1],
                                        ALU.subtract, ALU.mult).then_inc(xn_ready, 1)
                    for k in range(KT):
                        v.wait_ge(xt_ps_ready, PRIMED + it * KT + k + 1)
                        v.tensor_copy(xt[0][:, k, :], gu_ps[:, 0, k, 0:T]).then_inc(split_hi, 1)
                        v.wait_ge(split_hi, PRIMED + it * KT + k + 1)
                        v.tensor_tensor(xt[1][:, k, :], gu_ps[:, 0, k, 0:T], xt[0][:, k, :].bitcast(F32),
                                        ALU.subtract).then_inc(xt_ready, 1)
                    n = [0]

                    def step(ins):
                        ins.then_inc(router, 1)
                        n[0] += 1

                    def settle():
                        v.wait_ge(router, PRIMED + it * NR + n[0])
                    v.wait_ge(logits_ready, PRIMED + it + 1)
                    logits = gu_ps[0:S, 0, 2, 0:G * E].rearrange("p (b e) -> p b e", b=G)
                    over = lambda a: a.unsqueeze(2).broadcast_to((S, G, E))
                    step(v.tensor_reduce(rmax[:], logits, AX.X, ALU.max))
                    settle()
                    step(v.tensor_tensor(rdiff[:], logits, over(rmax[:]), ALU.subtract))
                    v.wait_ge(rexp_ready, PRIMED + it + 1)
                    step(v.tensor_reduce(rsum[:], rexp[:], AX.X, ALU.add))
                    settle()
                    step(v.reciprocal(rinv[:], rsum[:]))
                    settle()
                    step(v.tensor_tensor(rprob[:], rexp[:], over(rinv[:]), ALU.mult))
                    settle()
                    v.sem_inc(m.carrier, 1)
                    for b in range(G):
                        step(v.max(top[:, b, :], rprob[:, b, :]))
                    settle()
                    v.sem_inc(m.carrier, 1)
                    for b in range(G):
                        step(v.max_index(topi[:, b, :], top[:, b, :], rprob[:, b, :]))
                    step(v.tensor_tensor(wsum[:], top[:, :, 0], top[:, :, 1], ALU.add))
                    settle()
                    step(v.tensor_copy(topf[:], topi[:, :, 0:2]))
                    step(v.tensor_scalar(wsum[:], wsum[:], 1e-20, None, ALU.add))
                    settle()
                    step(v.reciprocal(winv[:], wsum[:]))
                    settle()
                    step(v.tensor_tensor(wtop[:], top[:, :, 0:2], winv[:].unsqueeze(2).broadcast_to((S, G, 2)), ALU.mult))
                    settle()
                    for b in range(G):
                        step(v.tensor_scalar(comb1[:, b, :], iota8[:], topf[:, b, 0:1], wtop[:, b, 0:1], ALU.is_equal, ALU.mult))
                        step(v.tensor_scalar(comb2[:, b, :], iota8[:], topf[:, b, 1:2], wtop[:, b, 1:2], ALU.is_equal, ALU.mult))
                    settle()
                    step(v.tensor_tensor(comb[:], comb1[:], comb2[:], ALU.add))
                    assert n[0] == NR
                    v.wait_ge(combt_ps_ready, PRIMED + it + 1)
                    cps = gu_ps[0:E, 1, 2, 0:T]
                    v.tensor_copy(combt[0:E, :], cps).then_inc(combt_hi, 1)
                    v.wait_ge(combt_hi, PRIMED + it + 1)
                    v.tensor_tensor(combt[32:32 + E, :], cps, combt[0:E, :].bitcast(F32), ALU.subtract).then_inc(combt_ready, 1)
                    for t in range(IT):
                        i = it * IT + t
                        v.wait_ge(silu_ready, PRIMED + i + 1)
                        v.wait_ge(up_ready, PRIMED + i + 1)
                        v.tensor_tensor(gated[:, t % 2, :], silu[:, t % 2, :], gu_ps[:, t % 2, 1, 0:T], ALU.mult).then_inc(gated_ready, 1)
                        v.wait_ge(gated_ready, PRIMED + i + 1)
                        v.wait_ge(spread_ready, PRIMED + i + 1)
                        if t >= 2:
                            v.wait_ge(down_done, PRIMED + i - 1)
                        v.tensor_tensor(act[:, t % 2, :], gated[:, t % 2, :], gu_ps[:, t % 2, 2, 0:T], ALU.mult).then_inc(act_ready, 1)
                    v.wait_ge(down_done, PRIMED + (it + 1) * IT)
                    for h in range(2):
                        xs = m.x[:, bass.ds((it * G + 2 * h) * D, 2 * D)]
                        v.scalar_tensor_tensor(xs, y_ps[0:S, h, :], m.tg[0:S, 2:3], xs, ALU.mult, ALU.add).then_inc(x_added, 1)
                    v.wait_ge(x_added, PRIMED + (it + 1) * 2)

            @block.scalar
            def _(a):
                with a.Fori(0, NG) as it:
                    a.wait_ge(router, PRIMED + it * NR + 2)
                    a.activation(rexp[:], rdiff[:], ACT.Exp).then_inc(rexp_ready, 1)
                    for t in range(IT):
                        i = it * IT + t
                        a.wait_ge(gate_ready, PRIMED + i + 1)
                        if t >= 2:
                            a.wait_ge(gated_ready, PRIMED + i - 1)
                        a.activation(silu[:, t % 2, :], gu_ps[:, t % 2, 0, 0:T], ACT.Silu).then_inc(silu_ready, 1)

            @block.tensor
            def _(pe):
                pe.wait_ge(w_ready, PRIMED + NW)
                parts = ((0, 0), (0, 1), (1, 0))
                with pe.Fori(0, NG) as it:
                    pe.wait_ge(xn_ready, PRIMED + (it + 1) * G)
                    for k in range(KT):
                        for j in range(G):
                            mm = pe.transpose(gu_ps[:, 0, k, j * S:(j + 1) * S], xn[:, j, k * 128:(k + 1) * 128], m.ident[0:S, 0:S])
                        mm.then_inc(xt_ps_ready, 1)
                    pe.wait_ge(xt_ready, PRIMED + (it + 1) * KT)
                    for b in range(G):
                        for i, (w, x) in enumerate(parts):
                            for k in range(KT):
                                mm = pe.matmul(gu_ps[0:S, 0, 2, b * E:(b + 1) * E], xt[x][:, k, b * S:(b + 1) * S], wr[w][:, k, :],
                                               start=(i == 0 and k == 0), stop=(i == 2 and k == KT - 1))
                    mm.then_inc(logits_ready, 1)

                    def rows_of(t):
                        n = it * IT + t
                        if t >= 2:
                            pe.wait_ge(act_ready, PRIMED + n - 1)
                        for j, (w, done) in enumerate(((wg, gate_ready), (wu, up_ready))):
                            for i, (wi, x) in enumerate(parts):
                                for k in range(KT):
                                    mm = pe.matmul(gu_ps[:, t % 2, j, 0:T], w[wi][:, k, t * 128:(t + 1) * 128], xt[x][:, k, :],
                                                   start=(i == 0 and k == 0), stop=(i == 2 and k == KT - 1))
                            mm.then_inc(done, 1)

                    def spread(t):
                        pe.matmul(gu_ps[:, t % 2, 2, 0:T], expert[:, t, :], combt[:], start=True, stop=True).then_inc(spread_ready, 1)

                    def down(t):
                        n = it * IT + t
                        pe.wait_ge(act_ready, PRIMED + n + 1)
                        if t == 0:
                            pe.wait_ge(x_added, PRIMED + it * 2)
                        for b in range(G):
                            mm = pe.matmul(y_ps[0:S, b // 2, (b % 2) * D:(b % 2 + 1) * D], act[:, t % 2, b * S:(b + 1) * S], wd[:, t, :],
                                           start=(t == 0 and b % 2 == 0), stop=(t == IT - 1), skip_group_check=True)
                        mm.then_inc(down_done, 1)
                    rows_of(0)
                    rows_of(1)
                    pe.wait_ge(router, PRIMED + (it + 1) * NR)
                    for b in range(G):
                        mm = pe.transpose(gu_ps[0:E, 1, 2, b * S:(b + 1) * S], comb[:, b, :], m.ident[0:S, 0:S])
                    mm.then_inc(combt_ps_ready, 1)
                    pe.wait_ge(combt_ready, PRIMED + it + 1)
                    spread(0)
                    spread(1)
                    for t in range(2, IT):
                        rows_of(t)
                        spread(t)
                        down(t - 2)
                    down(IT - 2)
                    down(IT - 1)


def phase_l1_weights(nc, outer, sem, io, m):
    with ExitStack() as ctx:
        sb = lambda n, s, d=F32: ctx.enter_context(nc.sbuf_tensor(n, s, d))
        ps = lambda n, s, d=F32: ctx.enter_context(nc.psum_tensor(n, s, d))
        wq, kcq = sb("w_wq", [128, H, D]), sb("w_kcq", [128, H, CQ])
        qr, kr = sb("w_qr", [R, H, CQ]), sb("w_kr", [R, H, DL])
        kckv, wo = sb("w_kckv", [128, H, DL]), sb("w_wo", [128, H, D])
        a_ps = ps("w_a_ps", [128, 4, 512])
        b_ps = ps("w_b_ps", [128, 4, 512])
        loaded = sem("w_loaded")
        a_mm, a_hi, a_out = sem("w_a_mm"), sem("w_a_hi"), sem("w_a_out")
        m_mm, m_out, c_mm, c_out = sem("w_m_mm"), sem("w_m_out"), sem("w_c_mm"), sem("w_c_out")
        with nc.Block() as block:
            @block.sync
            def _(sp):
                sp.dma_start(wq[:], io["L1_xattn_Wq"].rearrange("(h k) d -> k h d", k=HK)).then_inc(loaded, 16)
                sp.dma_start(kcq[:], io["L1_xattn_w_kc_q"].rearrange("h k q -> k h q")).then_inc(loaded, 16)
                sp.dma_start(qr[:], io["L1_qrT"]).then_inc(loaded, 16)
                sp.dma_start(kr[:], io["L1_krT"]).then_inc(loaded, 16)
                sp.dma_start(kckv[:], io["L1_xattn_w_kc_kv"].rearrange("h k d -> k h d")).then_inc(loaded, 16)
                sp.dma_start(wo[:], io["L1_WoT"].rearrange("(h k) o -> k h o", k=HK)).then_inc(loaded, 16)
                sp.wait_ge(loaded, 16 * 6)

            @block.tensor
            def _(pe):
                pe.wait_ge(loaded, 16 * 6)
                for h in range(H):
                    if h >= 4:
                        pe.wait_ge(a_out, h - 3)
                    for k in range(KT):
                        mm = pe.matmul(a_ps[:, h % 4, k * CQ:(k + 1) * CQ], wq[:, h, k * 128:(k + 1) * 128], kcq[:, h, :], start=True, stop=True)
                    mm.then_inc(a_mm, 1)
                for h in range(H):
                    if h >= 2:
                        pe.wait_ge(m_out, h - 1)
                    for i in range(2):
                        mm = pe.matmul(b_ps[0:HALF, h % 2, i * DL:(i + 1) * DL], qr[:, h, i * HALF:(i + 1) * HALF], kr[:, h, :], start=True, stop=True)
                    mm.then_inc(m_mm, 1)
                for hh in range(H // 2):
                    if hh >= 2:
                        pe.wait_ge(c_out, hh - 1)
                    for c in range(2):
                        mm = pe.matmul(b_ps[c * DL:(c + 1) * DL, 2 + hh % 2, 0:D], kckv[:, 2 * hh + c, :], wo[:, 2 * hh + c, :], start=True, stop=True)
                    mm.then_inc(c_mm, 1)

            @block.vector
            def _(v):
                for h in range(H):
                    v.wait_ge(a_mm, h + 1)
                    src = a_ps[:, h % 4, 0:KT * CQ].rearrange("p (k q) -> p k q", k=KT)
                    v.tensor_copy(m.a[0][:, :, h, :], src).then_inc(a_hi, 1)
                    v.wait_ge(a_hi, h + 1)
                    v.tensor_tensor(m.a[1][:, :, h, :], src, m.a[0][:, :, h, :].bitcast(F32), ALU.subtract).then_inc(a_out, 1)

            @block.scalar
            def _(a):
                for h in range(H):
                    a.wait_ge(m_mm, h + 1)
                    src = b_ps[0:HALF, h % 2, 0:2 * DL].rearrange("p (i d) -> p i d", i=2)
                    for i in range(2):
                        ins = a.activation(m.mqk[:, :, h, i * DL:(i + 1) * DL], src, ACT.Copy)
                    ins.then_inc(m_out, 1)
                for hh in range(H // 2):
                    a.wait_ge(c_mm, hh + 1)
                    a.activation(m.cvo[:, hh, :], b_ps[:, 2 + hh % 2, 0:D], ACT.Copy).then_inc(c_out, 1)


def phase_l1_attention(nc, outer, sem, io, m):
    NCH = B * CH
    NQT = len(QT)
    counters = []
    with ExitStack() as ctx:
        sb = lambda n, s, d=F32: ctx.enter_context(nc.sbuf_tensor(n, s, d))
        ps = lambda n, s, d=F32: ctx.enter_context(nc.psum_tensor(n, s, d))

        def count(name):
            counters.append(sem(name))
            return counters[-1]
        qcos, qsin = sb("c_qcos", [HALF, 2, S]), sb("c_qsin", [HALF, 2, S])
        kcos, ksin = sb("c_kcos", [KP, NT, DL]), sb("c_ksin", [KP, NT, DL])
        stats, mv, ve, rstd = sb("c_stats", [S, G, 6]), sb("c_mv", [S, G, 2]), sb("c_ve", [S, G]), sb("c_rstd", [S, G])
        xn = sb("c_xn", [S, G, D])
        xt = [sb(f"c_xt{i}", [128, KT, T], F32R) for i in range(2)]
        rot = sb("c_rot", [HALF, 2, 2, T])
        qg = sb("c_qg", [128, G, CH * CQS])
        q1 = sb("c_q1", [128, CH * CQS], F32R)
        q2 = sb("c_q2", [65, CH * CQS], F32R)
        kv = sb("c_kv", [KP, NT, DL])
        ks = sb("c_ks", [KP, NT, DL])
        kva = sb("c_kva", [KP, NT, DL + 1])
        k1 = sb("c_k1", [128, NT * KP], F32R)
        k2 = sb("c_k2", [65, NT * KP], F32R)
        mneg = sb("c_mneg", [128, NQT, 65], F32R)
        prob = sb("c_prob", [KP, 3, CQS])
        rc, rs = (prob[0:HALF, i, :].rearrange("p (i n) -> p i n", i=2) for i in range(2))
        rden = sb("c_rden", [128, NQT])
        cn = sb("c_cn", [128, NQT, CH, DL])
        ct = sb("c_ct", [128, CQS])
        s_ps = ps("c_s_ps", [128, 2, 2, 512])
        m_ps = ps("c_m_ps", [128, 3, 512])
        o_ps = ps("c_o_ps", [128, 512])
        t_loaded, consts = sem("c_t_loaded"), count("c_consts")
        ln, rstd_ready, xn_ready = count("c_ln"), count("c_rstd_ready"), count("c_xn_ready")
        xt_ps_ready, split_hi, xt_ready = count("c_xt_ps_ready"), count("c_split_hi"), count("c_xt_ready")
        wide_ready, roped, rot_ready = count("c_wide_ready"), count("c_roped"), count("c_rot_ready")
        qg_ps_ready, qg_ready = count("c_qg_ps_ready"), count("c_qg_ready")
        kv_loaded, kv_roped, kva_ready = sem("c_kv_loaded"), count("c_kv_roped"), count("c_kva_ready")
        kt_ready, k1_hi, k1_ready, k2_ready = count("c_kt_ready"), count("c_k1_hi"), count("c_k1_ready"), count("c_k2_ready")
        q1_ready, q2_ready = count("c_q1_ready"), count("c_q2_ready")
        maxs_ready, mneg_ready, row_ready, row_copied = count("c_maxs_ready"), count("c_mneg_ready"), count("c_row_ready"), count("c_row_copied")
        s_ready, prob_ready, pv_done = count("c_s_ready"), count("c_prob_ready"), count("c_pv_done")
        rden_ready, cn_ready, ct_ps_ready, ct_ready = count("c_rden_ready"), count("c_cn_ready"), count("c_ct_ps_ready"), count("c_ct_ready")
        f_ready, x_added = count("c_f_ready"), count("c_x_added")
        parts = ((0, 0), (0, 1), (1, 0))

        with nc.Block() as block:
            @block.sync
            def _(sp):
                for c in counters:
                    sp.sem_inc(c, PRIMED)
                sp.dma_start(qcos[:], io["qcos"]).then_inc(t_loaded, 16)
                sp.dma_start(qsin[:], io["qsin"]).then_inc(t_loaded, 16)
                sp.dma_start(kcos[:], io["kcos"]).then_inc(t_loaded, 16)
                sp.dma_start(ksin[:], io["ksin"]).then_inc(t_loaded, 16)
                with sp.Fori(0, B) as b:
                    sp.wait_ge(kva_ready, PRIMED + b * 2)
                    src = io["ctx_512"][bass.ds(b, 1)].rearrange("b l d -> (b l) d")
                    main = src[0:NT * 120].rearrange("(p r) d -> p r d", r=NT)
                    sp.dma_start(kv[0:120], main).then_inc(kv_loaded, 16)
                    sp.dma_start(kv[120:121, 0:4, :], src[1440:1444].unsqueeze(0)).then_inc(kv_loaded, 16)
                    sp.dma_start(kv[120:121, 4:NT, :], src[1432:1440].unsqueeze(0)).then_inc(kv_loaded, 16)
                sp.wait_ge(kv_loaded, B * 48)
                sp.wait_ge(t_loaded, 16 * 4)

            @block.gpsimd
            def _(g):
                g.wait_ge(t_loaded, 16 * 4)
                with g.Fori(0, NG) as it:
                    g.wait_ge(ln, PRIMED + (it + 1) * (2 * G + 1))
                    g.tensor_tensor(rstd[:], ve[:], m.mhalf[0:S, 0:G], ALU.pow).then_inc(rstd_ready, 1)
                    for h in range(H):
                        n = it * H + h
                        g.wait_ge(roped, PRIMED + 2 * (n + 1))
                        if h >= 2:
                            g.wait_ge(qg_ps_ready, PRIMED + n - 1)
                        for i in range(2):
                            ins = g.tensor_tensor(rot[:, h % 2, i, :], rc[:, i, :], rs[:, 1 - i, :], ALU.add)
                        ins.then_inc(rot_ready, 1)
                    with g.Fori(0, G) as j:
                        b = it * G + j
                        g.wait_ge(kv_loaded, (b + 1) * 48)
                        g.tensor_tensor(ks[:], kv[:], ksin[:], ALU.mult).then_inc(kv_roped, 1)
                        g.tensor_tensor(kv[:], kv[:], kcos[:], ALU.mult).then_inc(kv_roped, 1)
                        g.wait_ge(kv_roped, PRIMED + (b + 1) * 2)
                        g.wait_ge(pv_done, PRIMED + b * CH * NT)
                        for i in range(2):
                            c0 = slice(i * DL // 2, (i + 1) * DL // 2)
                            c1 = slice((1 - i) * DL // 2, (2 - i) * DL // 2)
                            g.tensor_tensor(kva[:, :, c0], kv[:, :, c0], ks[:, :, c1], ALU.add).then_inc(kva_ready, 1)
                        g.wait_ge(k1_hi, PRIMED + (b + 1) * 3)
                        g.sem_inc(m.carrier, 1)
                        g.tensor_copy(k2[0:DL, :], k1[0:DL, :]).then_inc(k2_ready, 1)

            def normalise(v, b, c):
                ch = b * CH + c
                v.wait_ge(pv_done, PRIMED + (ch + 1) * NT)
                o = o_ps[:, 0:NQT * (DL + 1)].rearrange("p (t d) -> p t d", t=NQT)
                last = QT[-1]
                v.reciprocal(rden[:, 0:NQT - 1], o[:, 0:NQT - 1, DL]).then_inc(rden_ready, 1)
                v.reciprocal(rden[0:last, NQT - 1:NQT], o[0:last, NQT - 1, DL:DL + 1]).then_inc(rden_ready, 1)
                v.wait_ge(rden_ready, PRIMED + (ch + 1) * 2)
                v.tensor_tensor(cn[:, 0:NQT - 1, c, :], o[:, 0:NQT - 1, 0:DL],
                                rden[:, 0:NQT - 1].unsqueeze(2).broadcast_to((128, NQT - 1, DL)), ALU.mult).then_inc(cn_ready, 1)
                v.tensor_scalar(cn[0:last, NQT - 1, c, :], o[0:last, NQT - 1, 0:DL], rden[0:last, NQT - 1:NQT], None,
                                ALU.mult).then_inc(cn_ready, 1)

            @block.vector
            def _(v):
                v.wait_ge(t_loaded, 16 * 4)
                v.memset(kva[:, :, DL], 1.0).then_inc(consts, 1)
                v.memset(k2[DL:DL + 1, :].bitcast(F32), 1.0).then_inc(consts, 1)
                v.memset(mneg[:].bitcast(F32), 0.0).then_inc(consts, 1)
                v.wait_ge(consts, PRIMED + 3)
                with v.Fori(0, NG) as it:
                    xg = lambda j: m.x[:, bass.ds((it * G + j) * D, D)]
                    layernorm_stats(v, xg, stats, mv, ve, G, ln, it * (2 * G + 1), m.carrier)
                    v.wait_ge(rstd_ready, PRIMED + it + 1)
                    for j in range(G):
                        v.tensor_scalar(xn[:, j, :], xg(j), mv[:, j, 0:1], rstd[:, j:j + 1],
                                        ALU.subtract, ALU.mult).then_inc(xn_ready, 1)
                    for k in range(KT):
                        v.wait_ge(xt_ps_ready, PRIMED + it * KT + k + 1)
                        v.tensor_copy(xt[0][:, k, :], m_ps[:, k, 0:T]).then_inc(split_hi, 1)
                        v.wait_ge(split_hi, PRIMED + it * KT + k + 1)
                        v.tensor_tensor(xt[1][:, k, :], m_ps[:, k, 0:T], xt[0][:, k, :].bitcast(F32), ALU.subtract).then_inc(xt_ready, 1)
                    table = lambda a: a[:].unsqueeze(2).broadcast_to((HALF, 2, G, S))
                    for h in range(H):
                        n = it * H + h
                        v.wait_ge(wide_ready, PRIMED + n + 1)
                        if h >= 1:
                            v.wait_ge(rot_ready, PRIMED + n)
                        src = s_ps[0:HALF, h % 2, :, 0:T].rearrange("p i (b s) -> p i b s", b=G)
                        v.tensor_tensor(rc.rearrange("p i (b s) -> p i b s", b=G), src, table(qcos), ALU.mult).then_inc(roped, 1)
                        v.tensor_tensor(rs.rearrange("p i (b s) -> p i b s", b=G), src, table(qsin), ALU.mult).then_inc(roped, 1)
                    v.wait_ge(qg_ready, PRIMED + (it + 1) * H)
                    v.sem_inc(m.carrier, 1)
                    with v.Fori(0, G) as j:
                        b = it * G + j
                        qj = qg[:, bass.ds(j, 1), :].rearrange("p a n -> p (a n)")
                        v.tensor_copy(q1[:], qj).then_inc(q1_ready, 1)
                        v.wait_ge(q1_ready, PRIMED + b + 1)
                        v.tensor_tensor(q2[0:DL, :], qg[0:DL, bass.ds(j, 1), :].rearrange("p a n -> p (a n)"),
                                        q1[0:DL, :].bitcast(F32), ALU.subtract).then_inc(q2_ready, 1)
                        for k in range(3):
                            cols = slice(k * 4 * KP, (k + 1) * 4 * KP)
                            v.wait_ge(kt_ready, PRIMED + b * 3 + k + 1)
                            v.tensor_copy(k1[0:DL, cols], m_ps[0:DL, k, 0:4 * KP]).then_inc(k1_hi, 1)
                            v.wait_ge(k1_hi, PRIMED + b * 3 + k + 1)
                            v.tensor_tensor(k1[DL:128, cols], m_ps[0:DL, k, 0:4 * KP], k1[0:DL, cols].bitcast(F32),
                                            ALU.subtract).then_inc(k1_ready, 1)
                        for c in range(CH):
                            ch = b * CH + c
                            for t, n in enumerate(QT):
                                v.wait_ge(maxs_ready, PRIMED + ch * NQT + t + 1)
                                v.tensor_reduce(mneg[0:n, t, DL:DL + 1], m_ps[0:n, :, 0:4 * KP], AX.XY, ALU.max,
                                                negate=True).then_inc(mneg_ready, 1)
                            v.wait_ge(row_ready, PRIMED + ch + 1)
                            v.tensor_copy(q2[DL:DL + 1, c * CQS:(c + 1) * CQS],
                                          m_ps[DL:DL + 1, :, :].rearrange("p a n -> p (a n)")[:, 0:CQS]).then_inc(row_copied, 1)
                            if c == 1:
                                normalise(v, b, 0)
                        normalise(v, b, 1)
                        v.wait_ge(f_ready, PRIMED + b + 1)
                        xs = m.x[:, bass.ds(b * D, D)]
                        v.scalar_tensor_tensor(xs, o_ps[0:S, 0:D], m.tg[0:S, 1:2], xs, ALU.mult, ALU.add).then_inc(x_added, 1)
                    v.wait_ge(x_added, PRIMED + (it + 1) * G)

            def qps(h):
                return m_ps[:, 2, 0:T] if h % 2 == 0 else o_ps[:, 0:T]

            @block.scalar
            def _(a):
                with a.Fori(0, NG) as it:
                    for h in range(H):
                        a.wait_ge(qg_ps_ready, PRIMED + it * H + h + 1)
                        c, hh = h % 2, h // 2
                        dst = qg[:, :, c * CQS + hh * S:c * CQS + (hh + 1) * S]
                        a.activation(dst, qps(h).rearrange("p (b s) -> p b s", b=G), ACT.Copy).then_inc(qg_ready, 1)
                    with a.Fori(0, G) as j:
                        b = it * G + j
                        for c in range(CH):
                            for r in range(NT):
                                n = (b * CH + c) * NT + r
                                a.wait_ge(s_ready, PRIMED + n + 1)
                                if c * NT + r >= 3:
                                    a.wait_ge(pv_done, PRIMED + n - 2)
                                k = keys_of(r)
                                a.activation(prob[0:k, r % 3, :].rearrange("p (i n) -> p i n", i=2),
                                             s_ps[0:k, r % 2, :, 0:CQS // 2], ACT.Exp).then_inc(prob_ready, 1)
                        a.wait_ge(ct_ps_ready, PRIMED + b + 1)
                        a.activation(ct[:], m_ps[:, :, :].rearrange("p a n -> p (a n)")[:, 0:CQS], ACT.Copy).then_inc(ct_ready, 1)

            @block.tensor
            def _(pe):
                pe.wait_ge(consts, PRIMED + 3)
                with pe.Fori(0, NG) as it:
                    pe.wait_ge(xn_ready, PRIMED + (it + 1) * G)
                    for k in range(KT):
                        for j in range(G):
                            mm = pe.transpose(m_ps[:, k, j * S:(j + 1) * S], xn[:, j, k * 128:(k + 1) * 128], m.ident[0:S, 0:S])
                        mm.then_inc(xt_ps_ready, 1)
                    pe.wait_ge(xt_ready, PRIMED + (it + 1) * KT)

                    def wide(h):
                        if h >= 2:
                            pe.wait_ge(roped, PRIMED + 2 * (it * H + h - 1))
                        for i in range(2):
                            for p, (w, x) in enumerate(parts):
                                for k in range(KT):
                                    mm = pe.matmul(s_ps[0:HALF, h % 2, i, 0:T], m.a[w][:, k, h, i * HALF:(i + 1) * HALF], xt[x][:, k, :],
                                                   start=(p == 0 and k == 0), stop=(p == 2 and k == KT - 1))
                        mm.then_inc(wide_ready, 1)

                    def absorbed(h):
                        n = it * H + h
                        pe.wait_ge(rot_ready, PRIMED + n + 1)
                        if h >= 2:
                            pe.wait_ge(qg_ready, PRIMED + n - 1)
                        for i in range(2):
                            mm = pe.matmul(qps(h), m.mqk[:, i, h, :], rot[:, h % 2, i, :], start=(i == 0), stop=(i == 1))
                        mm.then_inc(qg_ps_ready, 1)
                    wide(0)
                    wide(1)
                    for h in range(2, H):
                        wide(h)
                        absorbed(h - 2)
                    absorbed(H - 2)
                    absorbed(H - 1)

                    with pe.Fori(0, G) as j:
                        b = it * G + j
                        pe.wait_ge(kva_ready, PRIMED + (b + 1) * 2)
                        pe.wait_ge(qg_ready, PRIMED + (it + 1) * H)
                        pe.sem_inc(m.carrier, 1)
                        for k in range(3):
                            for r in range(4 * k, 4 * k + 4):
                                mm = pe.transpose(m_ps[0:DL, k, (r - 4 * k) * KP:(r - 4 * k + 1) * KP],
                                                  kva[:, r, 0:DL], m.ident[0:KP, 0:KP])
                            mm.then_inc(kt_ready, 1)
                        pe.wait_ge(k1_ready, PRIMED + (b + 1) * 3)
                        pe.wait_ge(q1_ready, PRIMED + b + 1)

                        def maxima(c, t):
                            ch = b * CH + c
                            if t > 0:
                                pe.wait_ge(mneg_ready, PRIMED + ch * NQT + t)
                            n = QT[t]
                            for k in range(3):
                                mm = pe.matmul(m_ps[0:n, k, 0:4 * KP], q1[:, c * CQS + t * 128:c * CQS + t * 128 + n],
                                               k1[:, k * 4 * KP:(k + 1) * 4 * KP], start=True, stop=True)
                            mm.then_inc(maxs_ready, 1)

                        def maxima_row(c):
                            ch = b * CH + c
                            pe.wait_ge(mneg_ready, PRIMED + (ch + 1) * NQT)
                            for t, n in enumerate(QT):
                                mm = pe.matmul(m_ps[0:DL + 1, t // 4, (t % 4) * 128:(t % 4) * 128 + n], mneg[0:n, t, :],
                                               m.identr[0:n, 0:n], start=True, stop=True)
                            mm.then_inc(row_ready, 1)

                        def scores(c, r):
                            n = (b * CH + c) * NT + r
                            k = keys_of(r)
                            if c * NT + r >= 2:
                                pe.wait_ge(prob_ready, PRIMED + n - 1)
                            for i in range(2):
                                cols = slice(c * CQS + i * CQS // 2, c * CQS + (i + 1) * CQS // 2)
                                o = s_ps[0:k, r % 2, i, 0:CQS // 2]
                                pe.matmul(o, k1[:, r * KP:r * KP + k], q1[:, cols], start=True, stop=False)
                                mm = pe.matmul(o, k2[:, r * KP:r * KP + k], q2[:, cols], start=False, stop=True)
                            mm.then_inc(s_ready, 1)

                        def values(c, r):
                            n = (b * CH + c) * NT + r
                            pe.wait_ge(prob_ready, PRIMED + n + 1)
                            if r == 0:
                                pe.wait_ge(cn_ready, PRIMED + (b * CH + c) * 2)
                                if c == 0:
                                    pe.wait_ge(x_added, PRIMED + b)
                            k = keys_of(r)
                            for t, w in enumerate(QT):
                                mm = pe.matmul(o_ps[0:w, t * (DL + 1):(t + 1) * (DL + 1)], prob[0:k, r % 3, t * 128:t * 128 + w],
                                               kva[0:k, r, :], start=(r == 0 and t == 0), stop=(r == NT - 1), skip_group_check=True)
                            mm.then_inc(pv_done, 1)

                        for t in range(NQT):
                            maxima(0, t)
                        maxima_row(0)
                        pe.wait_ge(k2_ready, PRIMED + b + 1)
                        pe.wait_ge(q2_ready, PRIMED + b + 1)
                        pe.wait_ge(row_copied, PRIMED + b * CH + 1)
                        for r in range(NT):
                            scores(0, r)
                            if 1 <= r < 1 + NQT:
                                maxima(1, r - 1)
                            if r == 9:
                                maxima_row(1)
                            if r > 0:
                                values(0, r - 1)
                        pe.wait_ge(row_copied, PRIMED + b * CH + 2)
                        scores(1, 0)
                        values(0, NT - 1)
                        for r in range(1, NT):
                            scores(1, r)
                            values(1, r - 1)
                        values(1, NT - 1)
                        pe.wait_ge(cn_ready, PRIMED + (b + 1) * CH * 2)
                        for t, w in enumerate(QT):
                            mm = pe.transpose(m_ps[:, t // 4, (t % 4) * 128:(t % 4) * 128 + w], cn[0:w, t, :, :], m.ident[0:w, 0:w])
                        mm.then_inc(ct_ps_ready, 1)
                        pe.wait_ge(ct_ready, PRIMED + b + 1)
                        for hh in range(H // 2):
                            mm = pe.matmul(o_ps[0:S, 0:D], ct[:, hh * S:(hh + 1) * S], m.cvo[:, hh, :], start=(hh == 0), stop=(hh == H // 2 - 1))
                        mm.then_inc(f_ready, 1)


def phase_l1_ffn(nc, outer, sem, io, m):
    FT = F // 128
    counters = []
    with ExitStack() as ctx:
        sb = lambda n, s, d=F32: ctx.enter_context(nc.sbuf_tensor(n, s, d))
        ps = lambda n, s, d=F32: ctx.enter_context(nc.psum_tensor(n, s, d))

        def count(name):
            counters.append(sem(name))
            return counters[-1]
        w1r, w2r = sb("d_w1r", [128, KT, F]), sb("d_w2r", [128, FT, D])
        w1, w2 = sb("d_w1", [128, KT, F], BF16), sb("d_w2", [128, FT, D], BF16)
        b1, gamma, beta, b2 = sb("d_b1", [S, F]), sb("d_gamma", [S, F]), sb("d_beta", [S, F]), sb("d_b2", [S, D])
        ones = sb("d_ones", [128, 128])
        wabs, wmean, wscale = sb("d_wabs", [128, 2]), sb("d_wmean", [128, 2]), sb("d_wscale", [128, 2])
        stats, mv, ve, rstd = sb("d_stats", [S, G, 6]), sb("d_mv", [S, G, 2]), sb("d_ve", [S, G]), sb("d_rstd", [S, G])
        xn = sb("d_xn", [S, G, D])
        xmax, xinv, xscale, xdeq = (sb(f"d_x{n}", [S, G]) for n in ("max", "inv", "scale", "deq"))
        xq = sb("d_xq", [S, G, D], BF16)
        xqt = sb("d_xqt", [128, KT, T], BF16)
        h1 = sb("d_h1", [S, G, F])
        hg = sb("d_hg", [S, G, F])
        hstats, hmv, hve, hrstd = sb("d_hstats", [S, G, 2, 6]), sb("d_hmv", [S, G, 2]), sb("d_hve", [S, G]), sb("d_hrstd", [S, G])
        hmax, hinv, hscale, hdeq = (sb(f"d_h{n}", [S, G]) for n in ("max", "inv", "scale", "deq"))
        hq = sb("d_hq", [S, G, F], BF16)
        hqt = sb("d_hqt", [128, 2, FT, S], BF16)
        res = sb("d_res", [S, G, D])
        h_ps = ps("d_h_ps", [128, 2, 1024])
        t_ps = ps("d_t_ps", [128, 2, 1024], BF16)
        y_ps = ps("d_y_ps", [128, 2, 512])
        loaded, w_ready, w_sum = sem("d_loaded"), count("d_w_ready"), count("d_w_sum")
        vec, rstd_ready, hrstd_ready = count("d_vec"), count("d_rstd_ready"), count("d_hrstd_ready")
        xq_ready, xt_ps_ready, xt_ready = count("d_xq_ready"), count("d_xt_ps_ready"), count("d_xt_ready")
        h_ready, h1_ready, hg_ready = count("d_h_ready"), count("d_h1_ready"), count("d_hg_ready")
        hn_ready, hb_ready = count("d_hn_ready"), count("d_hb_ready")
        hq_ready, ht_ps_ready, ht_ready = count("d_hq_ready"), count("d_ht_ps_ready"), count("d_ht_ready")
        y_ready, x_added, stored, res_ready = count("d_y_ready"), count("d_x_added"), sem("d_stored"), count("d_res_ready")
        NPRE = 16
        NV = 17 + 11 * G

        with nc.Block() as block:
            @block.sync
            def _(sp):
                for c in counters:
                    sp.sem_inc(c, PRIMED)
                sp.dma_start(w1r[:], io["L1_w1T"].rearrange("(k p) n -> p k n", p=128)).then_inc(loaded, 16)
                sp.dma_start(w2r[:], io["L1_w2T"].rearrange("(k p) n -> p k n", p=128)).then_inc(loaded, 16)
                for t, n in ((b1, "L1_ffn_b1"), (gamma, "L1_ffn_gamma"), (beta, "L1_ffn_beta"), (b2, "L1_ffn_b2")):
                    sp.dma_start(t[:], io[n].partition_broadcast(S)).then_inc(loaded, 16)
                with sp.Fori(0, NG) as it:
                    sp.wait_ge(x_added, PRIMED + (it + 1) * G)
                    sp.dma_start(io["out"][bass.ds(it * G, G)].rearrange("b s d -> s b d"),
                                 m.x[:, bass.ds(it * G * D, G * D)].rearrange("s (b d) -> s b d", b=G)).then_inc(stored, 16)
                sp.wait_ge(loaded, 16 * 6)
                sp.wait_ge(stored, 16 * NG)

            @block.gpsimd
            def _(g):
                g.wait_ge(w_ready, PRIMED + NPRE)
                with g.Fori(0, NG) as it:
                    g.wait_ge(vec, PRIMED + it * NV + 2 * G + 1)
                    g.tensor_tensor(rstd[:], ve[:], m.mhalf[0:S, 0:G], ALU.pow).then_inc(rstd_ready, 1)
                    for j in range(G):
                        n = it * G + j
                        g.wait_ge(vec, PRIMED + it * NV + 2 * G + 1 + G + 8 + 4 * (j + 1))
                        g.tensor_tensor(hrstd[:, j:j + 1], hve[:, j:j + 1], m.mhalf[0:S, 0:1], ALU.pow).then_inc(hrstd_ready, 1)
                        g.wait_ge(hn_ready, PRIMED + n + 1)
                        g.tensor_tensor(h1[:, j, :], h1[:, j, :], gamma[:], ALU.mult).then_inc(hb_ready, 1)
                        g.wait_ge(hb_ready, PRIMED + 2 * n + 1)
                        g.tensor_tensor(h1[:, j, :], h1[:, j, :], beta[:], ALU.add).then_inc(hb_ready, 1)

            @block.vector
            def _(v):
                v.wait_ge(loaded, 16 * 6)
                n = [0]

                def pre(ins):
                    ins.then_inc(w_ready, 1)
                    n[0] += 1
                    v.wait_ge(w_ready, PRIMED + n[0])
                pre(v.memset(ones[:], 1.0))
                pre(v.tensor_reduce(wabs[:, 0:1], w1r[:], AX.XY, ALU.add, apply_absolute_value=True))
                pre(v.tensor_reduce(wabs[:, 1:2], w2r[:], AX.XY, ALU.add, apply_absolute_value=True))
                v.wait_ge(w_sum, PRIMED + 1)
                pre(v.tensor_scalar(wmean[:], h_ps[:, 0, 0:2], 1.0 / (F * D), EPS, ALU.mult, ALU.max))
                pre(v.reciprocal(wscale[:], wmean[:]))
                pre(v.tensor_scalar(wmean[:], wmean[:], 1.0 / 127.0, None, ALU.mult))
                for i, (r_, w) in enumerate(((w1r, w1), (w2r, w2))):
                    pre(v.tensor_scalar(r_[:], r_[:], wscale[:, i:i + 1], ROUND, ALU.mult, ALU.add))
                    pre(v.tensor_scalar(r_[:], r_[:], -ROUND, 1.0, ALU.add, ALU.min))
                    pre(v.tensor_scalar(w[:], r_[:], -1.0, None, ALU.max))
                pre(v.tensor_scalar(b2[:], b2[:], m.tg[0:S, 3:4], None, ALU.mult))
                pre(v.memset(xmax[:], 0.0))
                pre(v.memset(hmax[:], 0.0))
                pre(v.memset(xinv[:], 0.0))
                assert n[0] == NPRE
                with v.Fori(0, NG) as it:
                    xg = lambda j: m.x[:, bass.ds((it * G + j) * D, D)]
                    layernorm_stats(v, xg, stats, mv, ve, G, vec, it * NV, m.carrier)
                    n = [2 * G + 1]

                    def step(ins):
                        ins.then_inc(vec, 1)
                        n[0] += 1

                    def settle():
                        v.wait_ge(vec, PRIMED + it * NV + n[0])
                    v.wait_ge(rstd_ready, PRIMED + it + 1)
                    for j in range(G):
                        step(v.tensor_scalar(xn[:, j, :], xg(j), mv[:, j, 0:1], rstd[:, j:j + 1], ALU.subtract, ALU.mult))
                    settle()

                    def scales(x, big, inv, scale, deq, wcol):
                        step(v.tensor_reduce(big, x, AX.X, ALU.max, apply_absolute_value=True))
                        settle()
                        step(v.tensor_scalar(big, big, EPS, None, ALU.max))
                        settle()
                        step(v.reciprocal(inv, big))
                        step(v.tensor_scalar(deq, big, wmean[0:S, wcol:wcol + 1], None, ALU.mult))
                        settle()
                        step(v.tensor_scalar(scale, inv, 127.0, None, ALU.mult))
                        settle()
                    scales(xn[:], xmax[:], xinv[:], xscale[:], xdeq[:], 0)
                    for j in range(G):
                        ins = v.tensor_scalar(xn[:, j, :], xn[:, j, :], xscale[:, j:j + 1], -128.0, ALU.mult, ALU.max)
                    step(ins)
                    settle()
                    step(v.tensor_scalar(xn[:], xn[:], 127.0, ROUND, ALU.min, ALU.add))
                    settle()
                    step(v.tensor_scalar(xq[:], xn[:], -ROUND, None, ALU.add))
                    v.wait_ge(xt_ps_ready, PRIMED + it + 1)
                    v.tensor_copy(xqt[:].rearrange("p k n -> p (k n)"), t_ps[:, 0, 0:KT * T]).then_inc(xt_ready, 1)
                    for j in range(G):
                        nb = it * G + j
                        v.wait_ge(h_ready, PRIMED + nb + 1)
                        v.scalar_tensor_tensor(h1[:, j, :], h_ps[0:S, j % 2, :], xdeq[:, j:j + 1], b1[:], ALU.mult, ALU.add).then_inc(h1_ready, 1)
                    for j in range(G):
                        nb = it * G + j
                        v.wait_ge(hg_ready, PRIMED + nb + 1)
                        for i in range(2):
                            step(v.bn_stats(hstats[:, j, i, :], hg[:, j, i * 512:(i + 1) * 512]))
                        settle()
                        v.sem_inc(m.carrier, 1)
                        step(v.bn_aggr(hmv[:, j, :], hstats[:, j, :, :].rearrange("p a b -> p (a b)")))
                        settle()
                        step(v.tensor_scalar(hve[:, j:j + 1], hmv[:, j, 1:2], EPS, None, ALU.add))
                    for j in range(G):
                        nb = it * G + j
                        v.wait_ge(hrstd_ready, PRIMED + nb + 1)
                        v.tensor_scalar(h1[:, j, :], hg[:, j, :], hmv[:, j, 0:1], hrstd[:, j:j + 1], ALU.subtract, ALU.mult).then_inc(hn_ready, 1)
                    for j in range(G):
                        nb = it * G + j
                        v.wait_ge(hb_ready, PRIMED + 2 * (nb + 1))
                        scales(h1[:, j, :], hmax[:, j:j + 1], hinv[:, j:j + 1], hscale[:, j:j + 1], hdeq[:, j:j + 1], 1)
                        step(v.tensor_scalar(h1[:, j, :], h1[:, j, :], hscale[:, j:j + 1], -128.0, ALU.mult, ALU.max))
                        settle()
                        v.tensor_scalar(h1[:, j, :], h1[:, j, :], 127.0, ROUND, ALU.min, ALU.add).then_inc(res_ready, 1)
                        v.wait_ge(res_ready, PRIMED + 3 * nb + 1)
                        v.tensor_scalar(hq[:, j, :], h1[:, j, :], -ROUND, None, ALU.add).then_inc(hq_ready, 1)
                        v.tensor_scalar(hdeq[:, j:j + 1], hdeq[:, j:j + 1], m.tg[0:S, 3:4], None, ALU.mult).then_inc(res_ready, 1)
                        v.tensor_tensor(res[:, j, :], xg(j), b2[:], ALU.add).then_inc(res_ready, 1)
                        v.wait_ge(ht_ps_ready, PRIMED + nb + 1)
                        if j >= 2:
                            v.wait_ge(y_ready, PRIMED + nb - 1)
                        v.tensor_copy(hqt[:, j % 2].rearrange("p a b -> p (a b)"), t_ps[:, 1, 0:FT * S]).then_inc(ht_ready, 1)
                    for j in range(G):
                        nb = it * G + j
                        v.wait_ge(y_ready, PRIMED + it * G + 2 * (j // 2) + 2)
                        v.wait_ge(res_ready, PRIMED + 3 * (nb + 1))
                        v.scalar_tensor_tensor(xg(j), y_ps[0:S, j // 2, (j % 2) * D:(j % 2 + 1) * D], hdeq[:, j:j + 1], res[:, j, :],
                                               ALU.mult, ALU.add).then_inc(x_added, 1)
                    assert n[0] == NV, n

            @block.scalar
            def _(a):
                with a.Fori(0, NG) as it:
                    for j in range(G):
                        a.wait_ge(h1_ready, PRIMED + it * G + j + 1)
                        a.activation(hg[:, j, :], h1[:, j, :], ACT.Gelu).then_inc(hg_ready, 1)

            @block.tensor
            def _(pe):
                pe.wait_ge(w_ready, PRIMED + 3)
                pe.matmul(h_ps[:, 0, 0:2], ones[:], wabs[:], start=True, stop=True).then_inc(w_sum, 1)
                pe.wait_ge(w_ready, PRIMED + NPRE)
                with pe.Fori(0, NG) as it:
                    pe.wait_ge(vec, PRIMED + it * NV + 2 * G + 1 + G + 5 + 3)
                    for k in range(KT):
                        for j in range(G):
                            mm = pe.transpose(t_ps[:, 0, (k * G + j) * S:(k * G + j + 1) * S], xq[:, j, k * 128:(k + 1) * 128], m.identb[0:S, 0:S])
                    mm.then_inc(xt_ps_ready, 1)
                    pe.wait_ge(xt_ready, PRIMED + it + 1)
                    for j in range(G):
                        if j >= 2:
                            pe.wait_ge(h1_ready, PRIMED + it * G + j - 1)
                        for i in range(2):
                            for k in range(KT):
                                mm = pe.matmul(h_ps[0:S, j % 2, i * 512:(i + 1) * 512], xqt[:, k, j * S:(j + 1) * S], w1[:, k, i * 512:(i + 1) * 512],
                                               start=(k == 0), stop=(k == KT - 1))
                        mm.then_inc(h_ready, 1)
                    for j in range(G):
                        nb = it * G + j
                        pe.wait_ge(hq_ready, PRIMED + nb + 1)
                        if j == 0:
                            pe.wait_ge(x_added, PRIMED + it * G)
                        for f in range(FT):
                            mm = pe.transpose(t_ps[:, 1, f * S:(f + 1) * S], hq[:, j, f * 128:(f + 1) * 128], m.identb[0:S, 0:S])
                        mm.then_inc(ht_ps_ready, 1)
                        pe.wait_ge(ht_ready, PRIMED + nb + 1)
                        for f in range(FT):
                            mm = pe.matmul(y_ps[0:S, j // 2, (j % 2) * D:(j % 2 + 1) * D], hqt[:, j % 2, f, :], w2[:, f, :],
                                           start=(f == 0), stop=(f == FT - 1))
                        mm.then_inc(y_ready, 1)


class Shared:
    pass


STOP = 5


def build(nc, io):
    with ExitStack() as outer:
        sb = lambda n, s, d=F32: outer.enter_context(nc.sbuf_tensor(n, s, d))
        sem = lambda n: outer.enter_context(nc.semaphore(n))
        m = Shared()
        m.x = sb("x_rows", [S, B * D])
        m.ident, m.identr, m.identb = sb("ident", [128, 128]), sb("identr", [128, 128], F32R), sb("identb", [128, 128], BF16)
        m.gates, m.tg = sb("gates", [128, 4]), sb("tanh_gates", [128, 4])
        m.mhalf = sb("minus_half", [128, G])
        m.carrier = sem("wait_carrier")
        phase_load(nc, outer, sem, io, m)
        if STOP >= 1:
            phase_l0_attention(nc, outer, sem, io, m)
        if STOP >= 2:
            phase_moe(nc, outer, sem, io, m)
        if STOP >= 3:
            with ExitStack() as l1:
                sl = lambda n, s, d=F32: l1.enter_context(nc.sbuf_tensor(n, s, d))
                m.a = [sl(f"l1_a{i}", [128, KT, H, CQ], F32R) for i in range(2)]
                m.mqk = sl("l1_mqk", [HALF, 2, H, 2 * DL])
                m.cvo = sl("l1_cvo", [128, H // 2, D])
                phase_l1_weights(nc, outer, sem, io, m)
                phase_l1_attention(nc, outer, sem, io, m)
        if STOP >= 4:
            phase_l1_ffn(nc, outer, sem, io, m)
        else:
            done = sem("debug_done")
            with nc.Block() as block:
                @block.sync
                def _(sp):
                    sp.dma_start(io["out"].rearrange("b s d -> s b d"), m.x[:].rearrange("s (b d) -> s b d", b=B)).then_inc(done, 16)
                    sp.wait_ge(done, 16)


def rope_tables(length, dim):
    import numpy as np
    f32 = np.float32
    inv = f32(1.0) / np.power(f32(10000.0), np.arange(0, dim, 2, dtype=f32) / f32(dim)).astype(f32)
    f = np.arange(length, dtype=f32)[:, None] * inv[None, :].astype(f32)
    return np.repeat(np.sin(f), 2, axis=-1).astype(f32), np.repeat(np.cos(f), 2, axis=-1).astype(f32)


def constants():
    import numpy as np
    c = {}
    c["ident"] = np.eye(128, dtype=np.float32)
    q, k = np.arange(S)[:, None], np.arange(S)[None, :]
    c["causal"] = np.where(k <= q, 0.0, -1e30).astype(np.float32)
    c["headsel"] = (np.arange(128)[:, None] // HD == np.arange(8)[None, :]).astype(np.float32)
    row_expert = np.arange(E * I) // I
    rows = np.zeros((40, E * I), np.float32)
    for e in range(E):
        rows[e] = rows[32 + e] = row_expert == e
    c["expert_rows"] = rows
    c["iota8"] = np.arange(E, dtype=np.float32)
    sin, cos = rope_tables(S, CQ)
    c["qcos"] = np.ascontiguousarray(np.stack([cos[:, :HALF].T, cos[:, HALF:].T], 1))
    c["qsin"] = np.ascontiguousarray(np.stack([sin[:, HALF:].T, -sin[:, :HALF].T], 1))
    sin, cos = rope_tables(LK, DL)
    p, r = np.arange(KP)[:, None], np.arange(NT)[None, :]
    key = NT * p + r
    key = np.where(key < LK, key, key - NT)
    hd = DL // 2
    c["kcos"] = np.ascontiguousarray(cos[key])
    c["ksin"] = np.ascontiguousarray(np.concatenate([sin[key][..., hd:], -sin[key][..., :hd]], -1))
    return c


def kernel(**inputs):
    import numpy as np
    import concourse.bacc as _bacc
    from concourse.bass_utils import run_bass_kernel_spmd as _run

    a = inputs
    t = lambda w: np.ascontiguousarray(np.transpose(w))
    lay = {n: np.ascontiguousarray(a[n]) for n in (
        "x", "ctx_512", "g_xattn", "g_ffn", "L1_xattn_Wq", "L1_xattn_w_kc_q", "L1_xattn_w_kc_kv",
        "L1_ffn_b1", "L1_ffn_gamma", "L1_ffn_beta", "L1_ffn_b2")}
    lay["L0_WqT"] = t(a["L0_xattn_Wq"])
    lay["L0_WkvT"] = t(a["L0_xattn_Wkv_expand"])
    lay["L0_WoutT"] = t(a["L0_xattn_Wout"])
    lay["L0_routerT"] = t(a["L0_ffn_router_w"])
    lay["L0_gateT"] = t(np.reshape(a["L0_ffn_w_gate"], (E * I, D)))
    lay["L0_upT"] = t(np.reshape(a["L0_ffn_w_up"], (E * I, D)))
    lay["L0_downT"] = np.ascontiguousarray(np.reshape(np.transpose(a["L0_ffn_w_down"], (0, 2, 1)), (E * I, D)))
    lay["L1_qrT"] = np.ascontiguousarray(np.transpose(a["L1_xattn_W_qr"], (2, 0, 1)))
    lay["L1_krT"] = np.ascontiguousarray(np.transpose(a["L1_xattn_W_kr"], (2, 0, 1)))
    lay["L1_WoT"] = t(a["L1_xattn_Wo"])
    lay["L1_w1T"] = t(a["L1_ffn_w1"])
    lay["L1_w2T"] = t(a["L1_ffn_w2"])
    lay.update(constants())

    nc = _bacc.Bacc("TRN2", target_bir_lowering=False, num_devices=1)
    arrays, io = {}, {}
    for n, v in lay.items():
        arrays[f"in_{n}"] = v
        io[n] = nc.dram_tensor(f"in_{n}", v.shape, F32, kind="ExternalInput").ap()
    io["out"] = nc.dram_tensor("out_rows", (B, S, D), F32, kind="ExternalOutput").ap()
    build(nc, io)
    r = _run(nc, [arrays], core_ids=[0])
    return r.results[0]["out_rows"]
```

```python
from contextlib import ExitStack

import concourse.bass as bass
from concourse import mybir

F32 = mybir.dt.float32
F32R = mybir.dt.float32r
BF16 = mybir.dt.bfloat16
U32 = mybir.dt.uint32
ALU = mybir.AluOpType
ACT = mybir.ActivationFunctionType
AX = mybir.AxisListType

B, S, D = 32, 100, 256
LK, DL = 1444, 64
G = 4
NG = B // G
T = G * S
KT = D // 128
H = 16
HD = D // H
E, I = 8, 176
IT = E * I // 128
HK, CQ, R = 128, 192, 64
HALF = CQ // 2
NT = 12
KP = 121
CH = 2
CQS = H * S // CH
QT = [128] * 6 + [32]
F = 1024
EPS = 1e-5
PRIMED = 1
ROUND = 12582912.0


def keys_of(r):
    return KP if r < 4 else KP - 1


def layernorm_stats(v, x, stats, mv, ve, n, done, at, carrier):
    for j in range(n):
        v.bn_stats(stats[:, j, :], x(j)).then_inc(done, 1)
    v.wait_ge(done, PRIMED + at + n)
    v.sem_inc(carrier, 1)
    for j in range(n):
        v.bn_aggr(mv[:, j, :], stats[:, j, :]).then_inc(done, 1)
    v.wait_ge(done, PRIMED + at + 2 * n)
    v.tensor_scalar(ve[:, 0:n], mv[:, 0:n, 1], EPS, None, ALU.add).then_inc(done, 1)


def phase_load(nc, ctx, sem, io, m):
    loaded, gates = sem("inputs_loaded"), sem("gates_ready")
    with nc.Block() as block:
        @block.sync
        def _(sp):
            for c in range(4):
                sp.dma_start(m.x[:, c * 8 * D:(c + 1) * 8 * D].rearrange("s (b d) -> s b d", b=8),
                             io["x"][c * 8:(c + 1) * 8].rearrange("b s d -> s b d")).then_inc(loaded, 16)
            sp.dma_start(m.ident[:], io["ident"]).then_inc(loaded, 16)
            sp.dma_start(m.gates[:, 0:2], io["g_xattn"].partition_broadcast(128)).then_inc(loaded, 16)
            sp.dma_start(m.gates[:, 2:4], io["g_ffn"].partition_broadcast(128)).then_inc(loaded, 16)
            sp.wait_ge(loaded, 16 * 7)

        @block.scalar
        def _(a):
            a.wait_ge(loaded, 16 * 7)
            a.activation(m.tg[:], m.gates[:], ACT.Tanh).then_inc(gates, 1)

        @block.vector
        def _(v):
            v.memset(m.mhalf[:], -0.5).then_inc(gates, 1)
            v.wait_ge(loaded, 16 * 7)
            v.tensor_copy(m.identr[:], m.ident[:]).then_inc(gates, 1)


def phase_l0_attention(nc, outer, sem, io, m):
    NQ = 4
    counters = []
    with ExitStack() as ctx:
        sb = lambda n, s, d=F32: ctx.enter_context(nc.sbuf_tensor(n, s, d))
        ps = lambda n, s, d=F32: ctx.enter_context(nc.psum_tensor(n, s, d))

        def count(name):
            counters.append(sem(name))
            return counters[-1]
        wq_raw, wk_raw, wv_raw = sb("a_wq_raw", [128, KT, D]), sb("a_wk_raw", [DL, D]), sb("a_wv_raw", [DL, D])
        wq = [sb(f"a_wq{i}", [128, KT, D], F32R) for i in range(2)]
        wk = [sb(f"a_wk{i}", [DL, D], F32R) for i in range(2)]
        wv = [sb(f"a_wv{i}", [DL, D], F32R) for i in range(2)]
        wo = sb("a_wo", [128, KT, D])
        lat = sb("a_lat", [S, B * DL])
        mask_raw = sb("a_mask_raw", [S, S])
        mask = sb("a_mask", [S, 4, S], BF16)
        identb = sb("a_identb", [128, 128], BF16)
        headsel_raw, headsel = sb("a_headsel_raw", [128, 8]), sb("a_headsel", [128, 8, S])
        latg = sb("a_latg", [S, G + 1, DL])
        stats, mv, ve, rstd = sb("a_stats", [S, G, 6]), sb("a_mv", [S, G, 2]), sb("a_ve", [S, G]), sb("a_rstd", [S, G])
        xn = sb("a_xn", [S, G, D])
        xt = [sb(f"a_xt{i}", [128, KT, T], F32R) for i in range(2)]
        latt = [sb(f"a_latt{i}", [DL, T], F32R) for i in range(2)]
        qt = sb("a_qt", [128, KT, T])
        kt = sb("a_kt", [128, KT, T])
        kbd = [sb(f"a_kbd{i}", [128, KT, 8, S]) for i in range(2)]
        va = sb("a_va", [S, G, H, HD + 1])
        mx = sb("a_mx", [S, NQ, 4])
        diff = sb("a_diff", [S, NQ, 4, S])
        prob = sb("a_prob", [S, NQ, 4, S])
        pt = sb("a_pt", [S, 2, 4, S])
        rden = sb("a_rden", [S, H])
        cn = sb("a_cn", [S, D])
        ct = sb("a_ct", [128, KT, S])
        s_ps = ps("a_s_ps", [128, 4, 512])
        p_ps = ps("a_p_ps", [128, 2, 512])
        o_ps = ps("a_o_ps", [128, 512])
        f_ps = ps("a_f_ps", [128, 512])
        w_loaded, w_ready = sem("a_w_loaded"), count("a_w_ready")
        ln, rstd_ready, xn_ready = count("a_ln"), count("a_rstd_ready"), count("a_xn_ready")
        dense_mm, dense_out = count("a_dense_mm"), count("a_dense_out")
        kbd_ready, split_hi, latg_ready = count("a_kbd_ready"), count("a_split_hi"), count("a_latg_ready")
        s_ready, max_ready, diff_ready = count("a_s_ready"), count("a_max_ready"), count("a_diff_ready")
        prob_ready, pt_ready, pt_copied, pv_done = count("a_prob_ready"), count("a_pt_ready"), count("a_pt_copied"), count("a_pv_done")
        rden_ready, cn_ready, ct_ready, ct_copied = count("a_rden_ready"), count("a_cn_ready"), count("a_ct_ready"), count("a_ct_copied")
        f_ready, x_added = count("a_f_ready"), count("a_x_added")
        NLOAD = 7
        NW = 11
        ND = 9

        with nc.Block() as block:
            @block.sync
            def _(sp):
                for c in counters:
                    sp.sem_inc(c, PRIMED)
                sp.dma_start(wq_raw[:], io["L0_WqT"].rearrange("(k p) n -> p k n", p=128)).then_inc(w_loaded, 16)
                sp.dma_start(wk_raw[:], io["L0_WkvT"][:, 0:D]).then_inc(w_loaded, 16)
                sp.dma_start(wv_raw[:], io["L0_WkvT"][:, D:2 * D]).then_inc(w_loaded, 16)
                sp.dma_start(wo[:], io["L0_WoutT"].rearrange("(k p) n -> p k n", p=128)).then_inc(w_loaded, 16)
                sp.dma_start(lat[:].rearrange("s (b d) -> s b d", b=B),
                             io["ctx_512"][:, 0:S, :].rearrange("b s d -> s b d")).then_inc(w_loaded, 16)
                sp.dma_start(mask_raw[:], io["causal"]).then_inc(w_loaded, 16)
                sp.dma_start(headsel_raw[:], io["headsel"]).then_inc(w_loaded, 16)
                sp.wait_ge(w_loaded, 16 * NLOAD)

            @block.gpsimd
            def _(g):
                g.wait_ge(w_loaded, 16 * NLOAD)
                with g.Fori(0, NG) as it:
                    g.wait_ge(dense_mm, PRIMED + it * ND)
                    g.tensor_copy(latg[:, 0:G, :].rearrange("s j d -> s (j d)"), lat[:, bass.ds(it * G * DL, G * DL)]).then_inc(latg_ready, 1)
                    g.wait_ge(ln, PRIMED + (it + 1) * (2 * G + 1))
                    g.tensor_tensor(rstd[:], ve[:], m.mhalf[0:S, 0:G], ALU.pow).then_inc(rstd_ready, 1)

            @block.vector
            def _(v):
                v.wait_ge(w_loaded, 16 * NLOAD)
                for raw, w in ((wq_raw, wq), (wk_raw, wk), (wv_raw, wv)):
                    v.tensor_copy(w[0][:], raw[:]).then_inc(w_ready, 1)
                v.wait_ge(w_ready, PRIMED + 3)
                for raw, w in ((wq_raw, wq), (wk_raw, wk), (wv_raw, wv)):
                    v.tensor_tensor(w[1][:], raw[:], w[0][:].bitcast(F32), ALU.subtract).then_inc(w_ready, 1)
                v.tensor_copy(mask[:], mask_raw[:].unsqueeze(1).broadcast_to((S, 4, S))).then_inc(w_ready, 1)
                v.memset(va[:, :, :, HD], 1.0).then_inc(w_ready, 1)
                v.memset(latg[:, G, :], 0.0).then_inc(w_ready, 1)
                v.tensor_copy(identb[:], m.ident[:]).then_inc(w_ready, 1)
                v.tensor_copy(headsel[:], headsel_raw[:].unsqueeze(2).broadcast_to((128, 8, S))).then_inc(w_ready, 1)
                v.wait_ge(w_ready, PRIMED + NW)
                with v.Fori(0, NG) as it:
                    xg = lambda j: m.x[:, bass.ds((it * G + j) * D, D)]
                    layernorm_stats(v, xg, stats, mv, ve, G, ln, it * (2 * G + 1), m.carrier)
                    v.wait_ge(rstd_ready, PRIMED + it + 1)
                    for j in range(G):
                        v.tensor_scalar(xn[:, j, :], xg(j), mv[:, j, 0:1], rstd[:, j:j + 1],
                                        ALU.subtract, ALU.mult).then_inc(xn_ready, 1)
                    for n in range(ND):
                        v.wait_ge(dense_mm, PRIMED + it * ND + n + 1)
                        src = p_ps[:, n % 2, 0:T]
                        if n < 3:
                            hi, lo = (xt[0][:, n, :], xt[1][:, n, :]) if n < 2 else (latt[0][:], latt[1][:])
                            src = src if n < 2 else p_ps[0:DL, 0, 0:T]
                            v.tensor_copy(hi, src).then_inc(split_hi, 1)
                            v.wait_ge(split_hi, PRIMED + it * 3 + n + 1)
                            v.tensor_tensor(lo, src, hi.bitcast(F32), ALU.subtract).then_inc(dense_out, 1)
                        elif n < 5:
                            v.tensor_copy(qt[:, n - 3, :], src).then_inc(dense_out, 1)
                        elif n < 7:
                            v.tensor_copy(kt[:, n - 5, :], src).then_inc(dense_out, 1)
                        else:
                            for j in range(2):
                                ins = v.tensor_copy(va[:, 2 * (n - 7) + j, :, 0:HD],
                                                    p_ps[0:S, n % 2, j * D:(j + 1) * D].rearrange("p (h d) -> p h d", h=H))
                            ins.then_inc(dense_out, 1)

                    def block_keys(b):
                        if b >= 2:
                            v.wait_ge(s_ready, PRIMED + (it * G + b - 1) * NQ)
                        for k in range(KT):
                            ins = v.tensor_tensor(kbd[b % 2][:, k], headsel[:],
                                                  kt[:, k, b * S:(b + 1) * S].unsqueeze(1).broadcast_to((128, 8, S)),
                                                  ALU.mult)
                        ins.then_inc(kbd_ready, 1)

                    v.wait_ge(dense_out, PRIMED + it * ND + 7)
                    block_keys(0)
                    block_keys(1)
                    for b in range(G):
                        for q in range(NQ):
                            n = it * G * NQ + b * NQ + q
                            v.wait_ge(s_ready, PRIMED + n + 1)
                            sc = s_ps[0:S, q, 0:4 * S].rearrange("p (h k) -> p h k", h=4)
                            v.tensor_reduce(mx[:, q, :], sc, AX.X, ALU.max).then_inc(max_ready, 1)
                            v.wait_ge(max_ready, PRIMED + n + 1)
                            if b > 0:
                                v.wait_ge(prob_ready, PRIMED + n - NQ + 1)
                            v.tensor_tensor(diff[:, q], sc, mx[:, q, :].unsqueeze(2).broadcast_to((S, 4, S)),
                                            ALU.subtract).then_inc(diff_ready, 1)
                        if b + 2 < G:
                            block_keys(b + 2)
                        nb = it * G + b
                        v.wait_ge(pv_done, PRIMED + (nb + 1) * NQ)
                        o = o_ps[0:S, 0:H * (HD + 1)].rearrange("p (h d) -> p h d", h=H)
                        v.reciprocal(rden[:], o[:, :, HD]).then_inc(rden_ready, 1)
                        v.wait_ge(rden_ready, PRIMED + nb + 1)
                        v.tensor_tensor(cn[:].rearrange("p (h d) -> p h d", h=H), o[:, :, 0:HD],
                                        rden[:].unsqueeze(2).broadcast_to((S, H, HD)), ALU.mult).then_inc(cn_ready, 1)
                        v.wait_ge(f_ready, PRIMED + nb + 1)
                        v.scalar_tensor_tensor(xg(b), f_ps[0:S, 0:D], m.tg[0:S, 0:1], xg(b), ALU.mult, ALU.add).then_inc(x_added, 1)
                    v.wait_ge(x_added, PRIMED + (it + 1) * G)

            @block.scalar
            def _(a):
                with a.Fori(0, NG) as it:
                    for b in range(G):
                        def copy_pt(q):
                            n = it * G * NQ + b * NQ + q
                            a.wait_ge(pt_ready, PRIMED + n + 1)
                            if b * NQ + q >= 2:
                                a.wait_ge(pv_done, PRIMED + n - 1)
                            a.activation(pt[:, q % 2], p_ps[0:S, q % 2, 0:4 * S].rearrange("p (h k) -> p h k", h=4),
                                         ACT.Copy).then_inc(pt_copied, 1)
                        for q in range(NQ):
                            n = it * G * NQ + b * NQ + q
                            a.wait_ge(diff_ready, PRIMED + n + 1)
                            if b > 0:
                                a.wait_ge(pt_ready, PRIMED + n - NQ + 1)
                            a.activation(prob[:, q], diff[:, q], ACT.Exp, scale=HD ** -0.5).then_inc(prob_ready, 1)
                            if q > 0:
                                copy_pt(q - 1)
                        copy_pt(NQ - 1)
                        nb = it * G + b
                        a.wait_ge(ct_ready, PRIMED + nb + 1)
                        a.activation(ct[:], f_ps[:, 256:256 + KT * S].rearrange("p (k s) -> p k s", k=KT), ACT.Copy).then_inc(ct_copied, 1)

            @block.tensor
            def _(pe):
                pe.wait_ge(w_ready, PRIMED + NW)
                with pe.Fori(0, NG) as it:
                    def out_of(n):
                        if n >= 2:
                            pe.wait_ge(dense_out, PRIMED + it * ND + n - 1)
                        else:
                            pe.wait_ge(pt_copied, PRIMED + it * G * NQ)
                        return p_ps[:, n % 2, 0:T]
                    pe.wait_ge(xn_ready, PRIMED + (it + 1) * G)
                    for k in range(KT):
                        o = out_of(k)
                        for j in range(G):
                            mm = pe.transpose(o[:, j * S:(j + 1) * S], xn[:, j, k * 128:(k + 1) * 128], m.ident[0:S, 0:S])
                        mm.then_inc(dense_mm, 1)
                    o = out_of(2)
                    pe.wait_ge(latg_ready, PRIMED + it + 1)
                    for j in range(G):
                        mm = pe.transpose(o[:, j * S:(j + 1) * S], latg[:, j:j + 2, :], m.ident[0:S, 0:S])
                    mm.then_inc(dense_mm, 1)
                    pe.wait_ge(dense_out, PRIMED + it * ND + 2)
                    for n in range(2):
                        o = out_of(3 + n)
                        for i, (w, x) in enumerate(((0, 0), (0, 1), (1, 0))):
                            for k in range(KT):
                                mm = pe.matmul(o, wq[w][:, k, n * 128:(n + 1) * 128], xt[x][:, k, :],
                                               start=(i == 0 and k == 0), stop=(i == 2 and k == KT - 1))
                        mm.then_inc(dense_mm, 1)
                    pe.wait_ge(dense_out, PRIMED + it * ND + 3)
                    for n in range(2):
                        o = out_of(5 + n)
                        for i, (w, x) in enumerate(((0, 0), (0, 1), (1, 0))):
                            mm = pe.matmul(o, wk[w][:, n * 128:(n + 1) * 128], latt[x][:], start=(i == 0), stop=(i == 2))
                        mm.then_inc(dense_mm, 1)
                    for n in range(2):
                        out_of(7 + n)
                        for j in range(2):
                            cols = slice((2 * n + j) * S, (2 * n + j + 1) * S)
                            for i, (w, x) in enumerate(((0, 0), (0, 1), (1, 0))):
                                mm = pe.matmul(p_ps[0:S, (7 + n) % 2, j * D:(j + 1) * D], latt[x][:, cols], wv[w][:],
                                               start=(i == 0), stop=(i == 2))
                        mm.then_inc(dense_mm, 1)

                    def scores(b, q):
                        n = it * G * NQ + b * NQ + q
                        pe.wait_ge(kbd_ready, PRIMED + it * G + b + 1)
                        pe.wait_ge(diff_ready, PRIMED + n - NQ + 1 if b > 0 else it * G * NQ)
                        o = s_ps[0:S, q, 0:4 * S]
                        pe.matmul(o, identb[0:S, 0:S], mask[:].rearrange("p h k -> p (h k)"), start=True, stop=False)
                        mm = pe.matmul(o, qt[:, q // 2, b * S:(b + 1) * S],
                                       kbd[b % 2][:, q // 2, 4 * (q % 2):4 * (q % 2) + 4, :].rearrange("p h k -> p (h k)"),
                                       start=False, stop=True)
                        mm.then_inc(s_ready, 1)

                    pe.wait_ge(dense_out, PRIMED + (it + 1) * ND)
                    for q in range(NQ):
                        scores(0, q)
                    for b in range(G):
                        nb = it * G + b

                        def probs_value(q):
                            n = nb * NQ + q
                            pe.wait_ge(pt_copied, PRIMED + n + 1)
                            if q == 0:
                                pe.wait_ge(cn_ready, PRIMED + nb)
                            for h in range(4):
                                mm = pe.matmul(o_ps[0:S, (4 * q + h) * (HD + 1):(4 * q + h + 1) * (HD + 1)],
                                               pt[:, q % 2, h, :], va[:, b, 4 * q + h, :], start=True, stop=True)
                            mm.then_inc(pv_done, 1)
                        for q in range(NQ):
                            n = nb * NQ + q
                            if b + 1 < G:
                                scores(b + 1, q)
                            pe.wait_ge(prob_ready, PRIMED + n + 1)
                            if b * NQ + q >= 2:
                                pe.wait_ge(pt_copied, PRIMED + n - 1)
                            for h in range(4):
                                mm = pe.transpose(p_ps[0:S, q % 2, h * S:(h + 1) * S], prob[:, q, h, :], m.ident[0:S, 0:S])
                            mm.then_inc(pt_ready, 1)
                            if q > 0:
                                probs_value(q - 1)
                        probs_value(NQ - 1)
                        pe.wait_ge(cn_ready, PRIMED + nb + 1)
                        pe.wait_ge(x_added, PRIMED + nb)
                        for k in range(KT):
                            mm = pe.transpose(f_ps[:, 256 + k * S:256 + (k + 1) * S], cn[:, k * 128:(k + 1) * 128], m.ident[0:S, 0:S])
                        mm.then_inc(ct_ready, 1)
                        pe.wait_ge(ct_copied, PRIMED + nb + 1)
                        for k in range(KT):
                            mm = pe.matmul(f_ps[0:S, 0:D], ct[:, k, :], wo[:, k, :], start=(k == 0), stop=(k == KT - 1))
                        mm.then_inc(f_ready, 1)


def phase_moe(nc, outer, sem, io, m):
    counters = []
    with ExitStack() as ctx:
        sb = lambda n, s, d=F32: ctx.enter_context(nc.sbuf_tensor(n, s, d))
        ps = lambda n, s, d=F32: ctx.enter_context(nc.psum_tensor(n, s, d))

        def count(name):
            counters.append(sem(name))
            return counters[-1]
        EI = E * I
        raw = [sb(f"b_raw{i}", [128, KT, EI]) for i in range(2)]
        wg = [sb(f"b_wg{i}", [128, KT, EI], F32R) for i in range(2)]
        wu = [sb(f"b_wu{i}", [128, KT, EI], F32R) for i in range(2)]
        wd = sb("b_wd", [128, IT, D])
        wr_raw = sb("b_wr_raw", [128, KT, E])
        wr = [sb(f"b_wr{i}", [128, KT, E], F32R) for i in range(2)]
        expert_raw = sb("b_expert_raw", [40, IT, 128])
        expert = sb("b_expert", [40, IT, 128], F32R)
        iota8 = sb("b_iota8", [S, E])
        stats, mv, ve, rstd = sb("b_stats", [S, G, 6]), sb("b_mv", [S, G, 2]), sb("b_ve", [S, G]), sb("b_rstd", [S, G])
        xn = sb("b_xn", [S, G, D])
        xt = [sb(f"b_xt{i}", [128, KT, T], F32R) for i in range(2)]
        rmax, rdiff, rexp, rsum, rinv = (sb("b_rmax", [S, G]), sb("b_rdiff", [S, G, E]), sb("b_rexp", [S, G, E]),
                                         sb("b_rsum", [S, G]), sb("b_rinv", [S, G]))
        rprob, top, topi, topf = sb("b_rprob", [S, G, E]), sb("b_top", [S, G, 8]), sb("b_topi", [S, G, 8], U32), sb("b_topf", [S, G, 2])
        wsum, winv, wtop = sb("b_wsum", [S, G]), sb("b_winv", [S, G]), sb("b_wtop", [S, G, 2])
        comb1, comb2, comb = sb("b_comb1", [S, G, E]), sb("b_comb2", [S, G, E]), sb("b_comb", [S, G, E])
        combt = sb("b_combt", [40, T], F32R)
        silu = sb("b_silu", [128, 2, T])
        gated = sb("b_gated", [128, 2, T])
        act = sb("b_act", [128, 2, T])
        gu_ps = ps("b_gu_ps", [128, 2, 3, 512])
        y_ps = ps("b_y_ps", [128, 2, 512])
        w_loaded, w_ready, raw_split = sem("b_w_loaded"), count("b_w_ready"), count("b_raw_split")
        ln, rstd_ready, xn_ready = count("b_ln"), count("b_rstd_ready"), count("b_xn_ready")
        xt_ps_ready, split_hi, xt_ready = count("b_xt_ps_ready"), count("b_split_hi"), count("b_xt_ready")
        logits_ready, router, rexp_ready = count("b_logits_ready"), count("b_router"), count("b_rexp_ready")
        combt_ps_ready, combt_hi, combt_ready = count("b_combt_ps_ready"), count("b_combt_hi"), count("b_combt_ready")
        gate_ready, up_ready, spread_ready = count("b_gate_ready"), count("b_up_ready"), count("b_spread_ready")
        silu_ready, gated_ready, act_ready, down_done = count("b_silu_ready"), count("b_gated_ready"), count("b_act_ready"), count("b_down_done")
        x_added = count("b_x_added")
        NW = 8
        NR = 11 + 4 * G

        with nc.Block() as block:
            @block.sync
            def _(sp):
                for c in counters:
                    sp.sem_inc(c, PRIMED)
                sp.dma_start(raw[0][:], io["L0_gateT"].rearrange("(k p) n -> p k n", p=128)).then_inc(w_loaded, 16)
                sp.dma_start(raw[1][:], io["L0_upT"].rearrange("(k p) n -> p k n", p=128)).then_inc(w_loaded, 16)
                sp.dma_start(wd[:], io["L0_downT"].rearrange("(t p) n -> p t n", p=128)).then_inc(w_loaded, 16)
                sp.dma_start(wr_raw[:], io["L0_routerT"].rearrange("(k p) n -> p k n", p=128)).then_inc(w_loaded, 16)
                sp.dma_start(expert_raw[:].rearrange("p t n -> p (t n)"), io["expert_rows"]).then_inc(w_loaded, 16)
                sp.dma_start(iota8[:], io["iota8"].partition_broadcast(S)).then_inc(w_loaded, 16)
                sp.wait_ge(w_loaded, 16 * 6)

            @block.gpsimd
            def _(g):
                with g.Fori(0, NG) as it:
                    g.wait_ge(ln, PRIMED + (it + 1) * (2 * G + 1))
                    g.tensor_tensor(rstd[:], ve[:], m.mhalf[0:S, 0:G], ALU.pow).then_inc(rstd_ready, 1)

            @block.vector
            def _(v):
                v.wait_ge(w_loaded, 16 * 6)
                for r_, w in ((raw[0], wg), (raw[1], wu), (wr_raw, wr)):
                    v.tensor_copy(w[0][:], r_[:]).then_inc(w_ready, 1)
                v.wait_ge(w_ready, PRIMED + 3)
                for r_, w in ((raw[0], wg), (raw[1], wu), (wr_raw, wr)):
                    v.tensor_tensor(w[1][:], r_[:], w[0][:].bitcast(F32), ALU.subtract).then_inc(w_ready, 1)
                v.tensor_copy(expert[:], expert_raw[:]).then_inc(w_ready, 1)
                v.memset(combt[:].bitcast(F32), 0.0).then_inc(w_ready, 1)
                v.wait_ge(w_ready, PRIMED + NW)
                with v.Fori(0, NG) as it:
                    xg = lambda j: m.x[:, bass.ds((it * G + j) * D, D)]
                    layernorm_stats(v, xg, stats, mv, ve, G, ln, it * (2 * G + 1), m.carrier)
                    v.wait_ge(rstd_ready, PRIMED + it + 1)
                    for j in range(G):
                        v.tensor_scalar(xn[:, j, :], xg(j), mv[:, j, 0:1], rstd[:, j:j + 1],
                                        ALU.subtract, ALU.mult).then_inc(xn_ready, 1)
                    for k in range(KT):
                        v.wait_ge(xt_ps_ready, PRIMED + it * KT + k + 1)
                        v.tensor_copy(xt[0][:, k, :], gu_ps[:, 0, k, 0:T]).then_inc(split_hi, 1)
                        v.wait_ge(split_hi, PRIMED + it * KT + k + 1)
                        v.tensor_tensor(xt[1][:, k, :], gu_ps[:, 0, k, 0:T], xt[0][:, k, :].bitcast(F32),
                                        ALU.subtract).then_inc(xt_ready, 1)
                    n = [0]

                    def step(ins):
                        ins.then_inc(router, 1)
                        n[0] += 1

                    def settle():
                        v.wait_ge(router, PRIMED + it * NR + n[0])
                    v.wait_ge(logits_ready, PRIMED + it + 1)
                    logits = gu_ps[0:S, 0, 2, 0:G * E].rearrange("p (b e) -> p b e", b=G)
                    over = lambda a: a.unsqueeze(2).broadcast_to((S, G, E))
                    step(v.tensor_reduce(rmax[:], logits, AX.X, ALU.max))
                    settle()
                    step(v.tensor_tensor(rdiff[:], logits, over(rmax[:]), ALU.subtract))
                    v.wait_ge(rexp_ready, PRIMED + it + 1)
                    step(v.tensor_reduce(rsum[:], rexp[:], AX.X, ALU.add))
                    settle()
                    step(v.reciprocal(rinv[:], rsum[:]))
                    settle()
                    step(v.tensor_tensor(rprob[:], rexp[:], over(rinv[:]), ALU.mult))
                    settle()
                    v.sem_inc(m.carrier, 1)
                    for b in range(G):
                        step(v.max(top[:, b, :], rprob[:, b, :]))
                    settle()
                    v.sem_inc(m.carrier, 1)
                    for b in range(G):
                        step(v.max_index(topi[:, b, :], top[:, b, :], rprob[:, b, :]))
                    step(v.tensor_tensor(wsum[:], top[:, :, 0], top[:, :, 1], ALU.add))
                    settle()
                    step(v.tensor_copy(topf[:], topi[:, :, 0:2]))
                    step(v.tensor_scalar(wsum[:], wsum[:], 1e-20, None, ALU.add))
                    settle()
                    step(v.reciprocal(winv[:], wsum[:]))
                    settle()
                    step(v.tensor_tensor(wtop[:], top[:, :, 0:2], winv[:].unsqueeze(2).broadcast_to((S, G, 2)), ALU.mult))
                    settle()
                    for b in range(G):
                        step(v.tensor_scalar(comb1[:, b, :], iota8[:], topf[:, b, 0:1], wtop[:, b, 0:1], ALU.is_equal, ALU.mult))
                        step(v.tensor_scalar(comb2[:, b, :], iota8[:], topf[:, b, 1:2], wtop[:, b, 1:2], ALU.is_equal, ALU.mult))
                    settle()
                    step(v.tensor_tensor(comb[:], comb1[:], comb2[:], ALU.add))
                    assert n[0] == NR
                    v.wait_ge(combt_ps_ready, PRIMED + it + 1)
                    cps = gu_ps[0:E, 1, 2, 0:T]
                    v.tensor_copy(combt[0:E, :], cps).then_inc(combt_hi, 1)
                    v.wait_ge(combt_hi, PRIMED + it + 1)
                    v.tensor_tensor(combt[32:32 + E, :], cps, combt[0:E, :].bitcast(F32), ALU.subtract).then_inc(combt_ready, 1)
                    for t in range(IT):
                        i = it * IT + t
                        v.wait_ge(silu_ready, PRIMED + i + 1)
                        v.wait_ge(up_ready, PRIMED + i + 1)
                        v.tensor_tensor(gated[:, t % 2, :], silu[:, t % 2, :], gu_ps[:, t % 2, 1, 0:T], ALU.mult).then_inc(gated_ready, 1)
                        v.wait_ge(gated_ready, PRIMED + i + 1)
                        v.wait_ge(spread_ready, PRIMED + i + 1)
                        if t >= 2:
                            v.wait_ge(down_done, PRIMED + i - 1)
                        v.tensor_tensor(act[:, t % 2, :], gated[:, t % 2, :], gu_ps[:, t % 2, 2, 0:T], ALU.mult).then_inc(act_ready, 1)
                    v.wait_ge(down_done, PRIMED + (it + 1) * IT)
                    for h in range(2):
                        xs = m.x[:, bass.ds((it * G + 2 * h) * D, 2 * D)]
                        v.scalar_tensor_tensor(xs, y_ps[0:S, h, :], m.tg[0:S, 2:3], xs, ALU.mult, ALU.add).then_inc(x_added, 1)
                    v.wait_ge(x_added, PRIMED + (it + 1) * 2)

            @block.scalar
            def _(a):
                with a.Fori(0, NG) as it:
                    a.wait_ge(router, PRIMED + it * NR + 2)
                    a.activation(rexp[:], rdiff[:], ACT.Exp).then_inc(rexp_ready, 1)
                    for t in range(IT):
                        i = it * IT + t
                        a.wait_ge(gate_ready, PRIMED + i + 1)
                        if t >= 2:
                            a.wait_ge(gated_ready, PRIMED + i - 1)
                        a.activation(silu[:, t % 2, :], gu_ps[:, t % 2, 0, 0:T], ACT.Silu).then_inc(silu_ready, 1)

            @block.tensor
            def _(pe):
                pe.wait_ge(w_ready, PRIMED + NW)
                parts = ((0, 0), (0, 1), (1, 0))
                with pe.Fori(0, NG) as it:
                    pe.wait_ge(xn_ready, PRIMED + (it + 1) * G)
                    for k in range(KT):
                        for j in range(G):
                            mm = pe.transpose(gu_ps[:, 0, k, j * S:(j + 1) * S], xn[:, j, k * 128:(k + 1) * 128], m.ident[0:S, 0:S])
                        mm.then_inc(xt_ps_ready, 1)
                    pe.wait_ge(xt_ready, PRIMED + (it + 1) * KT)
                    for b in range(G):
                        for i, (w, x) in enumerate(parts):
                            for k in range(KT):
                                mm = pe.matmul(gu_ps[0:S, 0, 2, b * E:(b + 1) * E], xt[x][:, k, b * S:(b + 1) * S], wr[w][:, k, :],
                                               start=(i == 0 and k == 0), stop=(i == 2 and k == KT - 1))
                    mm.then_inc(logits_ready, 1)

                    def rows_of(t):
                        n = it * IT + t
                        if t >= 2:
                            pe.wait_ge(act_ready, PRIMED + n - 1)
                        for j, (w, done) in enumerate(((wg, gate_ready), (wu, up_ready))):
                            for i, (wi, x) in enumerate(parts):
                                for k in range(KT):
                                    mm = pe.matmul(gu_ps[:, t % 2, j, 0:T], w[wi][:, k, t * 128:(t + 1) * 128], xt[x][:, k, :],
                                                   start=(i == 0 and k == 0), stop=(i == 2 and k == KT - 1))
                            mm.then_inc(done, 1)

                    def spread(t):
                        pe.matmul(gu_ps[:, t % 2, 2, 0:T], expert[:, t, :], combt[:], start=True, stop=True).then_inc(spread_ready, 1)

                    def down(t):
                        n = it * IT + t
                        pe.wait_ge(act_ready, PRIMED + n + 1)
                        if t == 0:
                            pe.wait_ge(x_added, PRIMED + it * 2)
                        for b in range(G):
                            mm = pe.matmul(y_ps[0:S, b // 2, (b % 2) * D:(b % 2 + 1) * D], act[:, t % 2, b * S:(b + 1) * S], wd[:, t, :],
                                           start=(t == 0 and b % 2 == 0), stop=(t == IT - 1), skip_group_check=True)
                        mm.then_inc(down_done, 1)
                    rows_of(0)
                    rows_of(1)
                    pe.wait_ge(router, PRIMED + (it + 1) * NR)
                    for b in range(G):
                        mm = pe.transpose(gu_ps[0:E, 1, 2, b * S:(b + 1) * S], comb[:, b, :], m.ident[0:S, 0:S])
                    mm.then_inc(combt_ps_ready, 1)
                    pe.wait_ge(combt_ready, PRIMED + it + 1)
                    spread(0)
                    spread(1)
                    for t in range(2, IT):
                        rows_of(t)
                        spread(t)
                        down(t - 2)
                    down(IT - 2)
                    down(IT - 1)


def phase_l1_weights(nc, outer, sem, io, m):
    with ExitStack() as ctx:
        sb = lambda n, s, d=F32: ctx.enter_context(nc.sbuf_tensor(n, s, d))
        ps = lambda n, s, d=F32: ctx.enter_context(nc.psum_tensor(n, s, d))
        wq, kcq = sb("w_wq", [128, H, D]), sb("w_kcq", [128, H, CQ])
        qr, kr = sb("w_qr", [R, H, CQ]), sb("w_kr", [R, H, DL])
        kckv, wo = sb("w_kckv", [128, H, DL]), sb("w_wo", [128, H, D])
        a_ps = ps("w_a_ps", [128, 4, 512])
        b_ps = ps("w_b_ps", [128, 4, 512])
        loaded = sem("w_loaded")
        a_mm, a_hi, a_out = sem("w_a_mm"), sem("w_a_hi"), sem("w_a_out")
        m_mm, m_out, c_mm, c_out = sem("w_m_mm"), sem("w_m_out"), sem("w_c_mm"), sem("w_c_out")
        with nc.Block() as block:
            @block.sync
            def _(sp):
                sp.dma_start(wq[:], io["L1_xattn_Wq"].rearrange("(h k) d -> k h d", k=HK)).then_inc(loaded, 16)
                sp.dma_start(kcq[:], io["L1_xattn_w_kc_q"].rearrange("h k q -> k h q")).then_inc(loaded, 16)
                sp.dma_start(qr[:], io["L1_qrT"]).then_inc(loaded, 16)
                sp.dma_start(kr[:], io["L1_krT"]).then_inc(loaded, 16)
                sp.dma_start(kckv[:], io["L1_xattn_w_kc_kv"].rearrange("h k d -> k h d")).then_inc(loaded, 16)
                sp.dma_start(wo[:], io["L1_WoT"].rearrange("(h k) o -> k h o", k=HK)).then_inc(loaded, 16)
                sp.wait_ge(loaded, 16 * 6)

            @block.tensor
            def _(pe):
                pe.wait_ge(loaded, 16 * 6)
                for h in range(H):
                    if h >= 4:
                        pe.wait_ge(a_out, h - 3)
                    for k in range(KT):
                        mm = pe.matmul(a_ps[:, h % 4, k * CQ:(k + 1) * CQ], wq[:, h, k * 128:(k + 1) * 128], kcq[:, h, :], start=True, stop=True)
                    mm.then_inc(a_mm, 1)
                for h in range(H):
                    if h >= 2:
                        pe.wait_ge(m_out, h - 1)
                    for i in range(2):
                        mm = pe.matmul(b_ps[0:HALF, h % 2, i * DL:(i + 1) * DL], qr[:, h, i * HALF:(i + 1) * HALF], kr[:, h, :], start=True, stop=True)
                    mm.then_inc(m_mm, 1)
                for hh in range(H // 2):
                    if hh >= 2:
                        pe.wait_ge(c_out, hh - 1)
                    for c in range(2):
                        mm = pe.matmul(b_ps[c * DL:(c + 1) * DL, 2 + hh % 2, 0:D], kckv[:, 2 * hh + c, :], wo[:, 2 * hh + c, :], start=True, stop=True)
                    mm.then_inc(c_mm, 1)

            @block.vector
            def _(v):
                for h in range(H):
                    v.wait_ge(a_mm, h + 1)
                    src = a_ps[:, h % 4, 0:KT * CQ].rearrange("p (k q) -> p k q", k=KT)
                    v.tensor_copy(m.a[0][:, :, h, :], src).then_inc(a_hi, 1)
                    v.wait_ge(a_hi, h + 1)
                    v.tensor_tensor(m.a[1][:, :, h, :], src, m.a[0][:, :, h, :].bitcast(F32), ALU.subtract).then_inc(a_out, 1)

            @block.scalar
            def _(a):
                for h in range(H):
                    a.wait_ge(m_mm, h + 1)
                    src = b_ps[0:HALF, h % 2, 0:2 * DL].rearrange("p (i d) -> p i d", i=2)
                    a.activation(m.mqk[:, :, h, :], src, ACT.Copy).then_inc(m_out, 1)
                for hh in range(H // 2):
                    a.wait_ge(c_mm, hh + 1)
                    a.activation(m.cvo[:, hh, :], b_ps[:, 2 + hh % 2, 0:D], ACT.Copy).then_inc(c_out, 1)


def phase_l1_attention(nc, outer, sem, io, m):
    NQT = len(QT)
    HEADS = [2 * i for i in range(H // 2)] + [2 * i + 1 for i in range(H // 2)]
    with ExitStack() as ctx:
        counters = []
        sb = lambda n, s, d=F32: ctx.enter_context(nc.sbuf_tensor(n, s, d))
        ps = lambda n, s, d=F32: ctx.enter_context(nc.psum_tensor(n, s, d))

        def count(name):
            counters.append(sem(name))
            return counters[-1]
        qcos, qsin = sb("c_qcos", [HALF, 2, S]), sb("c_qsin", [HALF, 2, S])
        kcos, ksin = sb("c_kcos", [KP, NT, DL]), sb("c_ksin", [KP, NT, DL])
        stats, mv, ve, rstd = sb("c_stats", [S, G, 6]), sb("c_mv", [S, G, 2]), sb("c_ve", [S, G]), sb("c_rstd", [S, G])
        xt = [sb(f"c_xt{i}", [128, KT, T], F32R) for i in range(2)]
        q1 = sb("c_q1", [128, G, CH * CQS], F32R)
        q2 = sb("c_q2", [65, G, CH * CQS], F32R)
        kv = sb("c_kv", [KP, NT, DL])
        kva = [sb(f"c_kva{i}", [KP, NT, DL + 1]) for i in range(2)]
        k1 = [sb(f"c_k1{i}", [128, NT * KP], F32R) for i in range(2)]
        k2 = [sb(f"c_k2{i}", [65, NT * KP], F32R) for i in range(2)]
        mneg = sb("c_mneg", [128, NQT, 65], F32R)
        prob = sb("c_prob", [KP, 2, CQS])
        rc, rs = (prob[0:HALF, i, :].rearrange("p (i n) -> p i n", i=2) for i in range(2))
        late = sb("c_late", [128, NQT * CH * DL + CQS])
        xn = late[0:S, 0:G * D].rearrange("p (b d) -> p b d", b=G)
        rot = late[0:HALF, 0:4 * T].rearrange("p (a i n) -> p a i n", a=2, i=2)
        cn = late[:, 0:NQT * CH * DL].rearrange("p (t c d) -> p t c d", t=NQT, c=CH)
        ct = late[:, NQT * CH * DL:]
        rden = sb("c_rden", [128, NQT])
        s_ps = ps("c_s_ps", [128, 2, 2, 512])
        m_ps = ps("c_m_ps", [128, 3, 512])
        o_ps = ps("c_o_ps", [128, 512])
        m_flat = m_ps[:, :, :].rearrange("p a n -> p (a n)")
        t_loaded, consts = sem("c_t_loaded"), count("c_consts")
        ln, rstd_ready, xn_ready = count("c_ln"), count("c_rstd_ready"), count("c_xn_ready")
        xt_ps_ready, split_hi, xt_ready = count("c_xt_ps_ready"), count("c_split_hi"), count("c_xt_ready")
        wide_ready, roped, rot_ready = count("c_wide_ready"), count("c_roped"), count("c_rot_ready")
        q_ps_ready, q1_ready, q2_ready = count("c_q_ps_ready"), count("c_q1_ready"), count("c_q2_ready")
        kv_loaded, kv_roped, kva_ready = sem("c_kv_loaded"), count("c_kv_roped"), count("c_kva_ready")
        kt_ready, k1_hi, k1_ready, k2_ready = count("c_kt_ready"), count("c_k1_hi"), count("c_k1_ready"), count("c_k2_ready")
        maxs_ready, mneg_ready, row_ready, row_copied = count("c_maxs_ready"), count("c_mneg_ready"), count("c_row_ready"), count("c_row_copied")
        s_ready, prob_ready, pv_done = count("c_s_ready"), count("c_prob_ready"), count("c_pv_done")
        rden_ready, cn_ready, ct_ps_ready, ct_ready = count("c_rden_ready"), count("c_cn_ready"), count("c_ct_ps_ready"), count("c_ct_ready")
        f_ready, x_added = count("c_f_ready"), count("c_x_added")
        parts = ((0, 0), (0, 1), (1, 0))

        def beside_head(i):
            if i == 3:
                return [("keys", 0)]
            if i >= 11:
                return [("max", 0, 0, t) for t in range(NQT) if t * 5 // NQT == i - 11] + ([("row", 0, 0)] if i == 15 else [])
            return []

        def beside_tile(j, c, r):
            todo = []
            if c == 0:
                if j > 0 and r in (1, 2):
                    todo.append(("turn", j - 1) if r == 1 else ("project", j - 1))
                if 3 <= r < 3 + NQT:
                    todo.append(("max", j, 1, r - 3))
                if r == 11:
                    todo.append(("row", j, 1))
            elif j + 1 < G:
                if r == 1:
                    todo.append(("keys", j + 1))
                if 3 <= r < 3 + NQT:
                    todo.append(("max", j + 1, 0, r - 3))
                if r == 11:
                    todo.append(("row", j + 1, 0))
            return todo

        with nc.Block() as block:
            @block.sync
            def _(sp):
                for c in counters:
                    sp.sem_inc(c, PRIMED)
                sp.dma_start(qcos[:], io["qcos"]).then_inc(t_loaded, 16)
                sp.dma_start(qsin[:], io["qsin"]).then_inc(t_loaded, 16)
                sp.dma_start(kcos[:], io["kcos"]).then_inc(t_loaded, 16)
                sp.dma_start(ksin[:], io["ksin"]).then_inc(t_loaded, 16)
                with sp.Fori(0, B) as b:
                    sp.wait_ge(kva_ready, PRIMED + b * 2)
                    src = io["ctx_512"][bass.ds(b, 1)].rearrange("b l d -> (b l) d")
                    main = src[0:NT * 120].rearrange("(p r) d -> p r d", r=NT)
                    sp.dma_start(kv[0:120], main).then_inc(kv_loaded, 16)
                    sp.dma_start(kv[120:121, 0:4, :], src[1440:1444].unsqueeze(0)).then_inc(kv_loaded, 16)
                    sp.dma_start(kv[120:121, 4:NT, :], src[1432:1440].unsqueeze(0)).then_inc(kv_loaded, 16)
                sp.wait_ge(kv_loaded, B * 48)
                sp.wait_ge(t_loaded, 16 * 4)

            @block.gpsimd
            def _(g):
                g.wait_ge(t_loaded, 16 * 4)
                with g.Fori(0, NG) as it:
                    def rotate_keys(j):
                        b = it * G + j
                        g.wait_ge(kv_loaded, (b + 1) * 48)
                        if j >= 2:
                            g.wait_ge(pv_done, PRIMED + (b - 1) * CH * NT)
                        else:
                            g.wait_ge(pv_done, PRIMED + it * G * CH * NT)
                        g.tensor_tensor(kva[j % 2][:, :, 0:DL], kv[:], kcos[:], ALU.mult).then_inc(kv_roped, 1)
                        g.wait_ge(kv_roped, PRIMED + 2 * b + 1)
                        g.tensor_tensor(kv[:], kv[:], ksin[:], ALU.mult).then_inc(kv_roped, 1)
                        g.wait_ge(kv_roped, PRIMED + 2 * b + 2)
                        for i in range(2):
                            c0 = slice(i * DL // 2, (i + 1) * DL // 2)
                            c1 = slice((1 - i) * DL // 2, (2 - i) * DL // 2)
                            g.tensor_tensor(kva[j % 2][:, :, c0], kva[j % 2][:, :, c0], kv[:, :, c1], ALU.add).then_inc(kva_ready, 1)

                    def copy_keys(j):
                        g.wait_ge(k1_hi, PRIMED + (it * G + j + 1) * 3)
                        g.sem_inc(m.carrier, 1)
                        g.tensor_copy(k2[j % 2][0:DL, :], k1[j % 2][0:DL, :]).then_inc(k2_ready, 1)
                    g.wait_ge(ln, PRIMED + (it + 1) * (2 * G + 1))
                    g.tensor_tensor(rstd[:], ve[:], m.mhalf[0:S, 0:G], ALU.pow).then_inc(rstd_ready, 1)
                    rotate_keys(0)
                    for i in range(H):
                        n = it * H + i
                        g.wait_ge(roped, PRIMED + 2 * (n + 1))
                        if i >= 2:
                            g.wait_ge(q_ps_ready, PRIMED + n - 1)
                        for a in range(2):
                            ins = g.tensor_tensor(rot[:, i % 2, a, :], rc[:, a, :], rs[:, 1 - a, :], ALU.add)
                        ins.then_inc(rot_ready, 1)
                        if i == 5:
                            copy_keys(0)
                    for j in range(1, G):
                        rotate_keys(j)
                        copy_keys(j)

            @block.vector
            def _(v):
                v.wait_ge(t_loaded, 16 * 4)
                for i in range(2):
                    v.memset(kva[i][:, :, DL], 1.0).then_inc(consts, 1)
                    v.memset(k2[i][DL:DL + 1, :].bitcast(F32), 1.0).then_inc(consts, 1)
                v.memset(mneg[:].bitcast(F32), 0.0).then_inc(consts, 1)
                v.wait_ge(consts, PRIMED + 5)
                with v.Fori(0, NG) as it:
                    xg = lambda j: m.x[:, bass.ds((it * G + j) * D, D)]

                    def split_keys(j):
                        b = it * G + j
                        for k in range(3):
                            cols = slice(k * 4 * KP, (k + 1) * 4 * KP)
                            v.wait_ge(kt_ready, PRIMED + b * 3 + k + 1)
                            v.tensor_copy(k1[j % 2][0:DL, cols], m_ps[0:DL, k, 0:4 * KP]).then_inc(k1_hi, 1)
                            v.wait_ge(k1_hi, PRIMED + b * 3 + k + 1)
                            v.tensor_tensor(k1[j % 2][DL:128, cols], m_ps[0:DL, k, 0:4 * KP], k1[j % 2][0:DL, cols].bitcast(F32),
                                            ALU.subtract).then_inc(k1_ready, 1)

                    def reduce_max(j, c, t):
                        ch, n = (it * G + j) * CH + c, QT[t]
                        v.wait_ge(maxs_ready, PRIMED + ch * NQT + t + 1)
                        v.tensor_reduce(mneg[0:n, t, DL:DL + 1], m_ps[0:n, :, 0:4 * KP], AX.XY, ALU.max, negate=True).then_inc(mneg_ready, 1)

                    def copy_row(j, c):
                        ch = (it * G + j) * CH + c
                        v.wait_ge(row_ready, PRIMED + ch + 1)
                        v.tensor_copy(q2[DL:DL + 1, j, c * CQS:(c + 1) * CQS], m_flat[DL:DL + 1, 0:CQS]).then_inc(row_copied, 1)

                    def normalise(j, c):
                        ch = (it * G + j) * CH + c
                        v.wait_ge(pv_done, PRIMED + (ch + 1) * NT)
                        o = o_ps[:, 0:NQT * (DL + 1)].rearrange("p (t d) -> p t d", t=NQT)
                        last = QT[-1]
                        v.reciprocal(rden[:, 0:NQT - 1], o[:, 0:NQT - 1, DL]).then_inc(rden_ready, 1)
                        v.reciprocal(rden[0:last, NQT - 1:NQT], o[0:last, NQT - 1, DL:DL + 1]).then_inc(rden_ready, 1)
                        v.wait_ge(rden_ready, PRIMED + (ch + 1) * 2)
                        if c == 0 and j > 0:
                            v.wait_ge(ct_ps_ready, PRIMED + it * G + j)
                        v.tensor_tensor(cn[:, 0:NQT - 1, c, :], o[:, 0:NQT - 1, 0:DL],
                                        rden[:, 0:NQT - 1].unsqueeze(2).broadcast_to((128, NQT - 1, DL)), ALU.mult).then_inc(cn_ready, 1)
                        v.tensor_scalar(cn[0:last, NQT - 1, c, :], o[0:last, NQT - 1, 0:DL], rden[0:last, NQT - 1:NQT], None,
                                        ALU.mult).then_inc(cn_ready, 1)

                    def add_x(j):
                        v.wait_ge(f_ready, PRIMED + it * G + j + 1)
                        v.scalar_tensor_tensor(xg(j), m_ps[0:S, 2, 0:D], m.tg[0:S, 1:2], xg(j), ALU.mult, ALU.add).then_inc(x_added, 1)

                    def beside(todo):
                        for what, *at in todo:
                            if what in ("keys", "max", "row", "project"):
                                {"keys": split_keys, "max": reduce_max, "row": copy_row, "project": add_x}[what](*at)

                    layernorm_stats(v, xg, stats, mv, ve, G, ln, it * (2 * G + 1), m.carrier)
                    v.wait_ge(rstd_ready, PRIMED + it + 1)
                    for j in range(G):
                        v.tensor_scalar(xn[:, j, :], xg(j), mv[:, j, 0:1], rstd[:, j:j + 1],
                                        ALU.subtract, ALU.mult).then_inc(xn_ready, 1)
                    for k in range(KT):
                        v.wait_ge(xt_ps_ready, PRIMED + it * KT + k + 1)
                        v.tensor_copy(xt[0][:, k, :], m_ps[:, k, 0:T]).then_inc(split_hi, 1)
                        v.wait_ge(split_hi, PRIMED + it * KT + k + 1)
                        v.tensor_tensor(xt[1][:, k, :], m_ps[:, k, 0:T], xt[0][:, k, :].bitcast(F32), ALU.subtract).then_inc(xt_ready, 1)
                    table = lambda a: a[:].unsqueeze(2).broadcast_to((HALF, 2, G, S))

                    def low_queries(i):
                        n, h = it * H + i, HEADS[i]
                        cols = slice((h % 2) * CQS + (h // 2) * S, (h % 2) * CQS + (h // 2 + 1) * S)
                        v.wait_ge(q1_ready, PRIMED + 2 * n + 2)
                        v.tensor_tensor(q2[0:DL, :, cols], o_ps[0:DL, 0:T].rearrange("p (b s) -> p b s", b=G),
                                        q1[0:DL, :, cols].bitcast(F32), ALU.subtract).then_inc(q2_ready, 1)
                    for i in range(H):
                        n = it * H + i
                        v.wait_ge(wide_ready, PRIMED + n + 1)
                        if i >= 1:
                            v.wait_ge(rot_ready, PRIMED + n)
                        src = s_ps[0:HALF, i % 2, :, 0:T].rearrange("p i (b s) -> p i b s", b=G)
                        v.tensor_tensor(rc.rearrange("p i (b s) -> p i b s", b=G), src, table(qcos), ALU.mult).then_inc(roped, 1)
                        v.tensor_tensor(rs.rearrange("p i (b s) -> p i b s", b=G), src, table(qsin), ALU.mult).then_inc(roped, 1)
                        if i >= 2:
                            low_queries(i - 2)
                        beside(beside_head(i))
                    low_queries(H - 2)
                    low_queries(H - 1)
                    for j in range(G):
                        for c in range(CH):
                            for r in range(NT):
                                if r == 0 and (j, c) != (0, 0):
                                    normalise(j if c else j - 1, 1 - c)
                                beside(beside_tile(j, c, r))
                    normalise(G - 1, 1)
                    add_x(G - 1)
                    v.wait_ge(x_added, PRIMED + (it + 1) * G)

            @block.scalar
            def _(a):
                with a.Fori(0, NG) as it:
                    for i in range(H):
                        n, h = it * H + i, HEADS[i]
                        cols = slice((h % 2) * CQS + (h // 2) * S, (h % 2) * CQS + (h // 2 + 1) * S)
                        a.wait_ge(q_ps_ready, PRIMED + n + 1)
                        for half in range(2):
                            a.activation(q1[half * DL:(half + 1) * DL, :, cols], o_ps[0:DL, 0:T].rearrange("p (b s) -> p b s", b=G),
                                         ACT.Copy).then_inc(q1_ready, 1)
                    for j in range(G):
                        b = it * G + j

                        def copy_turned(jj):
                            a.wait_ge(ct_ps_ready, PRIMED + it * G + jj + 1)
                            a.activation(ct, m_flat[:, 0:CQS], ACT.Copy).then_inc(ct_ready, 1)
                        for c in range(CH):
                            for r in range(NT):
                                n = (b * CH + c) * NT + r
                                a.wait_ge(s_ready, PRIMED + n + 1)
                                if (j * CH + c) * NT + r >= 2:
                                    a.wait_ge(pv_done, PRIMED + n - 1)
                                k = keys_of(r)
                                a.activation(prob[0:k, r % 2, :].rearrange("p (i n) -> p i n", i=2),
                                             s_ps[0:k, r % 2, :, 0:CQS // 2], ACT.Exp).then_inc(prob_ready, 1)
                                for what, *at in beside_tile(j, c, r):
                                    if what == "turn":
                                        copy_turned(*at)
                    copy_turned(G - 1)

            @block.tensor
            def _(pe):
                pe.wait_ge(consts, PRIMED + 5)
                with pe.Fori(0, NG) as it:
                    pe.wait_ge(xn_ready, PRIMED + (it + 1) * G)
                    for k in range(KT):
                        for j in range(G):
                            mm = pe.transpose(m_ps[:, k, j * S:(j + 1) * S], xn[:, j, k * 128:(k + 1) * 128], m.ident[0:S, 0:S])
                        mm.then_inc(xt_ps_ready, 1)
                    pe.wait_ge(xt_ready, PRIMED + (it + 1) * KT)

                    def wide(i):
                        if i >= 2:
                            pe.wait_ge(roped, PRIMED + 2 * (it * H + i - 1))
                        for a in range(2):
                            for p, (w, x) in enumerate(parts):
                                for k in range(KT):
                                    mm = pe.matmul(s_ps[0:HALF, i % 2, a, 0:T], m.a[w][:, k, HEADS[i], a * HALF:(a + 1) * HALF], xt[x][:, k, :],
                                                   start=(p == 0 and k == 0), stop=(p == 2 and k == KT - 1))
                        mm.then_inc(wide_ready, 1)

                    def absorbed(i):
                        n = it * H + i
                        pe.wait_ge(rot_ready, PRIMED + n + 1)
                        if i >= 1:
                            pe.wait_ge(q2_ready, PRIMED + n)
                            pe.wait_ge(q1_ready, PRIMED + 2 * n)
                        for a in range(2):
                            mm = pe.matmul(o_ps[0:DL, 0:T], m.mqk[:, a, HEADS[i], :], rot[:, i % 2, a, :], start=(a == 0), stop=(a == 1))
                        mm.then_inc(q_ps_ready, 1)

                    def turn_keys(j):
                        b = it * G + j
                        pe.wait_ge(kva_ready, PRIMED + (b + 1) * 2)
                        pe.sem_inc(m.carrier, 1)
                        for k in range(3):
                            for r in range(4 * k, 4 * k + 4):
                                mm = pe.transpose(m_ps[0:DL, k, (r - 4 * k) * KP:(r - 4 * k + 1) * KP], kva[j % 2][:, r, 0:DL], m.ident[0:KP, 0:KP])
                            mm.then_inc(kt_ready, 1)

                    def maxima(j, c, t):
                        ch, n = (it * G + j) * CH + c, QT[t]
                        if t > 0:
                            pe.wait_ge(mneg_ready, PRIMED + ch * NQT + t)
                        elif c == 0:
                            pe.wait_ge(k1_ready, PRIMED + (it * G + j + 1) * 3)
                            pe.wait_ge(q1_ready, PRIMED + 2 * (it * H + (H // 2 if j == 0 else H)))
                        elif j > 0:
                            pe.wait_ge(x_added, PRIMED + it * G + j)
                        else:
                            pe.wait_ge(q1_ready, PRIMED + 2 * (it + 1) * H)
                        for k in range(3):
                            mm = pe.matmul(m_ps[0:n, k, 0:4 * KP], q1[:, j, c * CQS + t * 128:c * CQS + t * 128 + n],
                                           k1[j % 2][:, k * 4 * KP:(k + 1) * 4 * KP], start=True, stop=True)
                        mm.then_inc(maxs_ready, 1)

                    def maxima_row(j, c):
                        ch = (it * G + j) * CH + c
                        pe.wait_ge(mneg_ready, PRIMED + (ch + 1) * NQT)
                        for t, n in enumerate(QT):
                            mm = pe.matmul(m_ps[0:DL + 1, t // 4, (t % 4) * 128:(t % 4) * 128 + n], mneg[0:n, t, :],
                                           m.identr[0:n, 0:n], start=True, stop=True)
                        mm.then_inc(row_ready, 1)

                    def turn_outputs(j):
                        pe.wait_ge(cn_ready, PRIMED + (it * G + j + 1) * CH * 2)
                        pe.wait_ge(row_copied, PRIMED + (it * G + j) * CH + (3 if j + 1 < G else 2))
                        for t, w in enumerate(QT):
                            mm = pe.transpose(m_ps[:, t // 4, (t % 4) * 128:(t % 4) * 128 + w], cn[0:w, t, :, :], m.ident[0:w, 0:w])
                        mm.then_inc(ct_ps_ready, 1)

                    def project(j):
                        pe.wait_ge(ct_ready, PRIMED + it * G + j + 1)
                        for hh in range(H // 2):
                            mm = pe.matmul(m_ps[0:S, 2, 0:D], ct[:, hh * S:(hh + 1) * S], m.cvo[:, hh, :], start=(hh == 0), stop=(hh == H // 2 - 1))
                        mm.then_inc(f_ready, 1)

                    def beside(todo):
                        for what, *at in todo:
                            {"keys": turn_keys, "max": maxima, "row": maxima_row, "turn": turn_outputs, "project": project}[what](*at)

                    def scores(j, c, r):
                        n = ((it * G + j) * CH + c) * NT + r
                        k = keys_of(r)
                        if (j * CH + c) * NT + r >= 2:
                            pe.wait_ge(prob_ready, PRIMED + n - 1)
                        if r == 0:
                            pe.wait_ge(row_copied, PRIMED + (it * G + j) * CH + c + 1)
                            pe.wait_ge(k2_ready, PRIMED + it * G + j + 1)
                        for i in range(2):
                            cols = slice(c * CQS + i * CQS // 2, c * CQS + (i + 1) * CQS // 2)
                            o = s_ps[0:k, r % 2, i, 0:CQS // 2]
                            pe.matmul(o, k1[j % 2][:, r * KP:r * KP + k], q1[:, j, cols], start=True, stop=False)
                            mm = pe.matmul(o, k2[j % 2][:, r * KP:r * KP + k], q2[:, j, cols], start=False, stop=True)
                        mm.then_inc(s_ready, 1)

                    def values(j, c, r):
                        n = ((it * G + j) * CH + c) * NT + r
                        pe.wait_ge(prob_ready, PRIMED + n + 1)
                        if r == 0 and (j, c) != (0, 0):
                            pe.wait_ge(cn_ready, PRIMED + ((it * G + j) * CH + c) * 2)
                        k = keys_of(r)
                        for t, w in enumerate(QT):
                            mm = pe.matmul(o_ps[0:w, t * (DL + 1):(t + 1) * (DL + 1)], prob[0:k, r % 2, t * 128:t * 128 + w],
                                           kva[j % 2][0:k, r, :], start=(r == 0 and t == 0), stop=(r == NT - 1), skip_group_check=True)
                        mm.then_inc(pv_done, 1)

                    for i in range(H):
                        wide(i)
                        if i >= 2:
                            absorbed(i - 2)
                        beside(beside_head(i))
                    absorbed(H - 2)
                    absorbed(H - 1)
                    pe.wait_ge(q2_ready, PRIMED + (it + 1) * H)
                    before = None
                    for j in range(G):
                        for c in range(CH):
                            for r in range(NT):
                                scores(j, c, r)
                                beside(beside_tile(j, c, r))
                                if before:
                                    values(*before)
                                before = (j, c, r)
                    values(*before)
                    turn_outputs(G - 1)
                    project(G - 1)


def phase_l1_ffn(nc, outer, sem, io, m):
    FT = F // 128
    counters = []
    with ExitStack() as ctx:
        sb = lambda n, s, d=F32: ctx.enter_context(nc.sbuf_tensor(n, s, d))
        ps = lambda n, s, d=F32: ctx.enter_context(nc.psum_tensor(n, s, d))

        def count(name):
            counters.append(sem(name))
            return counters[-1]
        w1r, w2r = sb("d_w1r", [128, KT, F]), sb("d_w2r", [128, FT, D])
        w1, w2 = sb("d_w1", [128, KT, F], BF16), sb("d_w2", [128, FT, D], BF16)
        b1, gamma, beta, b2 = sb("d_b1", [S, F]), sb("d_gamma", [S, F]), sb("d_beta", [S, F]), sb("d_b2", [S, D])
        ones = sb("d_ones", [128, 128])
        identb = sb("d_identb", [128, 128], BF16)
        wabs, wmean, wscale = sb("d_wabs", [128, 2]), sb("d_wmean", [128, 2]), sb("d_wscale", [128, 2])
        stats, mv, ve, rstd = sb("d_stats", [S, G, 6]), sb("d_mv", [S, G, 2]), sb("d_ve", [S, G]), sb("d_rstd", [S, G])
        xn = sb("d_xn", [S, G, D])
        xmax, xinv, xscale, xdeq = (sb(f"d_x{n}", [S, G]) for n in ("max", "inv", "scale", "deq"))
        xq = sb("d_xq", [S, G, D], BF16)
        xqt = sb("d_xqt", [128, KT, T], BF16)
        h1 = sb("d_h1", [S, G, F])
        hg = sb("d_hg", [S, G, F])
        hstats, hmv, hve, hrstd = sb("d_hstats", [S, G, 2, 6]), sb("d_hmv", [S, G, 2]), sb("d_hve", [S, G]), sb("d_hrstd", [S, G])
        hmax, hinv, hscale, hdeq = (sb(f"d_h{n}", [S, G]) for n in ("max", "inv", "scale", "deq"))
        hq = sb("d_hq", [S, G, F], BF16)
        hqt = sb("d_hqt", [128, 2, FT, S], BF16)
        res = sb("d_res", [S, G, D])
        h_ps = ps("d_h_ps", [128, 2, 1024])
        t_ps = ps("d_t_ps", [128, 2, 1024], BF16)
        y_ps = ps("d_y_ps", [128, 2, 512])
        loaded, w_ready, w_sum = sem("d_loaded"), count("d_w_ready"), count("d_w_sum")
        vec, rstd_ready, hrstd_ready = count("d_vec"), count("d_rstd_ready"), count("d_hrstd_ready")
        xq_ready, xt_ps_ready, xt_ready = count("d_xq_ready"), count("d_xt_ps_ready"), count("d_xt_ready")
        h_ready, h1_ready, hg_ready = count("d_h_ready"), count("d_h1_ready"), count("d_hg_ready")
        hn_ready, hb_ready = count("d_hn_ready"), count("d_hb_ready")
        hq_ready, ht_ps_ready, ht_ready = count("d_hq_ready"), count("d_ht_ps_ready"), count("d_ht_ready")
        y_ready, x_added, stored, res_ready = count("d_y_ready"), count("d_x_added"), sem("d_stored"), count("d_res_ready")
        NPRE = 16
        NV = 17 + 11 * G

        with nc.Block() as block:
            @block.sync
            def _(sp):
                for c in counters:
                    sp.sem_inc(c, PRIMED)
                sp.dma_start(w1r[:], io["L1_w1T"].rearrange("(k p) n -> p k n", p=128)).then_inc(loaded, 16)
                sp.dma_start(w2r[:], io["L1_w2T"].rearrange("(k p) n -> p k n", p=128)).then_inc(loaded, 16)
                for t, n in ((b1, "L1_ffn_b1"), (gamma, "L1_ffn_gamma"), (beta, "L1_ffn_beta"), (b2, "L1_ffn_b2")):
                    sp.dma_start(t[:], io[n].partition_broadcast(S)).then_inc(loaded, 16)
                with sp.Fori(0, NG) as it:
                    sp.wait_ge(x_added, PRIMED + (it + 1) * G)
                    sp.dma_start(io["out"][bass.ds(it * G, G)].rearrange("b s d -> s b d"),
                                 m.x[:, bass.ds(it * G * D, G * D)].rearrange("s (b d) -> s b d", b=G)).then_inc(stored, 16)
                sp.wait_ge(loaded, 16 * 6)
                sp.wait_ge(stored, 16 * NG)

            @block.gpsimd
            def _(g):
                g.wait_ge(w_ready, PRIMED + NPRE)
                with g.Fori(0, NG) as it:
                    g.wait_ge(vec, PRIMED + it * NV + 2 * G + 1)
                    g.tensor_tensor(rstd[:], ve[:], m.mhalf[0:S, 0:G], ALU.pow).then_inc(rstd_ready, 1)
                    for j in range(G):
                        n = it * G + j
                        g.wait_ge(vec, PRIMED + it * NV + 2 * G + 1 + G + 8 + 4 * (j + 1))
                        g.tensor_tensor(hrstd[:, j:j + 1], hve[:, j:j + 1], m.mhalf[0:S, 0:1], ALU.pow).then_inc(hrstd_ready, 1)
                        g.wait_ge(hn_ready, PRIMED + n + 1)
                        g.tensor_tensor(h1[:, j, :], h1[:, j, :], gamma[:], ALU.mult).then_inc(hb_ready, 1)
                        g.wait_ge(hb_ready, PRIMED + 2 * n + 1)
                        g.tensor_tensor(h1[:, j, :], h1[:, j, :], beta[:], ALU.add).then_inc(hb_ready, 1)

            @block.vector
            def _(v):
                v.wait_ge(loaded, 16 * 6)
                n = [0]

                def pre(ins):
                    ins.then_inc(w_ready, 1)
                    n[0] += 1
                    v.wait_ge(w_ready, PRIMED + n[0])
                pre(v.memset(ones[:], 1.0))
                pre(v.tensor_reduce(wabs[:, 0:1], w1r[:], AX.XY, ALU.add, apply_absolute_value=True))
                pre(v.tensor_reduce(wabs[:, 1:2], w2r[:], AX.XY, ALU.add, apply_absolute_value=True))
                v.wait_ge(w_sum, PRIMED + 1)
                pre(v.tensor_scalar(wmean[:], h_ps[:, 0, 0:2], 1.0 / (F * D), EPS, ALU.mult, ALU.max))
                pre(v.reciprocal(wscale[:], wmean[:]))
                pre(v.tensor_scalar(wmean[:], wmean[:], 1.0 / 127.0, None, ALU.mult))
                for i, (r_, w) in enumerate(((w1r, w1), (w2r, w2))):
                    pre(v.tensor_scalar(r_[:], r_[:], wscale[:, i:i + 1], ROUND, ALU.mult, ALU.add))
                    pre(v.tensor_scalar(r_[:], r_[:], -ROUND, 1.0, ALU.add, ALU.min))
                    pre(v.tensor_scalar(w[:], r_[:], -1.0, None, ALU.max))
                pre(v.tensor_scalar(b2[:], b2[:], m.tg[0:S, 3:4], None, ALU.mult))
                pre(v.tensor_copy(identb[:], m.ident[:]))
                pre(v.memset(hmax[:], 0.0))
                pre(v.memset(xinv[:], 0.0))
                assert n[0] == NPRE
                with v.Fori(0, NG) as it:
                    xg = lambda j: m.x[:, bass.ds((it * G + j) * D, D)]
                    layernorm_stats(v, xg, stats, mv, ve, G, vec, it * NV, m.carrier)
                    n = [2 * G + 1]

                    def step(ins):
                        ins.then_inc(vec, 1)
                        n[0] += 1

                    def settle():
                        v.wait_ge(vec, PRIMED + it * NV + n[0])
                    v.wait_ge(rstd_ready, PRIMED + it + 1)
                    for j in range(G):
                        step(v.tensor_scalar(xn[:, j, :], xg(j), mv[:, j, 0:1], rstd[:, j:j + 1], ALU.subtract, ALU.mult))
                    settle()

                    def scales(x, big, inv, scale, deq, wcol):
                        step(v.tensor_reduce(big, x, AX.X, ALU.max, apply_absolute_value=True))
                        settle()
                        step(v.tensor_scalar(big, big, EPS, None, ALU.max))
                        settle()
                        step(v.reciprocal(inv, big))
                        step(v.tensor_scalar(deq, big, wmean[0:S, wcol:wcol + 1], None, ALU.mult))
                        settle()
                        step(v.tensor_scalar(scale, inv, 127.0, None, ALU.mult))
                        settle()
                    scales(xn[:], xmax[:], xinv[:], xscale[:], xdeq[:], 0)
                    for j in range(G):
                        ins = v.tensor_scalar(xn[:, j, :], xn[:, j, :], xscale[:, j:j + 1], -128.0, ALU.mult, ALU.max)
                    step(ins)
                    settle()
                    step(v.tensor_scalar(xn[:], xn[:], 127.0, ROUND, ALU.min, ALU.add))
                    settle()
                    step(v.tensor_scalar(xq[:], xn[:], -ROUND, None, ALU.add))
                    v.wait_ge(xt_ps_ready, PRIMED + it + 1)
                    v.tensor_copy(xqt[:].rearrange("p k n -> p (k n)"), t_ps[:, 0, 0:KT * T]).then_inc(xt_ready, 1)
                    for j in range(G):
                        nb = it * G + j
                        v.wait_ge(h_ready, PRIMED + nb + 1)
                        v.scalar_tensor_tensor(h1[:, j, :], h_ps[0:S, j % 2, :], xdeq[:, j:j + 1], b1[:], ALU.mult, ALU.add).then_inc(h1_ready, 1)
                    for j in range(G):
                        nb = it * G + j
                        v.wait_ge(hg_ready, PRIMED + nb + 1)
                        for i in range(2):
                            step(v.bn_stats(hstats[:, j, i, :], hg[:, j, i * 512:(i + 1) * 512]))
                        settle()
                        v.sem_inc(m.carrier, 1)
                        step(v.bn_aggr(hmv[:, j, :], hstats[:, j, :, :].rearrange("p a b -> p (a b)")))
                        settle()
                        step(v.tensor_scalar(hve[:, j:j + 1], hmv[:, j, 1:2], EPS, None, ALU.add))
                    for j in range(G):
                        nb = it * G + j
                        v.wait_ge(hrstd_ready, PRIMED + nb + 1)
                        v.tensor_scalar(h1[:, j, :], hg[:, j, :], hmv[:, j, 0:1], hrstd[:, j:j + 1], ALU.subtract, ALU.mult).then_inc(hn_ready, 1)
                    for j in range(G):
                        nb = it * G + j
                        v.wait_ge(hb_ready, PRIMED + 2 * (nb + 1))
                        scales(h1[:, j, :], hmax[:, j:j + 1], hinv[:, j:j + 1], hscale[:, j:j + 1], hdeq[:, j:j + 1], 1)
                        step(v.tensor_scalar(h1[:, j, :], h1[:, j, :], hscale[:, j:j + 1], -128.0, ALU.mult, ALU.max))
                        settle()
                        v.tensor_scalar(h1[:, j, :], h1[:, j, :], 127.0, ROUND, ALU.min, ALU.add).then_inc(res_ready, 1)
                        v.wait_ge(res_ready, PRIMED + 3 * nb + 1)
                        v.tensor_scalar(hq[:, j, :], h1[:, j, :], -ROUND, None, ALU.add).then_inc(hq_ready, 1)
                        v.tensor_scalar(hdeq[:, j:j + 1], hdeq[:, j:j + 1], m.tg[0:S, 3:4], None, ALU.mult).then_inc(res_ready, 1)
                        v.tensor_tensor(res[:, j, :], xg(j), b2[:], ALU.add).then_inc(res_ready, 1)
                        v.wait_ge(ht_ps_ready, PRIMED + nb + 1)
                        if j >= 2:
                            v.wait_ge(y_ready, PRIMED + nb - 1)
                        v.tensor_copy(hqt[:, j % 2].rearrange("p a b -> p (a b)"), t_ps[:, 1, 0:FT * S]).then_inc(ht_ready, 1)
                    for j in range(G):
                        nb = it * G + j
                        v.wait_ge(y_ready, PRIMED + it * G + 2 * (j // 2) + 2)
                        v.wait_ge(res_ready, PRIMED + 3 * (nb + 1))
                        v.scalar_tensor_tensor(xg(j), y_ps[0:S, j // 2, (j % 2) * D:(j % 2 + 1) * D], hdeq[:, j:j + 1], res[:, j, :],
                                               ALU.mult, ALU.add).then_inc(x_added, 1)
                    assert n[0] == NV, n

            @block.scalar
            def _(a):
                with a.Fori(0, NG) as it:
                    for j in range(G):
                        a.wait_ge(h1_ready, PRIMED + it * G + j + 1)
                        a.activation(hg[:, j, :], h1[:, j, :], ACT.Gelu).then_inc(hg_ready, 1)

            @block.tensor
            def _(pe):
                pe.wait_ge(w_ready, PRIMED + 3)
                pe.matmul(h_ps[:, 0, 0:2], ones[:], wabs[:], start=True, stop=True).then_inc(w_sum, 1)
                pe.wait_ge(w_ready, PRIMED + NPRE)
                with pe.Fori(0, NG) as it:
                    pe.wait_ge(vec, PRIMED + it * NV + 2 * G + 1 + G + 5 + 3)
                    for k in range(KT):
                        for j in range(G):
                            mm = pe.transpose(t_ps[:, 0, (k * G + j) * S:(k * G + j + 1) * S], xq[:, j, k * 128:(k + 1) * 128], identb[0:S, 0:S])
                    mm.then_inc(xt_ps_ready, 1)
                    pe.wait_ge(xt_ready, PRIMED + it + 1)
                    for j in range(G):
                        if j >= 2:
                            pe.wait_ge(h1_ready, PRIMED + it * G + j - 1)
                        for i in range(2):
                            for k in range(KT):
                                mm = pe.matmul(h_ps[0:S, j % 2, i * 512:(i + 1) * 512], xqt[:, k, j * S:(j + 1) * S], w1[:, k, i * 512:(i + 1) * 512],
                                               start=(k == 0), stop=(k == KT - 1))
                        mm.then_inc(h_ready, 1)
                    for j in range(G):
                        nb = it * G + j
                        pe.wait_ge(hq_ready, PRIMED + nb + 1)
                        if j == 0:
                            pe.wait_ge(x_added, PRIMED + it * G)
                        for f in range(FT):
                            mm = pe.transpose(t_ps[:, 1, f * S:(f + 1) * S], hq[:, j, f * 128:(f + 1) * 128], identb[0:S, 0:S])
                        mm.then_inc(ht_ps_ready, 1)
                        pe.wait_ge(ht_ready, PRIMED + nb + 1)
                        for f in range(FT):
                            mm = pe.matmul(y_ps[0:S, j // 2, (j % 2) * D:(j % 2 + 1) * D], hqt[:, j % 2, f, :], w2[:, f, :],
                                           start=(f == 0), stop=(f == FT - 1))
                        mm.then_inc(y_ready, 1)


class Shared:
    pass


STOP = 5


def build(nc, io):
    with ExitStack() as outer:
        sb = lambda n, s, d=F32: outer.enter_context(nc.sbuf_tensor(n, s, d))
        sem = lambda n: outer.enter_context(nc.semaphore(n))
        m = Shared()
        m.x = sb("x_rows", [S, B * D])
        m.ident, m.identr = sb("ident", [128, 128]), sb("identr", [128, 128], F32R)
        m.gates, m.tg = sb("gates", [128, 4]), sb("tanh_gates", [128, 4])
        m.mhalf = sb("minus_half", [128, G])
        m.carrier = sem("wait_carrier")
        phase_load(nc, outer, sem, io, m)
        if STOP >= 1:
            phase_l0_attention(nc, outer, sem, io, m)
        if STOP >= 2:
            phase_moe(nc, outer, sem, io, m)
        if STOP >= 3:
            with ExitStack() as l1:
                sl = lambda n, s, d=F32: l1.enter_context(nc.sbuf_tensor(n, s, d))
                m.a = [sl(f"l1_a{i}", [128, KT, H, CQ], F32R) for i in range(2)]
                m.mqk = sl("l1_mqk", [HALF, 2, H, DL])
                m.cvo = sl("l1_cvo", [128, H // 2, D])
                phase_l1_weights(nc, outer, sem, io, m)
                phase_l1_attention(nc, outer, sem, io, m)
        if STOP >= 4:
            phase_l1_ffn(nc, outer, sem, io, m)
        else:
            done = sem("debug_done")
            with nc.Block() as block:
                @block.sync
                def _(sp):
                    sp.dma_start(io["out"].rearrange("b s d -> s b d"), m.x[:].rearrange("s (b d) -> s b d", b=B)).then_inc(done, 16)
                    sp.wait_ge(done, 16)


def rope_tables(length, dim):
    import numpy as np
    f32 = np.float32
    inv = f32(1.0) / np.power(f32(10000.0), np.arange(0, dim, 2, dtype=f32) / f32(dim)).astype(f32)
    f = np.arange(length, dtype=f32)[:, None] * inv[None, :].astype(f32)
    return np.repeat(np.sin(f), 2, axis=-1).astype(f32), np.repeat(np.cos(f), 2, axis=-1).astype(f32)


def constants():
    import numpy as np
    c = {}
    c["ident"] = np.eye(128, dtype=np.float32)
    q, k = np.arange(S)[:, None], np.arange(S)[None, :]
    c["causal"] = np.where(k <= q, 0.0, -1e30).astype(np.float32)
    c["headsel"] = (np.arange(128)[:, None] // HD == np.arange(8)[None, :]).astype(np.float32)
    row_expert = np.arange(E * I) // I
    rows = np.zeros((40, E * I), np.float32)
    for e in range(E):
        rows[e] = rows[32 + e] = row_expert == e
    c["expert_rows"] = rows
    c["iota8"] = np.arange(E, dtype=np.float32)
    sin, cos = rope_tables(S, CQ)
    c["qcos"] = np.ascontiguousarray(np.stack([cos[:, :HALF].T, cos[:, HALF:].T], 1))
    c["qsin"] = np.ascontiguousarray(np.stack([sin[:, HALF:].T, -sin[:, :HALF].T], 1))
    sin, cos = rope_tables(LK, DL)
    p, r = np.arange(KP)[:, None], np.arange(NT)[None, :]
    key = NT * p + r
    key = np.where(key < LK, key, key - NT)
    hd = DL // 2
    c["kcos"] = np.ascontiguousarray(cos[key])
    c["ksin"] = np.ascontiguousarray(np.concatenate([sin[key][..., hd:], -sin[key][..., :hd]], -1))
    return c


def kernel(**inputs):
    import numpy as np
    import concourse.bacc as _bacc
    from concourse.bass_utils import run_bass_kernel_spmd as _run

    a = inputs
    t = lambda w: np.ascontiguousarray(np.transpose(w))
    lay = {n: np.ascontiguousarray(a[n]) for n in (
        "x", "ctx_512", "g_xattn", "g_ffn", "L1_xattn_Wq", "L1_xattn_w_kc_q", "L1_xattn_w_kc_kv",
        "L1_ffn_b1", "L1_ffn_gamma", "L1_ffn_beta", "L1_ffn_b2")}
    lay["L0_WqT"] = t(a["L0_xattn_Wq"])
    lay["L0_WkvT"] = t(a["L0_xattn_Wkv_expand"])
    lay["L0_WoutT"] = t(a["L0_xattn_Wout"])
    lay["L0_routerT"] = t(a["L0_ffn_router_w"])
    lay["L0_gateT"] = t(np.reshape(a["L0_ffn_w_gate"], (E * I, D)))
    lay["L0_upT"] = t(np.reshape(a["L0_ffn_w_up"], (E * I, D)))
    lay["L0_downT"] = np.ascontiguousarray(np.reshape(np.transpose(a["L0_ffn_w_down"], (0, 2, 1)), (E * I, D)))
    lay["L1_qrT"] = np.ascontiguousarray(np.transpose(a["L1_xattn_W_qr"], (2, 0, 1)))
    lay["L1_krT"] = np.ascontiguousarray(np.transpose(a["L1_xattn_W_kr"], (2, 0, 1)))
    lay["L1_WoT"] = t(a["L1_xattn_Wo"])
    lay["L1_w1T"] = t(a["L1_ffn_w1"])
    lay["L1_w2T"] = t(a["L1_ffn_w2"])
    lay.update(constants())

    nc = _bacc.Bacc("TRN2", target_bir_lowering=False, num_devices=1)
    arrays, io = {}, {}
    for n, v in lay.items():
        arrays[f"in_{n}"] = v
        io[n] = nc.dram_tensor(f"in_{n}", v.shape, F32, kind="ExternalInput").ap()
    io["out"] = nc.dram_tensor("out_rows", (B, S, D), F32, kind="ExternalOutput").ap()
    build(nc, io)
    r = _run(nc, [arrays], core_ids=[0])
    return r.results[0]["out_rows"]
```

```python
from contextlib import ExitStack

import concourse.bass as bass
from concourse import mybir

F32 = mybir.dt.float32
F32R = mybir.dt.float32r
BF16 = mybir.dt.bfloat16
U32 = mybir.dt.uint32
ALU = mybir.AluOpType
ACT = mybir.ActivationFunctionType
AX = mybir.AxisListType

B, S, D = 32, 100, 256
LK, DL = 1444, 64
G = 4
NG = B // G
T = G * S
KT = D // 128
H = 16
HD = D // H
E, I = 8, 176
RAW = E * I * KT
IT = E * I // 128
HK, CQ, R = 128, 192, 64
HALF = CQ // 2
NT = 12
KP = 121
CH = 2
CQS = H * S // CH
QT = [128] * 6 + [32]
F = 1024
EPS = 1e-5
PRIMED = 1
ROUND = 12582912.0


def keys_of(r):
    return KP if r < 4 else KP - 1


def layernorm_stats(v, x, stats, mv, ve, n, done, at, carrier):
    for j in range(n):
        v.bn_stats(stats[:, j, :], x(j)).then_inc(done, 1)
    v.wait_ge(done, PRIMED + at + n)
    v.sem_inc(carrier, 1)
    for j in range(n):
        v.bn_aggr(mv[:, j, :], stats[:, j, :]).then_inc(done, 1)
    v.wait_ge(done, PRIMED + at + 2 * n)
    v.tensor_scalar(ve[:, 0:n], mv[:, 0:n, 1], EPS, None, ALU.add).then_inc(done, 1)


def phase_load(nc, ctx, sem, io, m):
    loaded, gates = sem("inputs_loaded"), sem("gates_ready")
    with nc.Block() as block:
        @block.sync
        def _(sp):
            sp.dma_start(m.ident[:], io["ident"]).then_inc(loaded, 16)
            sp.dma_start(m.gates[:, 0:2], io["g_xattn"].partition_broadcast(128)).then_inc(loaded, 16)
            sp.dma_start(m.gates[:, 2:4], io["g_ffn"].partition_broadcast(128)).then_inc(loaded, 16)
            sp.wait_ge(loaded, 16 * 3)

        @block.scalar
        def _(a):
            a.wait_ge(loaded, 16 * 3)
            a.activation(m.tg[:], m.gates[:], ACT.Tanh).then_inc(gates, 1)

        @block.vector
        def _(v):
            v.memset(m.mhalf[:], -0.5).then_inc(gates, 1)
            v.wait_ge(loaded, 16 * 3)
            v.tensor_copy(m.identr[:], m.ident[:]).then_inc(gates, 1)


def phase_l0_attention(nc, outer, sem, io, m):
    NQ = 4
    counters = []
    with ExitStack() as ctx:
        sb = lambda n, s, d=F32: ctx.enter_context(nc.sbuf_tensor(n, s, d))
        ps = lambda n, s, d=F32: ctx.enter_context(nc.psum_tensor(n, s, d))

        def count(name):
            counters.append(sem(name))
            return counters[-1]
        wq_raw, wo, wk_raw, wv_raw = m.cvo[:, 0:KT, :], m.cvo[:, KT:2 * KT, :], m.cvo[0:DL, 2 * KT, :], m.cvo[0:DL, 2 * KT + 1, :]
        wq = [sb(f"a_wq{i}", [128, KT, D], F32R) for i in range(2)]
        wk = [sb(f"a_wk{i}", [DL, D], F32R) for i in range(2)]
        wv = [sb(f"a_wv{i}", [DL, D], F32R) for i in range(2)]
        lat = sb("a_lat", [S, B * DL])
        mask_raw = sb("a_mask_raw", [S, S])
        mask = sb("a_mask", [S, 4, S], BF16)
        identb = sb("a_identb", [128, 128], BF16)
        headsel_raw, headsel = sb("a_headsel_raw", [128, 8]), sb("a_headsel", [128, 8, S])
        latg = sb("a_latg", [S, G + 1, DL])
        stats, mv, ve, rstd = sb("a_stats", [S, G, 6]), sb("a_mv", [S, G, 2]), sb("a_ve", [S, G]), sb("a_rstd", [S, G])
        xn = sb("a_xn", [S, G, D])
        xt = [sb(f"a_xt{i}", [128, KT, T], F32R) for i in range(2)]
        latt = [sb(f"a_latt{i}", [DL, T], F32R) for i in range(2)]
        qt = sb("a_qt", [128, KT, T])
        kt = sb("a_kt", [128, KT, T])
        kbd = [sb(f"a_kbd{i}", [128, KT, 8, S]) for i in range(2)]
        va = sb("a_va", [S, G, H, HD + 1])
        mx = sb("a_mx", [S, NQ, 4])
        diff = sb("a_diff", [S, NQ, 4, S])
        prob = sb("a_prob", [S, NQ, 4, S])
        pt = sb("a_pt", [S, 2, 4, S])
        rden = sb("a_rden", [S, H])
        cn = sb("a_cn", [S, D])
        ct = sb("a_ct", [128, KT, S])
        s_ps = ps("a_s_ps", [128, 4, 512])
        p_ps = ps("a_p_ps", [128, 2, 512])
        o_ps = ps("a_o_ps", [128, 512])
        f_ps = ps("a_f_ps", [128, 512])
        w_loaded, w_ready = sem("a_w_loaded"), count("a_w_ready")
        x_first, x_rest, moe_split = sem("a_x_first"), sem("a_x_rest"), count("a_moe_split")
        ln, rstd_ready, xn_ready = count("a_ln"), count("a_rstd_ready"), count("a_xn_ready")
        dense_mm, dense_out = count("a_dense_mm"), count("a_dense_out")
        kbd_ready, split_hi, latg_ready = count("a_kbd_ready"), count("a_split_hi"), count("a_latg_ready")
        s_ready, max_ready, diff_ready = count("a_s_ready"), count("a_max_ready"), count("a_diff_ready")
        prob_ready, pt_ready, pt_copied, pv_done = count("a_prob_ready"), count("a_pt_ready"), count("a_pt_copied"), count("a_pv_done")
        rden_ready, cn_ready, ct_ready, ct_copied = count("a_rden_ready"), count("a_cn_ready"), count("a_ct_ready"), count("a_ct_copied")
        f_ready, x_added = count("a_f_ready"), count("a_x_added")
        NLOAD = 7
        NW = 11
        BESIDE_MM, BESIDE_OUT = ((0, 1, 2), (3,), (4,), (5, 6)), ((0, 1, 2), (3,), (), (4, 5, 6))
        ND = 9

        with nc.Block() as block:
            @block.sync
            def _(sp):
                for c in counters:
                    sp.sem_inc(c, PRIMED)
                sp.dma_start(wq_raw, io["L0_WqT"].rearrange("(k p) n -> p k n", p=128)).then_inc(w_loaded, 16)
                sp.dma_start(wk_raw, io["L0_WkvT"][:, 0:D]).then_inc(w_loaded, 16)
                sp.dma_start(wv_raw, io["L0_WkvT"][:, D:2 * D]).then_inc(w_loaded, 16)
                sp.dma_start(wo, io["L0_WoutT"].rearrange("(k p) n -> p k n", p=128)).then_inc(w_loaded, 16)
                sp.dma_start(lat[:].rearrange("s (b d) -> s b d", b=B),
                             io["ctx_512"][:, 0:S, :].rearrange("b s d -> s b d")).then_inc(w_loaded, 16)
                sp.dma_start(mask_raw[:], io["causal"]).then_inc(w_loaded, 16)
                sp.dma_start(headsel_raw[:], io["headsel"]).then_inc(w_loaded, 16)
                for c in range(4):
                    sp.dma_start(m.x[:, c * 8 * D:(c + 1) * 8 * D].rearrange("s (b d) -> s b d", b=8),
                                 io["x"][c * 8:(c + 1) * 8].rearrange("b s d -> s b d")).then_inc(x_rest if c else x_first, 16)
                for i, n in enumerate(("L0_gateT", "L0_upT", "L0_downT")):
                    w = io[n].rearrange("(k p) n -> p k n", p=128)
                    sp.dma_start(m.moe_raw[i].rearrange("p (k n) -> p k n", k=w.shape[1]), w).then_inc(m.moe_loaded, 16)
                sp.wait_ge(w_loaded, 16 * NLOAD)
                sp.wait_ge(x_first, 16)
                sp.wait_ge(x_rest, 16 * 3)
                sp.wait_ge(m.moe_loaded, 16 * 3)

            @block.gpsimd
            def _(g):
                g.wait_ge(w_loaded, 16 * NLOAD)
                with g.Fori(0, NG) as it:
                    g.wait_ge(dense_mm, PRIMED + it * ND)
                    g.tensor_copy(latg[:, 0:G, :].rearrange("s j d -> s (j d)"), lat[:, bass.ds(it * G * DL, G * DL)]).then_inc(latg_ready, 1)
                    g.wait_ge(ln, PRIMED + (it + 1) * (2 * G + 1))
                    g.tensor_tensor(rstd[:], ve[:], m.mhalf[0:S, 0:G], ALU.pow).then_inc(rstd_ready, 1)

            @block.vector
            def _(v):
                v.wait_ge(w_loaded, 16 * NLOAD)
                for raw, w in ((wq_raw, wq), (wk_raw, wk), (wv_raw, wv)):
                    v.tensor_copy(w[0][:], raw).then_inc(w_ready, 1)
                v.wait_ge(w_ready, PRIMED + 3)
                for raw, w in ((wq_raw, wq), (wk_raw, wk), (wv_raw, wv)):
                    v.tensor_tensor(w[1][:], raw, w[0][:].bitcast(F32), ALU.subtract).then_inc(w_ready, 1)
                v.tensor_copy(mask[:], mask_raw[:].unsqueeze(1).broadcast_to((S, 4, S))).then_inc(w_ready, 1)
                v.memset(va[:, :, :, HD], 1.0).then_inc(w_ready, 1)
                v.memset(latg[:, G, :], 0.0).then_inc(w_ready, 1)
                v.tensor_copy(identb[:], m.ident[:]).then_inc(w_ready, 1)
                v.tensor_copy(headsel[:], headsel_raw[:].unsqueeze(2).broadcast_to((128, 8, S))).then_inc(w_ready, 1)
                v.wait_ge(w_ready, PRIMED + NW)
                def row_stats(it):
                    xg = lambda j: m.x[:, bass.ds((it * G + j) * D, D)]
                    layernorm_stats(v, xg, stats, mv, ve, G, ln, it * (2 * G + 1), m.carrier)

                def normalise_rows(it):
                    xg = lambda j: m.x[:, bass.ds((it * G + j) * D, D)]
                    v.wait_ge(rstd_ready, PRIMED + it + 1)
                    for j in range(G):
                        v.tensor_scalar(xn[:, j, :], xg(j), mv[:, j, 0:1], rstd[:, j:j + 1],
                                        ALU.subtract, ALU.mult).then_inc(xn_ready, 1)

                def evacuate(it, n):
                    v.wait_ge(dense_mm, PRIMED + it * ND + n + 1)
                    src = s_ps[:, n % 4, 0:T]
                    if n < 3:
                        hi, lo = (xt[0][:, n, :], xt[1][:, n, :]) if n < 2 else (latt[0][:], latt[1][:])
                        src = src if n < 2 else s_ps[0:DL, 2, 0:T]
                        v.tensor_copy(hi, src).then_inc(split_hi, 1)
                        v.wait_ge(split_hi, PRIMED + it * 3 + n + 1)
                        v.tensor_tensor(lo, src, hi.bitcast(F32), ALU.subtract).then_inc(dense_out, 1)
                    elif n < 5:
                        v.tensor_copy(qt[:, n - 3, :], src).then_inc(dense_out, 1)
                    elif n < 7:
                        v.tensor_copy(kt[:, n - 5, :], src).then_inc(dense_out, 1)
                    else:
                        for j in range(2):
                            ins = v.tensor_copy(va[:, 2 * (n - 7) + j, :, 0:HD],
                                                s_ps[0:S, n % 4, j * D:(j + 1) * D].rearrange("p (h d) -> p h d", h=H))
                        ins.then_inc(dense_out, 1)

                def block_keys(it, b):
                    if b >= 2:
                        v.wait_ge(s_ready, PRIMED + (it * G + b - 1) * NQ)
                    for k in range(KT):
                        ins = v.tensor_tensor(kbd[b % 2][:, k], headsel[:],
                                              kt[:, k, b * S:(b + 1) * S].unsqueeze(1).broadcast_to((128, 8, S)),
                                              ALU.mult)
                    ins.then_inc(kbd_ready, 1)

                def group(it, more):
                    xg = lambda j: m.x[:, bass.ds((it * G + j) * D, D)]

                    def differences(b, q):
                        n = it * G * NQ + b * NQ + q
                        v.wait_ge(s_ready, PRIMED + n + 1)
                        sc = s_ps[0:S, q, 0:4 * S].rearrange("p (h k) -> p h k", h=4)
                        v.tensor_reduce(mx[:, q, :], sc, AX.X, ALU.max).then_inc(max_ready, 1)
                        v.wait_ge(max_ready, PRIMED + n + 1)
                        if b > 0:
                            v.wait_ge(prob_ready, PRIMED + n - NQ + 1)
                        v.tensor_tensor(diff[:, q], sc, mx[:, q, :].unsqueeze(2).broadcast_to((S, 4, S)),
                                        ALU.subtract).then_inc(diff_ready, 1)

                    def normalise(b):
                        nb = it * G + b
                        v.wait_ge(pv_done, PRIMED + (nb + 1) * NQ)
                        o = o_ps[0:S, 0:H * (HD + 1)].rearrange("p (h d) -> p h d", h=H)
                        v.reciprocal(rden[:], o[:, :, HD]).then_inc(rden_ready, 1)
                        v.wait_ge(rden_ready, PRIMED + nb + 1)
                        v.tensor_tensor(cn[:].rearrange("p (h d) -> p h d", h=H), o[:, :, 0:HD],
                                        rden[:].unsqueeze(2).broadcast_to((S, H, HD)), ALU.mult).then_inc(cn_ready, 1)

                    def add_x(b):
                        v.wait_ge(f_ready, PRIMED + it * G + b + 1)
                        v.scalar_tensor_tensor(xg(b), f_ps[0:S, 0:D], m.tg[0:S, 0:1], xg(b), ALU.mult, ALU.add).then_inc(x_added, 1)
                    block_keys(it, 1)
                    for q in range(NQ):
                        differences(0, q)
                    for b in range(G):
                        for q in range(NQ):
                            if b + 1 < G:
                                differences(b + 1, q)
                            if b == G - 1 and more:
                                for k in BESIDE_OUT[q]:
                                    evacuate(it + 1, k)
                            if q == 1 and b + 2 < G:
                                block_keys(it, b + 2)
                            if q == 2 and b > 0:
                                add_x(b - 1)
                            if q == 0 and b == 1 and more:
                                row_stats(it + 1)
                            if q == 0 and b == 2 and more:
                                normalise_rows(it + 1)
                        if b == G - 1 and more:
                            v.wait_ge(dense_out, PRIMED + (it + 1) * ND + 7)
                            block_keys(it + 1, 0)
                        elif b == G - 1:
                            split_moe()
                        normalise(b)
                    if more:
                        for k in range(7, ND):
                            evacuate(it + 1, k)
                    add_x(G - 1)
                    v.wait_ge(x_added, PRIMED + (it + 1) * G)

                def split_moe():
                    v.wait_ge(m.moe_loaded, 16 * 3)
                    for i, w in enumerate((m.wg, m.wu)):
                        raw = m.moe_raw[i].rearrange("p (k n) -> p k n", k=KT)
                        v.tensor_copy(w[0], raw).then_inc(moe_split, 1)
                        v.wait_ge(moe_split, PRIMED + 2 * i + 1)
                        v.tensor_tensor(w[1], raw, w[0].bitcast(F32), ALU.subtract).then_inc(moe_split, 1)

                v.wait_ge(x_first, 16)
                row_stats(0)
                normalise_rows(0)
                for k in range(ND):
                    evacuate(0, k)
                v.wait_ge(dense_out, PRIMED + 7)
                block_keys(0, 0)
                v.wait_ge(x_rest, 16 * 3)
                with v.Fori(0, NG - 1) as it:
                    group(it, True)
                group(NG - 1, False)

            @block.scalar
            def _(a):
                with a.Fori(0, NG) as it:
                    def copy_ct(b):
                        a.wait_ge(ct_ready, PRIMED + it * G + b + 1)
                        a.activation(ct[:], f_ps[:, 256:256 + KT * S].rearrange("p (k s) -> p k s", k=KT), ACT.Copy).then_inc(ct_copied, 1)
                    for b in range(G):
                        def copy_pt(q):
                            n = it * G * NQ + b * NQ + q
                            a.wait_ge(pt_ready, PRIMED + n + 1)
                            if b * NQ + q >= 2:
                                a.wait_ge(pv_done, PRIMED + n - 1)
                            a.activation(pt[:, q % 2], p_ps[0:S, q % 2, 0:4 * S].rearrange("p (h k) -> p h k", h=4),
                                         ACT.Copy).then_inc(pt_copied, 1)
                        for q in range(NQ):
                            n = it * G * NQ + b * NQ + q
                            a.wait_ge(diff_ready, PRIMED + n + 1)
                            if b > 0:
                                a.wait_ge(pt_ready, PRIMED + n - NQ + 1)
                            a.activation(prob[:, q], diff[:, q], ACT.Exp, scale=HD ** -0.5).then_inc(prob_ready, 1)
                            if q > 0:
                                copy_pt(q - 1)
                            if q == 1 and b > 0:
                                copy_ct(b - 1)
                        copy_pt(NQ - 1)
                    copy_ct(G - 1)

            @block.tensor
            def _(pe):
                pe.wait_ge(w_ready, PRIMED + NW)
                parts = ((0, 0), (0, 1), (1, 0))

                def dense(it, n):
                    if n < 4:
                        pe.wait_ge(diff_ready, PRIMED + it * G * NQ)
                    else:
                        pe.wait_ge(dense_out, PRIMED + it * ND + n - 3)
                    o = s_ps[:, n % 4, 0:T]
                    if n < 2:
                        if n == 0:
                            pe.wait_ge(xn_ready, PRIMED + (it + 1) * G)
                        for j in range(G):
                            mm = pe.transpose(o[:, j * S:(j + 1) * S], xn[:, j, n * 128:(n + 1) * 128], m.ident[0:S, 0:S])
                    elif n == 2:
                        pe.wait_ge(latg_ready, PRIMED + it + 1)
                        for j in range(G):
                            mm = pe.transpose(o[:, j * S:(j + 1) * S], latg[:, j:j + 2, :], m.ident[0:S, 0:S])
                    elif n < 5:
                        pe.wait_ge(dense_out, PRIMED + it * ND + 2)
                        for i, (w, x) in enumerate(parts):
                            for k in range(KT):
                                mm = pe.matmul(o, wq[w][:, k, (n - 3) * 128:(n - 2) * 128], xt[x][:, k, :],
                                               start=(i == 0 and k == 0), stop=(i == 2 and k == KT - 1))
                    elif n < 7:
                        pe.wait_ge(dense_out, PRIMED + it * ND + 3)
                        for i, (w, x) in enumerate(parts):
                            mm = pe.matmul(o, wk[w][:, (n - 5) * 128:(n - 4) * 128], latt[x][:], start=(i == 0), stop=(i == 2))
                    else:
                        for j in range(2):
                            cols = slice((2 * (n - 7) + j) * S, (2 * (n - 7) + j + 1) * S)
                            for i, (w, x) in enumerate(parts):
                                mm = pe.matmul(s_ps[0:S, n % 4, j * D:(j + 1) * D], latt[x][:, cols], wv[w][:],
                                               start=(i == 0), stop=(i == 2))
                    mm.then_inc(dense_mm, 1)

                def group(it, more):
                    def scores(b, q):
                        n = it * G * NQ + b * NQ + q
                        pe.wait_ge(kbd_ready, PRIMED + it * G + b + 1)
                        pe.wait_ge(diff_ready, PRIMED + n - NQ + 1 if b > 0 else it * G * NQ)
                        o = s_ps[0:S, q, 0:4 * S]
                        pe.matmul(o, identb[0:S, 0:S], mask[:].rearrange("p h k -> p (h k)"), start=True, stop=False)
                        mm = pe.matmul(o, qt[:, q // 2, b * S:(b + 1) * S],
                                       kbd[b % 2][:, q // 2, 4 * (q % 2):4 * (q % 2) + 4, :].rearrange("p h k -> p (h k)"),
                                       start=False, stop=True)
                        mm.then_inc(s_ready, 1)

                    def turn_out(b):
                        nb = it * G + b
                        pe.wait_ge(cn_ready, PRIMED + nb + 1)
                        pe.wait_ge(x_added, PRIMED + nb)
                        for k in range(KT):
                            mm = pe.transpose(f_ps[:, 256 + k * S:256 + (k + 1) * S], cn[:, k * 128:(k + 1) * 128], m.ident[0:S, 0:S])
                        mm.then_inc(ct_ready, 1)

                    def project_out(b):
                        pe.wait_ge(ct_copied, PRIMED + it * G + b + 1)
                        for k in range(KT):
                            mm = pe.matmul(f_ps[0:S, 0:D], ct[:, k, :], wo[:, k, :], start=(k == 0), stop=(k == KT - 1))
                        mm.then_inc(f_ready, 1)
                    pe.wait_ge(dense_out, PRIMED + (it + 1) * ND)
                    for q in range(NQ):
                        scores(0, q)
                    for b in range(G):
                        nb = it * G + b

                        def probs_value(q):
                            n = nb * NQ + q
                            pe.wait_ge(pt_copied, PRIMED + n + 1)
                            if q == 0:
                                pe.wait_ge(cn_ready, PRIMED + nb)
                            for h in range(4):
                                mm = pe.matmul(o_ps[0:S, (4 * q + h) * (HD + 1):(4 * q + h + 1) * (HD + 1)],
                                               pt[:, q % 2, h, :], va[:, b, 4 * q + h, :], start=True, stop=True)
                            mm.then_inc(pv_done, 1)
                        for q in range(NQ):
                            n = nb * NQ + q
                            if b + 1 < G:
                                scores(b + 1, q)
                            pe.wait_ge(prob_ready, PRIMED + n + 1)
                            if b * NQ + q >= 2:
                                pe.wait_ge(pt_copied, PRIMED + n - 1)
                            for h in range(4):
                                mm = pe.transpose(p_ps[0:S, q % 2, h * S:(h + 1) * S], prob[:, q, h, :], m.ident[0:S, 0:S])
                            mm.then_inc(pt_ready, 1)
                            if q == 0 and b > 0:
                                turn_out(b - 1)
                            if q == 2 and b > 0:
                                project_out(b - 1)
                            if b == G - 1 and more:
                                for k in BESIDE_MM[q]:
                                    dense(it + 1, k)
                            if q > 0:
                                probs_value(q - 1)
                        probs_value(NQ - 1)
                    if more:
                        for k in range(7, ND):
                            dense(it + 1, k)
                    turn_out(G - 1)
                    project_out(G - 1)

                for k in range(ND):
                    dense(0, k)
                with pe.Fori(0, NG - 1) as it:
                    group(it, True)
                group(NG - 1, False)


def phase_moe(nc, outer, sem, io, m):
    counters = []
    with ExitStack() as ctx:
        sb = lambda n, s, d=F32: ctx.enter_context(nc.sbuf_tensor(n, s, d))
        ps = lambda n, s, d=F32: ctx.enter_context(nc.psum_tensor(n, s, d))

        def count(name):
            counters.append(sem(name))
            return counters[-1]
        RING = 4
        wg, wu = m.wg, m.wu
        wd = [sb(f"b_wd{i}", [128, IT, D], F32R) for i in range(2)]
        wd_raw = m.moe_raw[2].rearrange("p (t n) -> p t n", t=IT)
        wr_raw = sb("b_wr_raw", [128, KT, E])
        wr = [sb(f"b_wr{i}", [128, KT, E], F32R) for i in range(2)]
        expert_raw = m.cvo[0:40].rearrange("p a n -> p (a n)")[:, 0:E * I].rearrange("p (t n) -> p t n", t=IT)
        expert = sb("b_expert", [40, IT, 128], F32R)
        iota8 = sb("b_iota8", [S, E])
        stats, mv, ve, rstd = sb("b_stats", [S, G, 6]), sb("b_mv", [S, G, 2]), sb("b_ve", [S, G]), sb("b_rstd", [S, G])
        xn = sb("b_xn", [S, G, D])
        xt = [sb(f"b_xt{i}", [128, KT, T], F32R) for i in range(2)]
        rmax, rdiff, rexp, rsum, rinv = (sb("b_rmax", [S, G]), sb("b_rdiff", [S, G, E]), sb("b_rexp", [S, G, E]),
                                         sb("b_rsum", [S, G]), sb("b_rinv", [S, G]))
        rprob, top, topi, topf = sb("b_rprob", [S, G, E]), sb("b_top", [S, G, 8]), sb("b_topi", [S, G, 8], U32), sb("b_topf", [S, G, 2])
        wsum, winv, wtop = sb("b_wsum", [S, G]), sb("b_winv", [S, G]), sb("b_wtop", [S, G, 2])
        comb1, comb2, comb = sb("b_comb1", [S, G, E]), sb("b_comb2", [S, G, E]), sb("b_comb", [S, G, E])
        combt = sb("b_combt", [40, T], F32R)
        silu = sb("b_silu", [128, 2, T])
        gated = sb("b_gated", [128, RING, T])
        act = sb("b_act", [128, RING, T])
        act_hi, act_lo = sb("b_act_hi", [128, RING, T], F32R), sb("b_act_lo", [128, RING, T], F32R)
        gu_ps = ps("b_gu_ps", [128, 2, 3, 512])
        y_ps = ps("b_y_ps", [128, 2, 512])
        w_loaded, w_ready = sem("b_w_loaded"), count("b_w_ready")
        ln, rstd_ready, xn_ready = count("b_ln"), count("b_rstd_ready"), count("b_xn_ready")
        xt_ps_ready, split_hi, xt_ready = count("b_xt_ps_ready"), count("b_split_hi"), count("b_xt_ready")
        logits_ready, router, rexp_ready = count("b_logits_ready"), count("b_router"), count("b_rexp_ready")
        combt_ps_ready, combt_hi, combt_ready = count("b_combt_ps_ready"), count("b_combt_hi"), count("b_combt_ready")
        gate_ready, up_ready, spread_ready = count("b_gate_ready"), count("b_up_ready"), count("b_spread_ready")
        silu_ready, gated_ready, act_ready, down_done = count("b_silu_ready"), count("b_gated_ready"), count("b_act_ready"), count("b_down_done")
        wd_hi_ready, wd_lo_ready = count("b_wd_hi_ready"), count("b_wd_lo_ready")
        hi_ready, lo_ready = count("b_hi_ready"), count("b_lo_ready")
        x_added = count("b_x_added")
        NW = 4
        NR = 11 + 4 * G
        LN_AT = 4

        with nc.Block() as block:
            @block.sync
            def _(sp):
                for c in counters:
                    sp.sem_inc(c, PRIMED)
                sp.dma_start(wr_raw[:], io["L0_routerT"].rearrange("(k p) n -> p k n", p=128)).then_inc(w_loaded, 16)
                sp.dma_start(expert_raw.rearrange("p t n -> p (t n)"), io["expert_rows"]).then_inc(w_loaded, 16)
                sp.dma_start(iota8[:], io["iota8"].partition_broadcast(S)).then_inc(w_loaded, 16)
                sp.wait_ge(w_loaded, 16 * 3)
                sp.wait_ge(wd_lo_ready, PRIMED + 1)
                sp.dma_start(m.wq, io["L1_xattn_Wq"].rearrange("(h k) d -> k h d", k=HK)).then_inc(m.l1_loaded, 16)
                sp.dma_start(m.kcq, io["L1_xattn_w_kc_q"].rearrange("h k q -> k h q")).then_inc(m.l1_loaded, 16)

            @block.gpsimd
            def _(g):
                def deviation(it):
                    g.wait_ge(ln, PRIMED + (it + 1) * (2 * G + 1))
                    g.tensor_tensor(rstd[:], ve[:], m.mhalf[0:S, 0:G], ALU.pow).then_inc(rstd_ready, 1)

                def group(it, more):
                    for t in range(IT):
                        g.wait_ge(hi_ready, PRIMED + it * IT + t + 1)
                        g.tensor_tensor(act_lo[:, t % RING, :], act[:, t % RING, :], act_hi[:, t % RING, :].bitcast(F32),
                                        ALU.subtract).then_inc(lo_ready, 1)
                        if t == LN_AT and more:
                            deviation(it + 1)
                deviation(0)
                g.wait_ge(wd_hi_ready, PRIMED + 1)
                g.tensor_tensor(wd[1][:], wd_raw, wd[0][:].bitcast(F32), ALU.subtract).then_inc(wd_lo_ready, 1)
                with g.Fori(0, NG - 1) as it:
                    group(it, True)
                group(NG - 1, False)

            @block.vector
            def _(v):
                def normalise_rows(it):
                    xg = lambda j: m.x[:, bass.ds((it * G + j) * D, D)]
                    layernorm_stats(v, xg, stats, mv, ve, G, ln, it * (2 * G + 1), m.carrier)
                    v.wait_ge(rstd_ready, PRIMED + it + 1)
                    for j in range(G):
                        v.tensor_scalar(xn[:, j, :], xg(j), mv[:, j, 0:1], rstd[:, j:j + 1],
                                        ALU.subtract, ALU.mult).then_inc(xn_ready, 1)

                def split_rows(it):
                    for k in range(KT):
                        v.wait_ge(xt_ps_ready, PRIMED + it * KT + k + 1)
                        v.tensor_copy(xt[0][:, k, :], gu_ps[:, 1, k, 0:T]).then_inc(split_hi, 1)
                        v.wait_ge(split_hi, PRIMED + it * KT + k + 1)
                        v.tensor_tensor(xt[1][:, k, :], gu_ps[:, 1, k, 0:T], xt[0][:, k, :].bitcast(F32),
                                        ALU.subtract).then_inc(xt_ready, 1)

                def group(it, more):
                    def gate(t):
                        i = it * IT + t
                        v.wait_ge(silu_ready, PRIMED + i + 1)
                        v.wait_ge(up_ready, PRIMED + i + 1)
                        v.tensor_tensor(gated[:, t % RING, :], silu[:, t % 2, :], gu_ps[:, t % 2, 1, 0:T], ALU.mult).then_inc(gated_ready, 1)

                    def weigh(t):
                        i = it * IT + t
                        v.wait_ge(gated_ready, PRIMED + i + 1)
                        v.wait_ge(spread_ready, PRIMED + i + 1)
                        if t >= RING:
                            v.wait_ge(lo_ready, PRIMED + i - RING + 1)
                        v.tensor_tensor(act[:, t % RING, :], gated[:, t % RING, :], gu_ps[:, t % 2, 2, 0:T], ALU.mult).then_inc(act_ready, 1)
                    n = [0]

                    def step(ins):
                        ins.then_inc(router, 1)
                        n[0] += 1

                    def settle():
                        v.wait_ge(router, PRIMED + it * NR + n[0])
                    v.wait_ge(logits_ready, PRIMED + it + 1)
                    logits = gu_ps[0:S, 1, 2, 0:G * E].rearrange("p (b e) -> p b e", b=G)
                    over = lambda a: a.unsqueeze(2).broadcast_to((S, G, E))
                    step(v.tensor_reduce(rmax[:], logits, AX.X, ALU.max))
                    settle()
                    step(v.tensor_tensor(rdiff[:], logits, over(rmax[:]), ALU.subtract))
                    v.wait_ge(rexp_ready, PRIMED + it + 1)
                    step(v.tensor_reduce(rsum[:], rexp[:], AX.X, ALU.add))
                    settle()
                    step(v.reciprocal(rinv[:], rsum[:]))
                    settle()
                    step(v.tensor_tensor(rprob[:], rexp[:], over(rinv[:]), ALU.mult))
                    settle()
                    v.sem_inc(m.carrier, 1)
                    for b in range(G):
                        step(v.max(top[:, b, :], rprob[:, b, :]))
                    settle()
                    v.sem_inc(m.carrier, 1)
                    for b in range(G):
                        step(v.max_index(topi[:, b, :], top[:, b, :], rprob[:, b, :]))
                    gate(0)
                    step(v.tensor_tensor(wsum[:], top[:, :, 0], top[:, :, 1], ALU.add))
                    settle()
                    step(v.tensor_copy(topf[:], topi[:, :, 0:2]))
                    step(v.tensor_scalar(wsum[:], wsum[:], 1e-20, None, ALU.add))
                    settle()
                    step(v.reciprocal(winv[:], wsum[:]))
                    settle()
                    step(v.tensor_tensor(wtop[:], top[:, :, 0:2], winv[:].unsqueeze(2).broadcast_to((S, G, 2)), ALU.mult))
                    settle()
                    for b in range(G):
                        step(v.tensor_scalar(comb1[:, b, :], iota8[:], topf[:, b, 0:1], wtop[:, b, 0:1], ALU.is_equal, ALU.mult))
                        step(v.tensor_scalar(comb2[:, b, :], iota8[:], topf[:, b, 1:2], wtop[:, b, 1:2], ALU.is_equal, ALU.mult))
                    settle()
                    step(v.tensor_tensor(comb[:], comb1[:], comb2[:], ALU.add))
                    assert n[0] == NR
                    gate(1)
                    gate(2)
                    v.wait_ge(combt_ps_ready, PRIMED + it + 1)
                    cps = gu_ps[0:E, 0, 2, 0:T]
                    v.tensor_copy(combt[0:E, :], cps).then_inc(combt_hi, 1)
                    v.wait_ge(combt_hi, PRIMED + it + 1)
                    v.tensor_tensor(combt[32:32 + E, :], cps, combt[0:E, :].bitcast(F32), ALU.subtract).then_inc(combt_ready, 1)
                    gate(3)
                    weigh(0)
                    weigh(1)
                    for t in range(4, IT):
                        gate(t)
                        weigh(t - 2)
                        if t == LN_AT + 2 and more:
                            normalise_rows(it + 1)
                    weigh(IT - 2)
                    if more:
                        split_rows(it + 1)
                    weigh(IT - 1)
                    v.wait_ge(down_done, PRIMED + (it + 1) * IT)
                    for h in range(2):
                        xs = m.x[:, bass.ds((it * G + 2 * h) * D, 2 * D)]
                        v.scalar_tensor_tensor(xs, y_ps[0:S, h, :], m.tg[0:S, 2:3], xs, ALU.mult, ALU.add).then_inc(x_added, 1)
                    v.wait_ge(x_added, PRIMED + (it + 1) * 2)

                normalise_rows(0)
                v.wait_ge(w_loaded, 16 * 3)
                v.tensor_copy(wr[0][:], wr_raw[:]).then_inc(w_ready, 1)
                v.wait_ge(w_ready, PRIMED + 1)
                v.tensor_tensor(wr[1][:], wr_raw[:], wr[0][:].bitcast(F32), ALU.subtract).then_inc(w_ready, 1)
                v.tensor_copy(expert[:], expert_raw).then_inc(w_ready, 1)
                v.memset(combt[:].bitcast(F32), 0.0).then_inc(w_ready, 1)
                v.wait_ge(w_ready, PRIMED + NW)
                split_rows(0)
                with v.Fori(0, NG - 1) as it:
                    group(it, True)
                group(NG - 1, False)

            @block.scalar
            def _(a):
                def group(it):
                    def swish(t):
                        i = it * IT + t
                        a.wait_ge(gate_ready, PRIMED + i + 1)
                        if t >= 2:
                            a.wait_ge(gated_ready, PRIMED + i - 1)
                        a.activation(silu[:, t % 2, :], gu_ps[:, t % 2, 0, 0:T], ACT.Silu).then_inc(silu_ready, 1)

                    def high(t):
                        i = it * IT + t
                        a.wait_ge(act_ready, PRIMED + i + 1)
                        if t >= RING:
                            a.wait_ge(down_done, PRIMED + i - RING + 1)
                        a.activation(act_hi[:, t % RING, :], act[:, t % RING, :], ACT.Copy).then_inc(hi_ready, 1)
                    a.wait_ge(router, PRIMED + it * NR + 2)
                    a.activation(rexp[:], rdiff[:], ACT.Exp).then_inc(rexp_ready, 1)
                    for t in range(4):
                        swish(t)
                    high(0)
                    high(1)
                    for t in range(4, IT):
                        swish(t)
                        high(t - 2)
                    high(IT - 2)
                    high(IT - 1)
                a.activation(wd[0][:], wd_raw, ACT.Copy).then_inc(wd_hi_ready, 1)
                with a.Fori(0, NG) as it:
                    group(it)

            @block.tensor
            def _(pe):
                parts = ((0, 0), (0, 1), (1, 0))

                def turn_rows(it):
                    pe.wait_ge(xn_ready, PRIMED + (it + 1) * G)
                    for k in range(KT):
                        for j in range(G):
                            mm = pe.transpose(gu_ps[:, 1, k, j * S:(j + 1) * S], xn[:, j, k * 128:(k + 1) * 128], m.ident[0:S, 0:S])
                        mm.then_inc(xt_ps_ready, 1)

                def route(it):
                    pe.wait_ge(xt_ready, PRIMED + (it + 1) * KT)
                    for b in range(G):
                        for i, (w, x) in enumerate(parts):
                            for k in range(KT):
                                mm = pe.matmul(gu_ps[0:S, 1, 2, b * E:(b + 1) * E], xt[x][:, k, b * S:(b + 1) * S], wr[w][:, k, :],
                                               start=(i == 0 and k == 0), stop=(i == 2 and k == KT - 1))
                    mm.then_inc(logits_ready, 1)

                def group(it, more):
                    def rows_of(t):
                        n = it * IT + t
                        if t >= 2:
                            pe.wait_ge(gated_ready, PRIMED + n - 1)
                        for j, (w, done) in enumerate(((wg, gate_ready), (wu, up_ready))):
                            for i, (wi, x) in enumerate(parts):
                                for k in range(KT):
                                    mm = pe.matmul(gu_ps[:, t % 2, j, 0:T], w[wi][:, k, t * 128:(t + 1) * 128], xt[x][:, k, :],
                                                   start=(i == 0 and k == 0), stop=(i == 2 and k == KT - 1))
                            mm.then_inc(done, 1)

                    def spread(t):
                        if t >= 2:
                            pe.wait_ge(act_ready, PRIMED + it * IT + t - 1)
                        pe.matmul(gu_ps[:, t % 2, 2, 0:T], expert[:, t, :], combt[:], start=True, stop=True).then_inc(spread_ready, 1)

                    def down(t):
                        n = it * IT + t
                        pe.wait_ge(lo_ready, PRIMED + n + 1)
                        if t == 0:
                            pe.wait_ge(x_added, PRIMED + it * 2)
                        for b in range(G):
                            for i, (w, rows) in enumerate(((0, act_hi), (1, act_hi), (0, act_lo))):
                                mm = pe.matmul(y_ps[0:S, b // 2, (b % 2) * D:(b % 2 + 1) * D], rows[:, t % RING, b * S:(b + 1) * S], wd[w][:, t, :],
                                               start=(t == 0 and b % 2 == 0 and i == 0), stop=(t == IT - 1 and i == 2), skip_group_check=True)
                        mm.then_inc(down_done, 1)
                    for t in range(4):
                        rows_of(t)
                    pe.wait_ge(router, PRIMED + (it + 1) * NR)
                    pe.wait_ge(act_ready, PRIMED + it * IT)
                    for b in range(G):
                        mm = pe.transpose(gu_ps[0:E, 0, 2, b * S:(b + 1) * S], comb[:, b, :], m.ident[0:S, 0:S])
                    mm.then_inc(combt_ps_ready, 1)
                    pe.wait_ge(combt_ready, PRIMED + it + 1)
                    spread(0)
                    spread(1)
                    for t in range(4, IT):
                        rows_of(t)
                        spread(t - 2)
                        down(t - 4)
                    spread(IT - 2)
                    if more:
                        pe.wait_ge(gated_ready, PRIMED + it * IT + IT - 1)
                        turn_rows(it + 1)
                    spread(IT - 1)
                    for t in range(IT - 4, IT):
                        if t == IT - 1 and more:
                            route(it + 1)
                        down(t)

                turn_rows(0)
                pe.wait_ge(w_ready, PRIMED + NW)
                route(0)
                pe.wait_ge(wd_lo_ready, PRIMED + 1)
                with pe.Fori(0, NG - 1) as it:
                    group(it, True)
                group(NG - 1, False)


def phase_l1_weights(nc, outer, sem, io, m):
    with ExitStack() as ctx:
        sb = lambda n, s, d=F32: ctx.enter_context(nc.sbuf_tensor(n, s, d))
        ps = lambda n, s, d=F32: ctx.enter_context(nc.psum_tensor(n, s, d))
        wq, kcq = m.wq, m.kcq
        qr, kr = sb("w_qr", [R, H, CQ]), sb("w_kr", [R, H, DL])
        kckv, wo = sb("w_kckv", [128, H, DL]), sb("w_wo", [128, H, D])
        loaded = sem("w_loaded")
        a_ps = ps("w_a_ps", [128, 4, 512])
        b_ps = ps("w_b_ps", [128, 4, 512])
        a_mm, a_hi, a_out = sem("w_a_mm"), sem("w_a_hi"), sem("w_a_out")
        m_mm, m_out, c_mm, c_out = sem("w_m_mm"), sem("w_m_out"), sem("w_c_mm"), sem("w_c_out")
        with nc.Block() as block:
            @block.sync
            def _(sp):
                sp.dma_start(qr[:], io["L1_qrT"]).then_inc(loaded, 16)
                sp.dma_start(kr[:], io["L1_krT"]).then_inc(loaded, 16)
                sp.dma_start(kckv[:], io["L1_xattn_w_kc_kv"].rearrange("h k d -> k h d")).then_inc(loaded, 16)
                sp.dma_start(wo[:], io["L1_WoT"].rearrange("(h k) o -> k h o", k=HK)).then_inc(loaded, 16)
                sp.wait_ge(loaded, 16 * 4)

            @block.tensor
            def _(pe):
                pe.wait_ge(m.l1_loaded, 16 * 2)
                for h in range(H):
                    if h >= 4:
                        pe.wait_ge(a_out, h - 3)
                    for k in range(KT):
                        mm = pe.matmul(a_ps[:, h % 4, k * CQ:(k + 1) * CQ], wq[:, h, k * 128:(k + 1) * 128], kcq[:, h, :], start=True, stop=True)
                    mm.then_inc(a_mm, 1)
                pe.wait_ge(loaded, 16 * 4)
                for h in range(H):
                    if h >= 2:
                        pe.wait_ge(m_out, h - 1)
                    for i in range(2):
                        mm = pe.matmul(b_ps[0:HALF, h % 2, i * DL:(i + 1) * DL], qr[:, h, i * HALF:(i + 1) * HALF], kr[:, h, :], start=True, stop=True)
                    mm.then_inc(m_mm, 1)
                for hh in range(H // 2):
                    if hh >= 2:
                        pe.wait_ge(c_out, hh - 1)
                    for c in range(2):
                        mm = pe.matmul(b_ps[c * DL:(c + 1) * DL, 2 + hh % 2, 0:D], kckv[:, 2 * hh + c, :], wo[:, 2 * hh + c, :], start=True, stop=True)
                    mm.then_inc(c_mm, 1)

            @block.vector
            def _(v):
                for h in range(H):
                    v.wait_ge(a_mm, h + 1)
                    src = a_ps[:, h % 4, 0:KT * CQ].rearrange("p (k q) -> p k q", k=KT)
                    v.tensor_copy(m.a[0][:, :, h, :], src).then_inc(a_hi, 1)
                    v.wait_ge(a_hi, h + 1)
                    v.tensor_tensor(m.a[1][:, :, h, :], src, m.a[0][:, :, h, :].bitcast(F32), ALU.subtract).then_inc(a_out, 1)

            @block.scalar
            def _(a):
                for h in range(H):
                    a.wait_ge(m_mm, h + 1)
                    src = b_ps[0:HALF, h % 2, 0:2 * DL].rearrange("p (i d) -> p i d", i=2)
                    a.activation(m.mqk[:, :, h, :], src, ACT.Copy).then_inc(m_out, 1)
                for hh in range(H // 2):
                    a.wait_ge(c_mm, hh + 1)
                    a.activation(m.cvo[:, hh, :], b_ps[:, 2 + hh % 2, 0:D], ACT.Copy).then_inc(c_out, 1)


def phase_l1_attention(nc, outer, sem, io, m):
    NQT = len(QT)
    HEADS = [2 * i for i in range(H // 2)] + [2 * i + 1 for i in range(H // 2)]
    with ExitStack() as ctx:
        counters = []
        sb = lambda n, s, d=F32: ctx.enter_context(nc.sbuf_tensor(n, s, d))
        ps = lambda n, s, d=F32: ctx.enter_context(nc.psum_tensor(n, s, d))

        def count(name):
            counters.append(sem(name))
            return counters[-1]
        qcos, qsin = sb("c_qcos", [HALF, 2, S]), sb("c_qsin", [HALF, 2, S])
        kcos, ksin = sb("c_kcos", [KP, NT, DL]), sb("c_ksin", [KP, NT, DL])
        stats, mv, ve, rstd = sb("c_stats", [S, G, 6]), sb("c_mv", [S, G, 2]), sb("c_ve", [S, G]), sb("c_rstd", [S, G])
        xt = [sb(f"c_xt{i}", [128, KT, T], F32R) for i in range(2)]
        q1 = sb("c_q1", [128, G, CH * CQS], F32R)
        q2 = sb("c_q2", [65, G, CH * CQS], F32R)
        kv = sb("c_kv", [KP, NT, DL])
        kva = [sb(f"c_kva{i}", [KP, NT, DL + 1]) for i in range(2)]
        k1 = [sb(f"c_k1{i}", [128, NT * KP], F32R) for i in range(2)]
        k2 = [sb(f"c_k2{i}", [65, NT * KP], F32R) for i in range(2)]
        mneg = sb("c_mneg", [128, NQT, 65], F32R)
        prob = sb("c_prob", [KP, 2, CQS])
        rc, rs = (prob[0:HALF, i, :].rearrange("p (i n) -> p i n", i=2) for i in range(2))
        late = sb("c_late", [128, NQT * CH * DL + CQS])
        xn = [late[0:S, j * D:(j + 1) * D] for j in range(G - 1)] + [prob[0:S, 0, 0:D]]
        rot = late[0:HALF, 0:4 * T].rearrange("p (a i n) -> p a i n", a=2, i=2)
        cn = late[:, 0:NQT * CH * DL].rearrange("p (t c d) -> p t c d", t=NQT, c=CH)
        ct = late[:, NQT * CH * DL:]
        rden = sb("c_rden", [128, NQT])
        s_ps = ps("c_s_ps", [128, 2, 2, 512])
        m_ps = ps("c_m_ps", [128, 3, 512])
        o_ps = ps("c_o_ps", [128, 512])
        m_flat = m_ps[:, :, :].rearrange("p a n -> p (a n)")
        t_loaded, consts = sem("c_t_loaded"), count("c_consts")
        ln, rstd_ready, xn_ready = count("c_ln"), count("c_rstd_ready"), count("c_xn_ready")
        xt_ps_ready, split_hi, xt_ready = count("c_xt_ps_ready"), count("c_split_hi"), count("c_xt_ready")
        wide_ready, roped, rot_ready = count("c_wide_ready"), count("c_roped"), count("c_rot_ready")
        q_ps_ready, q1_ready, q2_ready = count("c_q_ps_ready"), count("c_q1_ready"), count("c_q2_ready")
        kv_loaded, kv_roped, kva_ready = sem("c_kv_loaded"), count("c_kv_roped"), count("c_kva_ready")
        kt_ready, k1_hi, k1_ready, k2_ready = count("c_kt_ready"), count("c_k1_hi"), count("c_k1_ready"), count("c_k2_ready")
        maxs_ready, mneg_ready, row_ready, row_copied = count("c_maxs_ready"), count("c_mneg_ready"), count("c_row_ready"), count("c_row_copied")
        s_ready, prob_ready, pv_done = count("c_s_ready"), count("c_prob_ready"), count("c_pv_done")
        rden_ready, cn_ready, ct_ps_ready, ct_ready = count("c_rden_ready"), count("c_cn_ready"), count("c_ct_ps_ready"), count("c_ct_ready")
        f_ready, x_added = count("c_f_ready"), count("c_x_added")
        parts = ((0, 0), (0, 1), (1, 0))

        def beside_head(i):
            if i == 3:
                return [("keys", 0)]
            if i >= 11:
                return [("max", 0, 0, t) for t in range(NQT) if t * 5 // NQT == i - 11] + ([("row", 0, 0)] if i == 15 else [])
            return []

        def beside_tile(j, c, r):
            todo = []
            if c == 0:
                if j > 0 and r in (1, 2):
                    todo.append(("turn", j - 1) if r == 1 else ("project", j - 1))
                if 3 <= r < 3 + NQT:
                    todo.append(("max", j, 1, r - 3))
                if r == 11:
                    todo.append(("row", j, 1))
            elif j + 1 < G:
                if r == 1:
                    todo.append(("keys", j + 1))
                if 3 <= r < 3 + NQT:
                    todo.append(("max", j + 1, 0, r - 3))
                if r == 11:
                    todo.append(("row", j + 1, 0))
            return todo

        with nc.Block() as block:
            @block.sync
            def _(sp):
                for c in counters:
                    sp.sem_inc(c, PRIMED)
                sp.dma_start(qcos[:], io["qcos"]).then_inc(t_loaded, 16)
                sp.dma_start(qsin[:], io["qsin"]).then_inc(t_loaded, 16)
                sp.dma_start(kcos[:], io["kcos"]).then_inc(t_loaded, 16)
                sp.dma_start(ksin[:], io["ksin"]).then_inc(t_loaded, 16)
                with sp.Fori(0, B) as b:
                    sp.wait_ge(kva_ready, PRIMED + b * 2)
                    src = io["ctx_512"][bass.ds(b, 1)].rearrange("b l d -> (b l) d")
                    main = src[0:NT * 120].rearrange("(p r) d -> p r d", r=NT)
                    sp.dma_start(kv[0:120], main).then_inc(kv_loaded, 16)
                    sp.dma_start(kv[120:121, 0:4, :], src[1440:1444].unsqueeze(0)).then_inc(kv_loaded, 16)
                    sp.dma_start(kv[120:121, 4:NT, :], src[1432:1440].unsqueeze(0)).then_inc(kv_loaded, 16)
                sp.wait_ge(kv_loaded, B * 48)
                sp.wait_ge(t_loaded, 16 * 4)

            @block.gpsimd
            def _(g):
                with g.Fori(0, NG) as it:
                    def rotate_keys(j):
                        b = it * G + j
                        g.wait_ge(kv_loaded, (b + 1) * 48)
                        if j >= 2:
                            g.wait_ge(pv_done, PRIMED + (b - 1) * CH * NT)
                        else:
                            g.wait_ge(pv_done, PRIMED + it * G * CH * NT)
                        g.tensor_tensor(kva[j % 2][:, :, 0:DL], kv[:], kcos[:], ALU.mult).then_inc(kv_roped, 1)
                        g.wait_ge(kv_roped, PRIMED + 2 * b + 1)
                        g.tensor_tensor(kv[:], kv[:], ksin[:], ALU.mult).then_inc(kv_roped, 1)
                        g.wait_ge(kv_roped, PRIMED + 2 * b + 2)
                        for i in range(2):
                            c0 = slice(i * DL // 2, (i + 1) * DL // 2)
                            c1 = slice((1 - i) * DL // 2, (2 - i) * DL // 2)
                            g.tensor_tensor(kva[j % 2][:, :, c0], kva[j % 2][:, :, c0], kv[:, :, c1], ALU.add).then_inc(kva_ready, 1)

                    def copy_keys(j):
                        g.wait_ge(k1_hi, PRIMED + (it * G + j + 1) * 3)
                        g.sem_inc(m.carrier, 1)
                        g.tensor_copy(k2[j % 2][0:DL, :], k1[j % 2][0:DL, :]).then_inc(k2_ready, 1)
                    g.wait_ge(ln, PRIMED + (it + 1) * (2 * G + 1))
                    g.tensor_tensor(rstd[:], ve[:], m.mhalf[0:S, 0:G], ALU.pow).then_inc(rstd_ready, 1)
                    g.wait_ge(t_loaded, 16 * 4)
                    rotate_keys(0)
                    for i in range(H):
                        n = it * H + i
                        if i >= 2:
                            g.wait_ge(q_ps_ready, PRIMED + n - 1)
                        for a in range(2):
                            g.wait_ge(roped, PRIMED + 4 * n + 2 * (a + 1))
                            g.tensor_tensor(rot[:, i % 2, a, :], rc[:, a, :], rs[:, a, :], ALU.add).then_inc(rot_ready, 1)
                        if i == 5:
                            copy_keys(0)
                    for j in range(1, G):
                        rotate_keys(j)
                        copy_keys(j)

            @block.vector
            def _(v):
                def row_stats(it):
                    xg = lambda j: m.x[:, bass.ds((it * G + j) * D, D)]
                    layernorm_stats(v, xg, stats, mv, ve, G, ln, it * (2 * G + 1), m.carrier)

                def normalise_rows(it):
                    v.wait_ge(rstd_ready, PRIMED + it + 1)
                    v.wait_ge(ct_ps_ready, PRIMED + it * G)
                    for j in range(G):
                        v.tensor_scalar(xn[j], m.x[:, bass.ds((it * G + j) * D, D)], mv[:, j, 0:1], rstd[:, j:j + 1],
                                        ALU.subtract, ALU.mult).then_inc(xn_ready, 1)

                def group(it, more):
                    xg = lambda j: m.x[:, bass.ds((it * G + j) * D, D)]

                    def split_keys(j):
                        b = it * G + j
                        for k in range(3):
                            cols = slice(k * 4 * KP, (k + 1) * 4 * KP)
                            v.wait_ge(kt_ready, PRIMED + b * 3 + k + 1)
                            v.tensor_copy(k1[j % 2][0:DL, cols], m_ps[0:DL, k, 0:4 * KP]).then_inc(k1_hi, 1)
                            v.wait_ge(k1_hi, PRIMED + b * 3 + k + 1)
                            v.tensor_tensor(k1[j % 2][DL:128, cols], m_ps[0:DL, k, 0:4 * KP], k1[j % 2][0:DL, cols].bitcast(F32),
                                            ALU.subtract).then_inc(k1_ready, 1)

                    def reduce_max(j, c, t):
                        ch, n = (it * G + j) * CH + c, QT[t]
                        v.wait_ge(maxs_ready, PRIMED + ch * NQT + t + 1)
                        v.tensor_reduce(mneg[0:n, t, DL:DL + 1], m_ps[0:n, :, 0:4 * KP], AX.XY, ALU.max, negate=True).then_inc(mneg_ready, 1)

                    def copy_row(j, c):
                        ch = (it * G + j) * CH + c
                        v.wait_ge(row_ready, PRIMED + ch + 1)
                        v.tensor_copy(q2[DL:DL + 1, j, c * CQS:(c + 1) * CQS], m_flat[DL:DL + 1, 0:CQS]).then_inc(row_copied, 1)

                    def normalise(j, c):
                        ch = (it * G + j) * CH + c
                        v.wait_ge(pv_done, PRIMED + (ch + 1) * NT)
                        o = o_ps[:, 0:NQT * (DL + 1)].rearrange("p (t d) -> p t d", t=NQT)
                        last = QT[-1]
                        v.reciprocal(rden[:, 0:NQT - 1], o[:, 0:NQT - 1, DL]).then_inc(rden_ready, 1)
                        v.reciprocal(rden[0:last, NQT - 1:NQT], o[0:last, NQT - 1, DL:DL + 1]).then_inc(rden_ready, 1)
                        v.wait_ge(rden_ready, PRIMED + (ch + 1) * 2)
                        if c == 0 and j > 0:
                            v.wait_ge(ct_ps_ready, PRIMED + it * G + j)
                        v.tensor_tensor(cn[:, 0:NQT - 1, c, :], o[:, 0:NQT - 1, 0:DL],
                                        rden[:, 0:NQT - 1].unsqueeze(2).broadcast_to((128, NQT - 1, DL)), ALU.mult).then_inc(cn_ready, 1)
                        v.tensor_scalar(cn[0:last, NQT - 1, c, :], o[0:last, NQT - 1, 0:DL], rden[0:last, NQT - 1:NQT], None,
                                        ALU.mult).then_inc(cn_ready, 1)

                    def add_x(j):
                        v.wait_ge(f_ready, PRIMED + it * G + j + 1)
                        v.scalar_tensor_tensor(xg(j), m_ps[0:S, 2, 0:D], m.tg[0:S, 1:2], xg(j), ALU.mult, ALU.add).then_inc(x_added, 1)

                    def beside(todo):
                        for what, *at in todo:
                            if what in ("keys", "max", "row", "project"):
                                {"keys": split_keys, "max": reduce_max, "row": copy_row, "project": add_x}[what](*at)

                    for k in range(KT):
                        v.wait_ge(xt_ps_ready, PRIMED + it * KT + k + 1)
                        v.tensor_copy(xt[0][:, k, :], m_ps[:, k, 0:T]).then_inc(split_hi, 1)
                        v.wait_ge(split_hi, PRIMED + it * KT + k + 1)
                        v.tensor_tensor(xt[1][:, k, :], m_ps[:, k, 0:T], xt[0][:, k, :].bitcast(F32), ALU.subtract).then_inc(xt_ready, 1)

                    def low_queries(i):
                        n, h = it * H + i, HEADS[i]
                        cols = slice((h % 2) * CQS + (h // 2) * S, (h % 2) * CQS + (h // 2 + 1) * S)
                        v.wait_ge(q1_ready, PRIMED + 2 * n + 2)
                        v.tensor_tensor(q2[0:DL, :, cols], o_ps[0:DL, 0:T].rearrange("p (b s) -> p b s", b=G),
                                        q1[0:DL, :, cols].bitcast(F32), ALU.subtract).then_inc(q2_ready, 1)
                    for i in range(H):
                        n = it * H + i
                        v.wait_ge(wide_ready, PRIMED + n + 1)
                        for a in range(2):
                            if i >= 1:
                                v.wait_ge(rot_ready, PRIMED + 2 * n - 1 + a)
                            for dst, tab, half in ((rc, qcos, a), (rs, qsin, 1 - a)):
                                v.tensor_tensor(dst[:, a, :].rearrange("p (b s) -> p b s", b=G),
                                                s_ps[0:HALF, i % 2, half, 0:T].rearrange("p (b s) -> p b s", b=G),
                                                tab[:, half, :].unsqueeze(1).broadcast_to((HALF, G, S)), ALU.mult).then_inc(roped, 1)
                        if i >= 2:
                            low_queries(i - 2)
                        beside(beside_head(i))
                    low_queries(H - 2)
                    low_queries(H - 1)
                    for j in range(G):
                        for c in range(CH):
                            for r in range(NT):
                                if r == 0 and (j, c) != (0, 0):
                                    normalise(j if c else j - 1, 1 - c)
                                beside(beside_tile(j, c, r))
                                if (j, c, r) == (G - 1, 1, 2) and more:
                                    row_stats(it + 1)
                    normalise(G - 1, 1)
                    if more:
                        normalise_rows(it + 1)
                    add_x(G - 1)
                    v.wait_ge(x_added, PRIMED + (it + 1) * G)

                row_stats(0)
                for i in range(2):
                    v.memset(kva[i][:, :, DL], 1.0).then_inc(consts, 1)
                    v.memset(k2[i][DL:DL + 1, :].bitcast(F32), 1.0).then_inc(consts, 1)
                v.memset(mneg[:].bitcast(F32), 0.0).then_inc(consts, 1)
                v.wait_ge(consts, PRIMED + 5)
                normalise_rows(0)
                v.wait_ge(t_loaded, 16 * 4)
                with v.Fori(0, NG - 1) as it:
                    group(it, True)
                group(NG - 1, False)

            @block.scalar
            def _(a):
                with a.Fori(0, NG) as it:
                    for i in range(H):
                        n, h = it * H + i, HEADS[i]
                        cols = slice((h % 2) * CQS + (h // 2) * S, (h % 2) * CQS + (h // 2 + 1) * S)
                        a.wait_ge(q_ps_ready, PRIMED + n + 1)
                        for half in range(2):
                            a.activation(q1[half * DL:(half + 1) * DL, :, cols], o_ps[0:DL, 0:T].rearrange("p (b s) -> p b s", b=G),
                                         ACT.Copy).then_inc(q1_ready, 1)
                    for j in range(G):
                        b = it * G + j

                        def copy_turned(jj):
                            a.wait_ge(ct_ps_ready, PRIMED + it * G + jj + 1)
                            a.activation(ct, m_flat[:, 0:CQS], ACT.Copy).then_inc(ct_ready, 1)
                        for c in range(CH):
                            for r in range(NT):
                                n = (b * CH + c) * NT + r
                                a.wait_ge(s_ready, PRIMED + n + 1)
                                if (j * CH + c) * NT + r >= 2:
                                    a.wait_ge(pv_done, PRIMED + n - 1)
                                k = keys_of(r)
                                a.activation(prob[0:k, r % 2, :].rearrange("p (i n) -> p i n", i=2),
                                             s_ps[0:k, r % 2, :, 0:CQS // 2], ACT.Exp).then_inc(prob_ready, 1)
                                for what, *at in beside_tile(j, c, r):
                                    if what == "turn":
                                        copy_turned(*at)
                    copy_turned(G - 1)

            @block.tensor
            def _(pe):
                pe.wait_ge(consts, PRIMED + 5)
                with pe.Fori(0, NG) as it:
                    pe.wait_ge(xn_ready, PRIMED + (it + 1) * G)
                    for k in range(KT):
                        for j in range(G):
                            mm = pe.transpose(m_ps[:, k, j * S:(j + 1) * S], xn[j][:, k * 128:(k + 1) * 128], m.ident[0:S, 0:S])
                        mm.then_inc(xt_ps_ready, 1)
                    pe.wait_ge(xt_ready, PRIMED + (it + 1) * KT)

                    def wide(i):
                        if i >= 2:
                            pe.wait_ge(roped, PRIMED + 4 * (it * H + i - 1))
                        for a in range(2):
                            for p, (w, x) in enumerate(parts):
                                for k in range(KT):
                                    mm = pe.matmul(s_ps[0:HALF, i % 2, a, 0:T], m.a[w][:, k, HEADS[i], a * HALF:(a + 1) * HALF], xt[x][:, k, :],
                                                   start=(p == 0 and k == 0), stop=(p == 2 and k == KT - 1))
                        mm.then_inc(wide_ready, 1)

                    def absorbed(i):
                        n = it * H + i
                        pe.wait_ge(rot_ready, PRIMED + 2 * (n + 1))
                        if i >= 1:
                            pe.wait_ge(q2_ready, PRIMED + n)
                            pe.wait_ge(q1_ready, PRIMED + 2 * n)
                        for a in range(2):
                            mm = pe.matmul(o_ps[0:DL, 0:T], m.mqk[:, a, HEADS[i], :], rot[:, i % 2, a, :], start=(a == 0), stop=(a == 1))
                        mm.then_inc(q_ps_ready, 1)

                    def turn_keys(j):
                        b = it * G + j
                        pe.wait_ge(kva_ready, PRIMED + (b + 1) * 2)
                        pe.sem_inc(m.carrier, 1)
                        for k in range(3):
                            for r in range(4 * k, 4 * k + 4):
                                mm = pe.transpose(m_ps[0:DL, k, (r - 4 * k) * KP:(r - 4 * k + 1) * KP], kva[j % 2][:, r, 0:DL], m.ident[0:KP, 0:KP])
                            mm.then_inc(kt_ready, 1)

                    def maxima(j, c, t):
                        ch, n = (it * G + j) * CH + c, QT[t]
                        if t > 0:
                            pe.wait_ge(mneg_ready, PRIMED + ch * NQT + t)
                        elif c == 0:
                            pe.wait_ge(k1_ready, PRIMED + (it * G + j + 1) * 3)
                            pe.wait_ge(q1_ready, PRIMED + 2 * (it * H + (H // 2 if j == 0 else H)))
                        elif j > 0:
                            pe.wait_ge(x_added, PRIMED + it * G + j)
                        else:
                            pe.wait_ge(q1_ready, PRIMED + 2 * (it + 1) * H)
                        for k in range(3):
                            mm = pe.matmul(m_ps[0:n, k, 0:4 * KP], q1[:, j, c * CQS + t * 128:c * CQS + t * 128 + n],
                                           k1[j % 2][:, k * 4 * KP:(k + 1) * 4 * KP], start=True, stop=True)
                        mm.then_inc(maxs_ready, 1)

                    def maxima_row(j, c):
                        ch = (it * G + j) * CH + c
                        pe.wait_ge(mneg_ready, PRIMED + (ch + 1) * NQT)
                        for t, n in enumerate(QT):
                            mm = pe.matmul(m_ps[0:DL + 1, t // 4, (t % 4) * 128:(t % 4) * 128 + n], mneg[0:n, t, :],
                                           m.identr[0:n, 0:n], start=True, stop=True)
                        mm.then_inc(row_ready, 1)

                    def turn_outputs(j):
                        pe.wait_ge(cn_ready, PRIMED + (it * G + j + 1) * CH * 2)
                        pe.wait_ge(row_copied, PRIMED + (it * G + j) * CH + (3 if j + 1 < G else 2))
                        for t, w in enumerate(QT):
                            mm = pe.transpose(m_ps[:, t // 4, (t % 4) * 128:(t % 4) * 128 + w], cn[0:w, t, :, :], m.ident[0:w, 0:w])
                        mm.then_inc(ct_ps_ready, 1)

                    def project(j):
                        pe.wait_ge(ct_ready, PRIMED + it * G + j + 1)
                        for hh in range(H // 2):
                            mm = pe.matmul(m_ps[0:S, 2, 0:D], ct[:, hh * S:(hh + 1) * S], m.cvo[:, hh, :], start=(hh == 0), stop=(hh == H // 2 - 1))
                        mm.then_inc(f_ready, 1)

                    def beside(todo):
                        for what, *at in todo:
                            {"keys": turn_keys, "max": maxima, "row": maxima_row, "turn": turn_outputs, "project": project}[what](*at)

                    def scores(j, c, r):
                        n = ((it * G + j) * CH + c) * NT + r
                        k = keys_of(r)
                        if (j * CH + c) * NT + r >= 2:
                            pe.wait_ge(prob_ready, PRIMED + n - 1)
                        if r == 0:
                            pe.wait_ge(row_copied, PRIMED + (it * G + j) * CH + c + 1)
                            pe.wait_ge(k2_ready, PRIMED + it * G + j + 1)
                        for i in range(2):
                            cols = slice(c * CQS + i * CQS // 2, c * CQS + (i + 1) * CQS // 2)
                            o = s_ps[0:k, r % 2, i, 0:CQS // 2]
                            pe.matmul(o, k1[j % 2][:, r * KP:r * KP + k], q1[:, j, cols], start=True, stop=False)
                            mm = pe.matmul(o, k2[j % 2][:, r * KP:r * KP + k], q2[:, j, cols], start=False, stop=True)
                        mm.then_inc(s_ready, 1)

                    def values(j, c, r):
                        n = ((it * G + j) * CH + c) * NT + r
                        pe.wait_ge(prob_ready, PRIMED + n + 1)
                        if r == 0 and (j, c) != (0, 0):
                            pe.wait_ge(cn_ready, PRIMED + ((it * G + j) * CH + c) * 2)
                        k = keys_of(r)
                        for t, w in enumerate(QT):
                            mm = pe.matmul(o_ps[0:w, t * (DL + 1):(t + 1) * (DL + 1)], prob[0:k, r % 2, t * 128:t * 128 + w],
                                           kva[j % 2][0:k, r, :], start=(r == 0 and t == 0), stop=(r == NT - 1), skip_group_check=True)
                        mm.then_inc(pv_done, 1)

                    for i in range(H):
                        wide(i)
                        if i >= 2:
                            absorbed(i - 2)
                        beside(beside_head(i))
                    absorbed(H - 2)
                    absorbed(H - 1)
                    pe.wait_ge(q2_ready, PRIMED + (it + 1) * H)
                    before = None
                    for j in range(G):
                        for c in range(CH):
                            for r in range(NT):
                                scores(j, c, r)
                                beside(beside_tile(j, c, r))
                                if before:
                                    values(*before)
                                before = (j, c, r)
                    values(*before)
                    turn_outputs(G - 1)
                    project(G - 1)


def phase_l1_ffn(nc, outer, sem, io, m):
    FT = F // 128
    GD = 8
    ND = B // GD
    with ExitStack() as ctx:
        counters = []
        sb = lambda n, s, d=F32: ctx.enter_context(nc.sbuf_tensor(n, s, d))
        ps = lambda n, s, d=F32: ctx.enter_context(nc.psum_tensor(n, s, d))

        def count(name):
            counters.append(sem(name))
            return counters[-1]
        w1r, w2r = sb("d_w1r", [128, KT, F]), sb("d_w2r", [128, FT, D])
        w1, w2 = sb("d_w1", [128, KT, F], BF16), sb("d_w2", [128, FT, D], BF16)
        b1, gamma, beta, b2 = sb("d_b1", [S, F]), sb("d_gamma", [S, F]), sb("d_beta", [S, F]), sb("d_b2", [S, D])
        ones = sb("d_ones", [128, 128])
        identb = sb("d_identb", [128, 128], BF16)
        mhalf = sb("d_minus_half", [S, GD])
        wabs, wmean, wscale = sb("d_wabs", [128, 2]), sb("d_wmean", [128, 2]), sb("d_wscale", [128, 2])
        stats, mv, ve, rstd = sb("d_stats", [S, GD, 6]), sb("d_mv", [S, GD, 2]), sb("d_ve", [S, GD]), sb("d_rstd", [S, GD])
        xn = sb("d_xn", [S, GD, D])
        xmax, xinv, xscale, xdeq, xdeq_next = (sb(f"d_x{n}", [S, GD]) for n in ("max", "inv", "scale", "deq", "deq_next"))
        xq = sb("d_xq", [S, GD, D], BF16)
        xqt = sb("d_xqt", [128, KT, GD * S], BF16)
        h1 = sb("d_h1", [S, GD, F])
        hg = sb("d_hg", [S, GD, F])
        hstats, hmv, hve, hrstd, hshift = (sb("d_hstats", [S, GD, 2, 6]), sb("d_hmv", [S, GD, 2]), sb("d_hve", [S, GD]),
                                           sb("d_hrstd", [S, GD]), sb("d_hshift", [S, GD]))
        hmax, hinv, hscale, hdeq = (sb(f"d_h{n}", [S, GD]) for n in ("max", "inv", "scale", "deq"))
        hq = sb("d_hq", [S, 2, F], BF16)
        hqt = sb("d_hqt", [128, 2, FT, S], BF16)
        res = sb("d_res", [S, GD, D])
        h_ps = ps("d_h_ps", [128, 2, 1024])
        t_ps = ps("d_t_ps", [128, 2, 1024], BF16)
        y_ps = ps("d_y_ps", [128, 2, 512])
        w_loaded, loaded, w_ready, w_sum = sem("d_w_loaded"), sem("d_loaded"), count("d_w_ready"), count("d_w_sum")
        ln, vec, rstd_ready = count("d_ln"), count("d_vec"), count("d_rstd_ready")
        xt_ps_ready, xt_ready = count("d_xt_ps_ready"), count("d_xt_ready")
        h_ready, h1_ready, gelu_ready = count("d_h_ready"), count("d_h1_ready"), count("d_gelu_ready")
        bn_ready, mv_ready, ve_ready, hrstd_ready = count("d_bn_ready"), count("d_mv_ready"), count("d_ve_ready"), count("d_hrstd_ready")
        shift_ready, norm_ready, gamma_ready, beta_ready = count("d_shift_ready"), count("d_norm_ready"), count("d_gamma_ready"), count("d_beta_ready")
        scale_steps, rounded, clipped, hq_ready = count("d_scale_steps"), count("d_rounded"), count("d_clipped"), count("d_hq_ready")
        ht_ps_ready, ht_ready = count("d_ht_ps_ready"), count("d_ht_ready")
        y_ready, x_added, stored, res_ready = count("d_y_ready"), count("d_x_added"), sem("d_stored"), count("d_res_ready")
        NPRE = 16
        NX = GD + 5 + 1 + 2 + 1
        NXQ = NX - 1
        NS = 6

        def at_step(it, i, n, first, last):
            if (first and i < n) or (last and i >= n):
                return None
            return (i - n) % GD, it * GD + (i - n)

        def turns(engine, turn):
            turn(0, True, True, False)
            with engine.Fori(1, ND - 1) as it:
                turn(it, False, True, False)
            turn(ND - 1, False, False, False)
            turn(ND, False, False, True)

        with nc.Block() as block:
            @block.sync
            def _(sp):
                for c in counters:
                    sp.sem_inc(c, PRIMED)
                sp.dma_start(w1r[:], io["L1_w1T"].rearrange("(k p) n -> p k n", p=128)).then_inc(w_loaded, 16)
                sp.dma_start(w2r[:], io["L1_w2T"].rearrange("(k p) n -> p k n", p=128)).then_inc(w_loaded, 16)
                for t, n in ((b2, "L1_ffn_b2"), (b1, "L1_ffn_b1"), (gamma, "L1_ffn_gamma"), (beta, "L1_ffn_beta")):
                    sp.dma_start(t[:], io[n].partition_broadcast(S)).then_inc(loaded, 16)
                with sp.Fori(0, ND) as it:
                    sp.wait_ge(x_added, PRIMED + (it + 1) * GD)
                    sp.dma_start(io["out"][bass.ds(it * GD, GD)].rearrange("b s d -> s b d"),
                                 m.x[:, bass.ds(it * GD * D, GD * D)].rearrange("s (b d) -> s b d", b=GD)).then_inc(stored, 16)
                sp.wait_ge(w_loaded, 16 * 2)
                sp.wait_ge(loaded, 16 * 4)
                sp.wait_ge(stored, 16 * ND)

            @block.gpsimd
            def _(g):
                def deviation(it):
                    g.wait_ge(ln, PRIMED + (it + 1) * (2 * GD + 1))
                    g.tensor_tensor(rstd[:], ve[:], mhalf[:], ALU.pow).then_inc(rstd_ready, 1)

                def turn(it, first, more, last):
                    for i in range(GD):
                        at = lambda n: at_step(it, i, n, first, last)
                        if at(1):
                            j, nb = at(1)
                            g.wait_ge(ve_ready, PRIMED + nb + 1)
                            g.tensor_tensor(hrstd[:, j:j + 1], hve[:, j:j + 1], mhalf[:, 0:1], ALU.pow).then_inc(hrstd_ready, 1)
                        if i == 2 and more:
                            deviation(it + 1)
                        if at(3):
                            j, nb = at(3)
                            g.wait_ge(norm_ready, PRIMED + nb + 1)
                            g.tensor_tensor(h1[:, j, :], hg[:, j, :], gamma[:], ALU.mult).then_inc(gamma_ready, 1)
                            g.wait_ge(gamma_ready, PRIMED + nb + 1)
                            g.tensor_tensor(h1[:, j, :], h1[:, j, :], beta[:], ALU.add).then_inc(beta_ready, 1)
                            g.tensor_tensor(res[:, j, :], m.x[:, bass.ds(nb * D, D)], b2[:], ALU.add).then_inc(res_ready, 1)
                g.wait_ge(w_ready, PRIMED + 1)
                deviation(0)
                g.wait_ge(loaded, 16 * 4)
                g.wait_ge(w_ready, PRIMED + NPRE)
                turns(g, turn)

            @block.vector
            def _(v):
                n = [0]

                def pre(ins):
                    ins.then_inc(w_ready, 1)
                    n[0] += 1
                    v.wait_ge(w_ready, PRIMED + n[0])

                def rows_ahead(it):
                    xg = lambda j: m.x[:, bass.ds((it * GD + j) * D, D)]
                    n = [0]

                    def step(ins):
                        ins.then_inc(vec, 1)
                        n[0] += 1

                    def settle():
                        v.wait_ge(vec, PRIMED + it * NX + n[0])
                    layernorm_stats(v, xg, stats, mv, ve, GD, ln, it * (2 * GD + 1), m.carrier)
                    yield
                    yield
                    v.wait_ge(rstd_ready, PRIMED + it + 1)
                    for j in range(GD):
                        step(v.tensor_scalar(xn[:, j, :], xg(j), mv[:, j, 0:1], rstd[:, j:j + 1], ALU.subtract, ALU.mult))
                    yield
                    settle()
                    step(v.tensor_reduce(xmax[:], xn[:], AX.X, ALU.max, apply_absolute_value=True))
                    yield
                    settle()
                    step(v.tensor_scalar(xmax[:], xmax[:], EPS, None, ALU.max))
                    settle()
                    step(v.reciprocal(xinv[:], xmax[:]))
                    step(v.tensor_scalar(xdeq_next[:], xmax[:], wmean[0:S, 0:1], None, ALU.mult))
                    settle()
                    step(v.tensor_scalar(xscale[:], xinv[:], 127.0, None, ALU.mult))
                    yield
                    settle()
                    for j in range(GD):
                        ins = v.tensor_scalar(xn[:, j, :], xn[:, j, :], xscale[:, j:j + 1], -128.0, ALU.mult, ALU.max)
                    step(ins)
                    yield
                    settle()
                    step(v.tensor_scalar(xn[:], xn[:], 127.0, ROUND, ALU.min, ALU.add))
                    settle()
                    step(v.tensor_scalar(xq[:], xn[:], -ROUND, None, ALU.add))
                    assert n[0] == NXQ, n
                    yield
                    step(v.tensor_copy(xdeq[:], xdeq_next[:]))
                    for half in range(2):
                        v.wait_ge(xt_ps_ready, PRIMED + it * 2 + half + 1)
                        v.tensor_copy(xqt[:, :, half * T:(half + 1) * T], t_ps[:, 0, 0:KT * T].rearrange("p (k n) -> p k n", k=KT)).then_inc(xt_ready, 1)
                    settle()
                    yield

                def turn(it, first, more, last):
                    ahead = rows_ahead(it + 1) if more else None
                    for i in range(GD):
                        at = lambda n: at_step(it, i, n, first, last)
                        if at(6):
                            j, nb = at(6)
                            v.wait_ge(rounded, PRIMED + nb + 1)
                            v.tensor_scalar(hg[:, j, :], hg[:, j, :], ROUND + 127.0, ROUND - 128.0, ALU.min, ALU.max).then_inc(clipped, 1)
                        if at(2):
                            j, nb = at(2)
                            v.wait_ge(hrstd_ready, PRIMED + nb + 1)
                            v.tensor_scalar(hshift[:, j:j + 1], hmv[:, j, 0:1], hrstd[:, j:j + 1], -1.0, ALU.mult, ALU.mult).then_inc(shift_ready, 1)
                        if at(0):
                            j, nb = at(0)
                            v.wait_ge(h_ready, PRIMED + nb + 1)
                            v.scalar_tensor_tensor(h1[:, j, :], h_ps[0:S, j % 2, :], xdeq[:, j:j + 1], b1[:], ALU.mult, ALU.add).then_inc(h1_ready, 1)
                        if at(1):
                            j, nb = at(1)
                            v.wait_ge(gelu_ready, PRIMED + nb + 1)
                            for a in range(2):
                                v.bn_stats(hstats[:, j, a, :], hg[:, j, a * 512:(a + 1) * 512]).then_inc(bn_ready, 1)
                            v.wait_ge(bn_ready, PRIMED + 2 * nb + 2)
                            v.sem_inc(m.carrier, 1)
                            v.bn_aggr(hmv[:, j, :], hstats[:, j, :, :].rearrange("p a b -> p (a b)")).then_inc(mv_ready, 1)
                            v.wait_ge(mv_ready, PRIMED + nb + 1)
                            v.tensor_scalar(hve[:, j:j + 1], hmv[:, j, 1:2], EPS, None, ALU.add).then_inc(ve_ready, 1)
                        if at(5):
                            j, nb = at(5)
                            big, base = hmax[:, j:j + 1], NS * nb
                            v.wait_ge(beta_ready, PRIMED + nb + 1)
                            v.tensor_reduce(big, h1[:, j, :], AX.X, ALU.max, apply_absolute_value=True).then_inc(scale_steps, 1)
                            v.wait_ge(scale_steps, PRIMED + base + 1)
                            v.tensor_scalar(big, big, EPS, None, ALU.max).then_inc(scale_steps, 1)
                            v.wait_ge(scale_steps, PRIMED + base + 2)
                            v.reciprocal(hinv[:, j:j + 1], big).then_inc(scale_steps, 1)
                            v.tensor_scalar(hdeq[:, j:j + 1], big, wmean[0:S, 1:2], None, ALU.mult).then_inc(scale_steps, 1)
                            v.wait_ge(scale_steps, PRIMED + base + 4)
                            v.tensor_scalar(hscale[:, j:j + 1], hinv[:, j:j + 1], 127.0, None, ALU.mult).then_inc(scale_steps, 2)
                        if at(8):
                            j, nb = at(8)
                            xs = m.x[:, bass.ds(nb * D, D)]
                            v.wait_ge(y_ready, PRIMED + nb + 1)
                            v.wait_ge(res_ready, PRIMED + nb + 1)
                            v.scalar_tensor_tensor(xs, y_ps[0:S, j % 2, 0:D], hdeq[:, j:j + 1], res[:, j, :], ALU.mult, ALU.add).then_inc(x_added, 1)
                        if more:
                            next(ahead)
                    if last:
                        v.wait_ge(x_added, PRIMED + B)

                pre(v.memset(mhalf[:], -0.5))
                first_rows = rows_ahead(0)
                for part in range(4):
                    next(first_rows)
                pre(v.memset(ones[:], 1.0))
                pre(v.tensor_copy(identb[:], m.ident[:]))
                v.wait_ge(w_loaded, 16 * 2)
                pre(v.tensor_reduce(wabs[:, 0:1], w1r[:], AX.XY, ALU.add, apply_absolute_value=True))
                pre(v.tensor_reduce(wabs[:, 1:2], w2r[:], AX.XY, ALU.add, apply_absolute_value=True))
                v.wait_ge(w_sum, PRIMED + 1)
                pre(v.tensor_scalar(wmean[:], h_ps[:, 0, 0:2], 1.0 / (F * D), EPS, ALU.mult, ALU.max))
                pre(v.reciprocal(wscale[:], wmean[:]))
                pre(v.tensor_scalar(wmean[:], wmean[:], 1.0 / 127.0, None, ALU.mult))
                pre(v.tensor_scalar(wmean[:, 1:2], wmean[:, 1:2], m.tg[:, 3:4], None, ALU.mult))
                for part in range(4):
                    next(first_rows)
                for i, (r_, w) in enumerate(((w1r, w1), (w2r, w2))):
                    pre(v.tensor_scalar(r_[:], r_[:], wscale[:, i:i + 1], ROUND, ALU.mult, ALU.add))
                    pre(v.tensor_scalar(r_[:], r_[:], -ROUND, 1.0, ALU.add, ALU.min))
                    pre(v.tensor_scalar(w[:], r_[:], -1.0, None, ALU.max))
                v.wait_ge(loaded, 16 * 4)
                pre(v.tensor_scalar(b2[:], b2[:], m.tg[0:S, 3:4], None, ALU.mult))
                assert n[0] == NPRE, n
                turns(v, turn)

            @block.scalar
            def _(a):
                def turn(it, first, more, last):
                    for i in range(GD):
                        at = lambda n: at_step(it, i, n, first, last)
                        if at(7):
                            j, nb = at(7)
                            a.wait_ge(ht_ps_ready, PRIMED + nb + 1)
                            if not (first and j < 2):
                                a.wait_ge(y_ready, PRIMED + nb - 1)
                            a.activation(hqt[:, j % 2].rearrange("p a b -> p (a b)"), t_ps[:, 1, 0:FT * S], ACT.Copy).then_inc(ht_ready, 1)
                        if at(2):
                            j, nb = at(2)
                            a.wait_ge(shift_ready, PRIMED + nb + 1)
                            a.activation(hg[:, j, :], hg[:, j, :], ACT.Identity, bias=hshift[:, j:j + 1], scale=hrstd[:, j:j + 1]).then_inc(norm_ready, 1)
                        if at(0):
                            j, nb = at(0)
                            a.wait_ge(h1_ready, PRIMED + nb + 1)
                            a.activation(hg[:, j, :], h1[:, j, :], ACT.Gelu).then_inc(gelu_ready, 1)
                        if at(6):
                            j, nb = at(6)
                            a.wait_ge(clipped, PRIMED + nb + 1)
                            if not (first and j < 2):
                                a.wait_ge(ht_ps_ready, PRIMED + nb - 1)
                            a.activation(hq[:, j % 2, :], hg[:, j, :], ACT.Copy, bias=-ROUND).then_inc(hq_ready, 1)
                        if at(5):
                            j, nb = at(5)
                            a.wait_ge(scale_steps, PRIMED + NS * (nb + 1))
                            a.activation(hg[:, j, :], h1[:, j, :], ACT.Copy, bias=ROUND, scale=hscale[:, j:j + 1]).then_inc(rounded, 1)
                turns(a, turn)

            @block.tensor
            def _(pe):
                def turn_rows(it):
                    pe.wait_ge(vec, PRIMED + it * NX + NXQ)
                    for half in range(2):
                        if half:
                            pe.wait_ge(xt_ready, PRIMED + it * 2 + 1)
                        for k in range(KT):
                            for j in range(G):
                                mm = pe.transpose(t_ps[:, 0, (k * G + j) * S:(k * G + j + 1) * S],
                                                  xq[:, half * G + j, k * 128:(k + 1) * 128], identb[0:S, 0:S])
                        mm.then_inc(xt_ps_ready, 1)

                def turn(it, first, more, last):
                    for i in range(GD):
                        at = lambda n: at_step(it, i, n, first, last)
                        if at(0):
                            j, nb = at(0)
                            if j % G == 0:
                                pe.wait_ge(xt_ready, PRIMED + it * 2 + j // G + 1)
                            if not (first and j < 2):
                                pe.wait_ge(h1_ready, PRIMED + nb - 1)
                            for a in range(2):
                                for k in range(KT):
                                    mm = pe.matmul(h_ps[0:S, j % 2, a * 512:(a + 1) * 512], xqt[:, k, j * S:(j + 1) * S], w1[:, k, a * 512:(a + 1) * 512],
                                                   start=(k == 0), stop=(k == KT - 1))
                            mm.then_inc(h_ready, 1)
                        if at(7):
                            j, nb = at(7)
                            pe.wait_ge(ht_ready, PRIMED + nb + 1)
                            if not (first and j < 2):
                                pe.wait_ge(x_added, PRIMED + nb - 1)
                            for f in range(FT):
                                mm = pe.matmul(y_ps[0:S, j % 2, 0:D], hqt[:, j % 2, f, :], w2[:, f, :], start=(f == 0), stop=(f == FT - 1))
                            mm.then_inc(y_ready, 1)
                        if at(6):
                            j, nb = at(6)
                            pe.wait_ge(hq_ready, PRIMED + nb + 1)
                            if not (first and j == 0):
                                pe.wait_ge(ht_ready, PRIMED + nb)
                            for f in range(FT):
                                mm = pe.transpose(t_ps[:, 1, f * S:(f + 1) * S], hq[:, j % 2, f * 128:(f + 1) * 128], identb[0:S, 0:S])
                            mm.then_inc(ht_ps_ready, 1)
                        if i == GD - 1 and more:
                            turn_rows(it + 1)

                pe.wait_ge(w_ready, PRIMED + 5)
                pe.matmul(h_ps[:, 0, 0:2], ones[:], wabs[:], start=True, stop=True).then_inc(w_sum, 1)
                turn_rows(0)
                pe.wait_ge(w_ready, PRIMED + NPRE)
                turns(pe, turn)


class Shared:
    pass


def build(nc, io):
    with ExitStack() as outer:
        sb = lambda n, s, d=F32: outer.enter_context(nc.sbuf_tensor(n, s, d))
        sem = lambda n: outer.enter_context(nc.semaphore(n))
        m = Shared()
        m.x = sb("x_rows", [S, B * D])
        m.ident, m.identr = sb("ident", [128, 128]), sb("identr", [128, 128], F32R)
        m.gates, m.tg = sb("gates", [128, 4]), sb("tanh_gates", [128, 4])
        m.mhalf = sb("minus_half", [128, G])
        m.carrier = sem("wait_carrier")
        with ExitStack() as l1:
            sl = lambda n, s, d=F32: l1.enter_context(nc.sbuf_tensor(n, s, d))
            m.a = [sl(f"l1_a{i}", [128, KT, H, CQ], F32R) for i in range(2)]
            m.mqk = sl("l1_mqk", [HALF, 2, H, DL])
            m.cvo = sl("l1_cvo", [128, H // 2, D])
            with nc.sbuf_tensor("raw_weights", [128, 3 * RAW], F32) as early:
                m.moe_raw = [early[:, i * RAW:(i + 1) * RAW] for i in range(3)]
                m.wq = early[:, 0:H * D].rearrange("p (h d) -> p h d", h=H)
                m.kcq = early[:, H * D:H * (D + CQ)].rearrange("p (h q) -> p h q", h=H)
                m.wg, m.wu = ([m.a[j][:].rearrange("p k h q -> p (k h q)")[:, i * RAW:(i + 1) * RAW].rearrange("p (k n) -> p k n", k=KT)
                               for i in range(2)] for j in range(2))
                m.moe_loaded, m.l1_loaded = sem("moe_loaded"), sem("l1_loaded")
                phase_load(nc, outer, sem, io, m)
                phase_l0_attention(nc, outer, sem, io, m)
                phase_moe(nc, outer, sem, io, m)
                phase_l1_weights(nc, outer, sem, io, m)
            phase_l1_attention(nc, outer, sem, io, m)
        phase_l1_ffn(nc, outer, sem, io, m)


def rope_tables(length, dim):
    import numpy as np
    f32 = np.float32
    inv = f32(1.0) / np.power(f32(10000.0), np.arange(0, dim, 2, dtype=f32) / f32(dim)).astype(f32)
    f = np.arange(length, dtype=f32)[:, None] * inv[None, :].astype(f32)
    return np.repeat(np.sin(f), 2, axis=-1).astype(f32), np.repeat(np.cos(f), 2, axis=-1).astype(f32)


def constants():
    import numpy as np
    c = {}
    c["ident"] = np.eye(128, dtype=np.float32)
    q, k = np.arange(S)[:, None], np.arange(S)[None, :]
    c["causal"] = np.where(k <= q, 0.0, -1e30).astype(np.float32)
    c["headsel"] = (np.arange(128)[:, None] // HD == np.arange(8)[None, :]).astype(np.float32)
    row_expert = np.arange(E * I) // I
    rows = np.zeros((40, E * I), np.float32)
    for e in range(E):
        rows[e] = rows[32 + e] = row_expert == e
    c["expert_rows"] = rows
    c["iota8"] = np.arange(E, dtype=np.float32)
    sin, cos = rope_tables(S, CQ)
    c["qcos"] = np.ascontiguousarray(np.stack([cos[:, :HALF].T, cos[:, HALF:].T], 1))
    c["qsin"] = np.ascontiguousarray(np.stack([sin[:, HALF:].T, -sin[:, :HALF].T], 1))
    sin, cos = rope_tables(LK, DL)
    p, r = np.arange(KP)[:, None], np.arange(NT)[None, :]
    key = NT * p + r
    key = np.where(key < LK, key, key - NT)
    hd = DL // 2
    c["kcos"] = np.ascontiguousarray(cos[key])
    c["ksin"] = np.ascontiguousarray(np.concatenate([sin[key][..., hd:], -sin[key][..., :hd]], -1))
    return c


def kernel(**inputs):
    import numpy as np
    import concourse.bacc as _bacc
    from concourse.bass_utils import run_bass_kernel_spmd as _run

    a = inputs
    t = lambda w: np.ascontiguousarray(np.transpose(w))
    lay = {n: np.ascontiguousarray(a[n]) for n in (
        "x", "ctx_512", "g_xattn", "g_ffn", "L1_xattn_Wq", "L1_xattn_w_kc_q", "L1_xattn_w_kc_kv",
        "L1_ffn_b1", "L1_ffn_gamma", "L1_ffn_beta", "L1_ffn_b2")}
    lay["L0_WqT"] = t(a["L0_xattn_Wq"])
    lay["L0_WkvT"] = t(a["L0_xattn_Wkv_expand"])
    lay["L0_WoutT"] = t(a["L0_xattn_Wout"])
    lay["L0_routerT"] = t(a["L0_ffn_router_w"])
    lay["L0_gateT"] = t(np.reshape(a["L0_ffn_w_gate"], (E * I, D)))
    lay["L0_upT"] = t(np.reshape(a["L0_ffn_w_up"], (E * I, D)))
    lay["L0_downT"] = np.ascontiguousarray(np.reshape(np.transpose(a["L0_ffn_w_down"], (0, 2, 1)), (E * I, D)))
    lay["L1_qrT"] = np.ascontiguousarray(np.transpose(a["L1_xattn_W_qr"], (2, 0, 1)))
    lay["L1_krT"] = np.ascontiguousarray(np.transpose(a["L1_xattn_W_kr"], (2, 0, 1)))
    lay["L1_WoT"] = t(a["L1_xattn_Wo"])
    lay["L1_w1T"] = t(a["L1_ffn_w1"])
    lay["L1_w2T"] = t(a["L1_ffn_w2"])
    lay.update(constants())

    nc = _bacc.Bacc("TRN2", target_bir_lowering=False, num_devices=1)
    arrays, io = {}, {}
    for n, v in lay.items():
        arrays[f"in_{n}"] = v
        io[n] = nc.dram_tensor(f"in_{n}", v.shape, F32, kind="ExternalInput").ap()
    io["out"] = nc.dram_tensor("out_rows", (B, S, D), F32, kind="ExternalOutput").ap()
    build(nc, io)
    r = _run(nc, [arrays], core_ids=[0])
    return r.results[0]["out_rows"]
```
